# Optimizing a Trainium2 kernel written in Bass

```python
import numpy as np
import jax
import jax.numpy as jnp

def _softmax(x, axis=-1):
    return jax.nn.softmax(x, axis=axis)

def _gelu(x):
    return jax.nn.gelu(x, approximate=True)

def _silu(x):
    return jax.nn.silu(x)

def _sigmoid(x):
    return jax.nn.sigmoid(x)

def _layernorm(x, axis=-1, eps=1e-05):
    m = jnp.mean(x, axis=axis, keepdims=True)
    v = jnp.var(x, axis=axis, keepdims=True)
    return (x - m) / jnp.sqrt(v + eps)

def _scatter_add(tgt, idx, src, axis=0):
    return tgt.at[idx].add(src)

def _segment_sum(src, seg, n):
    return jax.ops.segment_sum(src, seg, n)
kernel_name = 'mk_seq_preln_d1_jaxref_r2_08388b'

def setup_inputs(seed: int=0):
    np.random.seed(seed)
    _w = jnp.asarray

    def _L0_attn_setup():
        import jax, jax.numpy as jnp
        import numpy as np
        BATCH, L, D_MODEL, STATE_DIM = (8, 1024, 512, 64)
        DT = 0.1
        key = jax.random.key(seed)
        k1, k2, k3 = jax.random.split(key, 3)
        x = jax.random.normal(k1, (BATCH, L, D_MODEL), dtype=jnp.float32)
        log_A = jnp.zeros((D_MODEL, STATE_DIM), dtype=jnp.float32)
        B_param = jax.random.normal(k2, (D_MODEL, STATE_DIM), dtype=jnp.float32) * 0.01
        C = jax.random.normal(k3, (D_MODEL, STATE_DIM), dtype=jnp.float32) * 0.01
        D = jnp.ones((D_MODEL,), dtype=jnp.float32)
        return {'x': x, 'log_A': log_A, 'B_param': B_param, 'C': C, 'D': D}
    _L0_attn_in = _L0_attn_setup()

    def _L0_ffn_setup():
        import jax, jax.numpy as jnp
        import numpy as np
        DIM = 512
        HEADS = 8
        DH = 64
        HDH = HEADS * DH
        SEQ = 4096
        BATCH = 2
        WIN = 64
        N_ITERS = 50
        EPS = 1.0
        NQ = 512
        NKV = 1024
        FETCH_K = 9.0 / 8.0

        def rmsnorm(x, g):
            n = jnp.maximum(jnp.sqrt(jnp.sum(x * x, axis=-1, keepdims=True)), 1e-12)
            return x / n * DIM ** 0.5 * g

        def layernorm(x, g, b):
            m = jnp.mean(x, axis=-1, keepdims=True)
            v = jnp.mean((x - m) ** 2, axis=-1, keepdims=True)
            return (x - m) / jnp.sqrt(v + 1e-05) * g + b

        def coor_descent(s, k_eff):
            logk = jnp.log(jnp.float32(k_eff))

            def body(carry, _):
                a, b = carry
                sb = (s + b) / EPS
                a = EPS * (logk - jax.nn.logsumexp(sb, axis=-1, keepdims=True))
                b = -jax.nn.relu(s + a)
                return ((a, b), None)
            init = (jnp.zeros_like(s[..., :1]), -s)
            (a, b), _ = jax.lax.scan(body, init, None, length=N_ITERS)
            return jnp.exp((s + a + b) / EPS)

        def route(x, routing_token, num_tokens, k_eff):
            s = jnp.einsum('bnd,rd->brn', x, routing_token)[:, 0]
            scores = coor_descent(s, k_eff)
            sel_scores, sel_idx = jax.lax.top_k(scores, num_tokens)
            sel_scores = sel_scores + jax.lax.stop_gradient(1.0 - sel_scores)
            return (sel_scores, sel_idx)

        def light_attn(x, ln_g, ln_b, w_qkv, w_out):
            b, n, _ = x.shape
            xn = layernorm(x, ln_g, ln_b)
            q, k, v = jnp.split(xn @ w_qkv, 3, axis=-1)

            def towin(t):
                return t.reshape(b, n // WIN, WIN, HEADS, DH).transpose(0, 3, 1, 2, 4)
            q, k, v = (towin(q), towin(k), towin(v))

            def around(t):
                pad = jnp.pad(t, ((0, 0), (0, 0), (1, 1), (0, 0), (0, 0)))
                return jnp.concatenate([pad[:, :, :-2], pad[:, :, 1:-1], pad[:, :, 2:]], axis=3)
            kk, vv = (around(k), around(v))
            nw = n // WIN
            wvalid = jnp.pad(jnp.ones((nw,), bool), (1, 1))
            kmask = jnp.concatenate([jnp.repeat(wvalid[:-2, None], WIN, 1), jnp.repeat(wvalid[1:-1, None], WIN, 1), jnp.repeat(wvalid[2:, None], WIN, 1)], axis=1)
            sim = jnp.einsum('bhnwd,bhnWd->bhnwW', q * DH ** (-0.5), kk)
            sim = jnp.where(kmask[None, None, :, None, :], sim, -jnp.finfo(sim.dtype).max)
            attn = jax.nn.softmax(sim, axis=-1)
            o = jnp.einsum('bhnwW,bhnWd->bhnwd', attn, vv)
            o = o.transpose(0, 2, 3, 1, 4).reshape(b, n, HDH)
            return o @ w_out

        def heavy_attn(xq, ctx, scores_kv, rms_g, w_q, w_kv, null_kv, w_out):
            b = xq.shape[0]
            xq = rmsnorm(xq, rms_g)
            ctx = rmsnorm(ctx, rms_g)
            q = (xq @ w_q).reshape(b, -1, HEADS, DH).transpose(0, 2, 1, 3)
            kv = jnp.einsum('bni,ihd->bhnd', ctx, w_kv)
            k, v = (kv[..., :DH], kv[..., DH:])
            v = v * scores_kv[:, None, :, None]
            nk = jnp.broadcast_to(null_kv[0][None, :, None, :], (b, HEADS, 1, DH))
            nv = jnp.broadcast_to(null_kv[1][None, :, None, :], (b, HEADS, 1, DH))
            k = jnp.concatenate([nk, k], axis=2)
            v = jnp.concatenate([nv, v], axis=2)
            sim = jnp.einsum('bhqd,bhkd->bhqk', q * DH ** (-0.5), k)
            attn = jax.nn.softmax(sim, axis=-1)
            o = jnp.einsum('bhqk,bhkd->bhqd', attn, v)
            o = o.transpose(0, 2, 1, 3).reshape(b, -1, HDH)
            return o @ w_out

        def forward(x, ln_g, ln_b, w_qkv_l, w_out_l, null_q, rt_q, rt_kv, rms_g, w_q_h, w_kv_h, null_kv, w_out_h):
            light = light_attn(x, ln_g, ln_b, w_qkv_l, w_out_l)
            sq, iq = route(x, rt_q, NQ, min(NQ * FETCH_K, SEQ))
            skv, ikv = route(x, rt_kv, NKV, min(NKV * FETCH_K, SEQ))
            batch_idx = jnp.arange(x.shape[0])[:, None]
            xq = x[batch_idx, iq]
            xkv = x[batch_idx, ikv]
            routed_out = heavy_attn(xq, xkv, skv, rms_g, w_q_h, w_kv_h, null_kv, w_out_h)
            routed_out = routed_out * sq[..., None]
            out = jnp.broadcast_to(null_q, x.shape)
            out = out.at[batch_idx, iq].set(routed_out)
            return light + out
        key = jax.random.key(seed)
        ks = jax.random.split(key, 10)
        p = lambda i, shape: jax.random.normal(ks[i], shape, jnp.float32) * 0.02
        return dict(x=jax.random.normal(ks[0], (BATCH, SEQ, DIM), jnp.float32), ln_g=jnp.ones((DIM,), jnp.float32), ln_b=jnp.zeros((DIM,), jnp.float32), w_qkv_l=p(1, (DIM, 3 * HDH)), w_out_l=p(2, (HDH, DIM)), null_q=jax.random.normal(ks[3], (DIM,), jnp.float32), rt_q=jax.random.normal(ks[4], (1, DIM), jnp.float32), rt_kv=jax.random.normal(ks[5], (1, DIM), jnp.float32), rms_g=jnp.ones((DIM,), jnp.float32), w_q_h=p(6, (DIM, HDH)), w_kv_h=p(7, (DIM, HEADS, 2 * DH)), null_kv=jax.random.normal(ks[8], (2, HEADS, DH), jnp.float32), w_out_h=p(9, (HDH, DIM)))
    _L0_ffn_in = _L0_ffn_setup()
    _d = {'L0_attn_x': _L0_attn_in['x'], 'L0_attn_log_A': _L0_attn_in['log_A'], 'L0_attn_B_param': _L0_attn_in['B_param'], 'L0_attn_C': _L0_attn_in['C'], 'L0_attn_D': _L0_attn_in['D'], 'L0_ffn_ln_g': _L0_ffn_in['ln_g'], 'L0_ffn_ln_b': _L0_ffn_in['ln_b'], 'L0_ffn_w_qkv_l': _L0_ffn_in['w_qkv_l'], 'L0_ffn_w_out_l': _L0_ffn_in['w_out_l'], 'L0_ffn_null_q': _L0_ffn_in['null_q'], 'L0_ffn_rt_q': _L0_ffn_in['rt_q'], 'L0_ffn_rt_kv': _L0_ffn_in['rt_kv'], 'L0_ffn_rms_g': _L0_ffn_in['rms_g'], 'L0_ffn_w_q_h': _L0_ffn_in['w_q_h'], 'L0_ffn_w_kv_h': _L0_ffn_in['w_kv_h'], 'L0_ffn_null_kv': _L0_ffn_in['null_kv'], 'L0_ffn_w_out_h': _L0_ffn_in['w_out_h']}
    _x0 = _d['L0_attn_x']
    _d['L0_attn_x'] = jax.random.normal(jax.random.fold_in(jax.random.key(seed), 1), (8, 2048, 512), dtype=_x0.dtype)
    del _x0
    return _d

def reference(L0_attn_x, L0_attn_log_A, L0_attn_B_param, L0_attn_C, L0_attn_D, L0_ffn_ln_g, L0_ffn_ln_b, L0_ffn_w_qkv_l, L0_ffn_w_out_l, L0_ffn_null_q, L0_ffn_rt_q, L0_ffn_rt_kv, L0_ffn_rms_g, L0_ffn_w_q_h, L0_ffn_w_kv_h, L0_ffn_null_kv, L0_ffn_w_out_h):

    def _L0_attn_ref(x, log_A, B_param, C, D):
        import jax, jax.numpy as jnp
        import numpy as np
        BATCH, L, D_MODEL, STATE_DIM = (8, 1024, 512, 64)
        DT = 0.1
        batch, seq_len, d_model = x.shape
        A = -jnp.exp(log_A)
        A_bar = jnp.exp(DT * A)
        B_bar = (A_bar - 1.0) / A * B_param
        t = jnp.arange(seq_len, dtype=x.dtype)
        powers = jnp.exp(jnp.log(A_bar)[:, :, None] * t)
        K = jnp.einsum('dn,dnl->dl', C * B_bar, powers)
        x_t = jnp.swapaxes(x, 1, 2)
        fft_size = 2 * seq_len
        K_fft = jnp.fft.rfft(K, n=fft_size, axis=-1)
        x_fft = jnp.fft.rfft(x_t, n=fft_size, axis=-1)
        y = jnp.fft.irfft(K_fft[None] * x_fft, n=fft_size, axis=-1)[:, :, :seq_len]
        y = y + D[:, None] * x_t
        return jnp.swapaxes(y, 1, 2)

    def _L0_ffn_ref(x, ln_g, ln_b, w_qkv_l, w_out_l, null_q, rt_q, rt_kv, rms_g, w_q_h, w_kv_h, null_kv, w_out_h):
        import jax, jax.numpy as jnp
        import numpy as np
        DIM = 512
        HEADS = 8
        DH = 64
        HDH = HEADS * DH
        SEQ = 4096
        BATCH = 2
        WIN = 64
        N_ITERS = 50
        EPS = 1.0
        NQ = 512
        NKV = 1024
        FETCH_K = 9.0 / 8.0

        def rmsnorm(x, g):
            n = jnp.maximum(jnp.sqrt(jnp.sum(x * x, axis=-1, keepdims=True)), 1e-12)
            return x / n * DIM ** 0.5 * g

        def layernorm(x, g, b):
            m = jnp.mean(x, axis=-1, keepdims=True)
            v = jnp.mean((x - m) ** 2, axis=-1, keepdims=True)
            return (x - m) / jnp.sqrt(v + 1e-05) * g + b

        def coor_descent(s, k_eff):
            logk = jnp.log(jnp.float32(k_eff))

            def body(carry, _):
                a, b = carry
                sb = (s + b) / EPS
                a = EPS * (logk - jax.nn.logsumexp(sb, axis=-1, keepdims=True))
                b = -jax.nn.relu(s + a)
                return ((a, b), None)
            init = (jnp.zeros_like(s[..., :1]), -s)
            (a, b), _ = jax.lax.scan(body, init, None, length=N_ITERS)
            return jnp.exp((s + a + b) / EPS)

        def route(x, routing_token, num_tokens, k_eff):
            s = jnp.einsum('bnd,rd->brn', x, routing_token)[:, 0]
            scores = coor_descent(s, k_eff)
            sel_scores, sel_idx = jax.lax.top_k(scores, num_tokens)
            sel_scores = sel_scores + jax.lax.stop_gradient(1.0 - sel_scores)
            return (sel_scores, sel_idx)

        def light_attn(x, ln_g, ln_b, w_qkv, w_out):
            b, n, _ = x.shape
            xn = layernorm(x, ln_g, ln_b)
            q, k, v = jnp.split(xn @ w_qkv, 3, axis=-1)

            def towin(t):
                return t.reshape(b, n // WIN, WIN, HEADS, DH).transpose(0, 3, 1, 2, 4)
            q, k, v = (towin(q), towin(k), towin(v))

            def around(t):
                pad = jnp.pad(t, ((0, 0), (0, 0), (1, 1), (0, 0), (0, 0)))
                return jnp.concatenate([pad[:, :, :-2], pad[:, :, 1:-1], pad[:, :, 2:]], axis=3)
            kk, vv = (around(k), around(v))
            nw = n // WIN
            wvalid = jnp.pad(jnp.ones((nw,), bool), (1, 1))
            kmask = jnp.concatenate([jnp.repeat(wvalid[:-2, None], WIN, 1), jnp.repeat(wvalid[1:-1, None], WIN, 1), jnp.repeat(wvalid[2:, None], WIN, 1)], axis=1)
            sim = jnp.einsum('bhnwd,bhnWd->bhnwW', q * DH ** (-0.5), kk)
            sim = jnp.where(kmask[None, None, :, None, :], sim, -jnp.finfo(sim.dtype).max)
            attn = jax.nn.softmax(sim, axis=-1)
            o = jnp.einsum('bhnwW,bhnWd->bhnwd', attn, vv)
            o = o.transpose(0, 2, 3, 1, 4).reshape(b, n, HDH)
            return o @ w_out

        def heavy_attn(xq, ctx, scores_kv, rms_g, w_q, w_kv, null_kv, w_out):
            b = xq.shape[0]
            xq = rmsnorm(xq, rms_g)
            ctx = rmsnorm(ctx, rms_g)
            q = (xq @ w_q).reshape(b, -1, HEADS, DH).transpose(0, 2, 1, 3)
            kv = jnp.einsum('bni,ihd->bhnd', ctx, w_kv)
            k, v = (kv[..., :DH], kv[..., DH:])
            v = v * scores_kv[:, None, :, None]
            nk = jnp.broadcast_to(null_kv[0][None, :, None, :], (b, HEADS, 1, DH))
            nv = jnp.broadcast_to(null_kv[1][None, :, None, :], (b, HEADS, 1, DH))
            k = jnp.concatenate([nk, k], axis=2)
            v = jnp.concatenate([nv, v], axis=2)
            sim = jnp.einsum('bhqd,bhkd->bhqk', q * DH ** (-0.5), k)
            attn = jax.nn.softmax(sim, axis=-1)
            o = jnp.einsum('bhqk,bhkd->bhqd', attn, v)
            o = o.transpose(0, 2, 1, 3).reshape(b, -1, HDH)
            return o @ w_out

        def forward(x, ln_g, ln_b, w_qkv_l, w_out_l, null_q, rt_q, rt_kv, rms_g, w_q_h, w_kv_h, null_kv, w_out_h):
            light = light_attn(x, ln_g, ln_b, w_qkv_l, w_out_l)
            sq, iq = route(x, rt_q, NQ, min(NQ * FETCH_K, SEQ))
            skv, ikv = route(x, rt_kv, NKV, min(NKV * FETCH_K, SEQ))
            batch_idx = jnp.arange(x.shape[0])[:, None]
            xq = x[batch_idx, iq]
            xkv = x[batch_idx, ikv]
            routed_out = heavy_attn(xq, xkv, skv, rms_g, w_q_h, w_kv_h, null_kv, w_out_h)
            routed_out = routed_out * sq[..., None]
            out = jnp.broadcast_to(null_q, x.shape)
            out = out.at[batch_idx, iq].set(routed_out)
            return light + out
        return forward(x, ln_g, ln_b, w_qkv_l, w_out_l, null_q, rt_q, rt_kv, rms_g, w_q_h, w_kv_h, null_kv, w_out_h)
    x = L0_attn_x
    x = x + _L0_attn_ref(_layernorm(x, axis=-1), L0_attn_log_A, L0_attn_B_param, L0_attn_C, L0_attn_D)
    x = x + _L0_ffn_ref(_layernorm(x, axis=-1), L0_ffn_ln_g, L0_ffn_ln_b, L0_ffn_w_qkv_l, L0_ffn_w_out_l, L0_ffn_null_q, L0_ffn_rt_q, L0_ffn_rt_kv, L0_ffn_rms_g, L0_ffn_w_q_h, L0_ffn_w_kv_h, L0_ffn_null_kv, L0_ffn_w_out_h)
    return x

_drawn_inputs = setup_inputs


def setup_inputs(seed=0):
    import zlib

    import numpy as np

    out = dict(_drawn_inputs(seed))
    spreads = {'L0_attn_log_A': (0.0, 0.8),
     'L0_attn_D': (1.0, 0.2),
     'L0_ffn_ln_g': (1.0, 0.6),
     'L0_ffn_ln_b': (0.0, 0.8),
     'L0_ffn_rms_g': (1.0, 0.6)}
    factors = {'L0_attn_B_param': 8.0,
     'L0_attn_C': 8.0,
     'L0_ffn_w_qkv_l': 4.854,
     'L0_ffn_w_out_l': 4.631,
     'L0_ffn_rt_kv': 8.0,
     'L0_ffn_w_q_h': 8.0,
     'L0_ffn_w_kv_h': 8.0,
     'L0_ffn_null_kv': 8.0,
     'L0_ffn_w_out_h': 8.0}
    for name, (base, spread) in spreads.items():
        noise = np.random.default_rng([zlib.crc32(name.encode()), seed]).standard_normal(out[name].shape)
        drawn = base * np.exp(spread * noise) if base else spread * noise
        out[name] = jnp.asarray(drawn.astype(out[name].dtype))
    for name, factor in factors.items():
        out[name] = (out[name] * factor).astype(out[name].dtype)
    return out
```

```python
from contextlib import ExitStack

import numpy as np

import concourse.bass as bass
import concourse.mybir as mybir

F32 = mybir.dt.float32
I32 = mybir.dt.int32
U32 = mybir.dt.uint32
BF16 = mybir.dt.bfloat16
ALU = mybir.AluOpType
ACT = mybir.ActivationFunctionType
AX_X = mybir.AxisListType.X

P = 128
BATCH, SEQ, DIM, STATE = 8, 2048, 512, 64
HEADS, DH = 8, 64
HDH = HEADS * DH
WIN = 64
PAIRS = HEADS // 2
CHUNK = P
NCH = SEQ // CHUNK
TILES = BATCH * NCH
KC = DIM // P
DT = 0.1
EPS = 1e-5
N_ITERS = 50
NQ, NKV = 512, 1024
K_EFF_Q, K_EFF_KV = 576.0, 1152.0

CPAIRS = DIM // 2
SUB = 16
SPAIRS = SUB // 2
NSUB = DIM // SUB
SUBS_PER_GROUP = P // SUB
KPAD = 2 * CHUNK - 1


def open_tensors(nc, ctx, dtype=F32):
    def sb(name, shape, dt=dtype):
        return ctx.enter_context(nc.sbuf_tensor(name, shape, dt))

    def ps(name, shape, dt=dtype):
        return ctx.enter_context(nc.psum_tensor(name, shape, dt))

    def sem(name):
        return ctx.enter_context(nc.semaphore(name))

    return sb, ps, sem


def spread(ap, *dims):
    return bass.AP(tensor=ap.tensor, offset=ap.offset, ap=[list(ap.ap[0])] + [list(d) for d in dims])


def prepare_phase(nc, x, log_A, B_param, C, D, keep, kpad):
    tiles_per_load = 4
    loads = TILES // tiles_per_load
    x_rows = x.rearrange("b (c p) d -> p (b c) d", p=P)

    with ExitStack() as ctx:
        sb, ps, sem = open_tensors(nc, ctx)
        xin = [sb(f"xin{i}", [P, tiles_per_load, DIM]) for i in range(4)]
        bn = sb("bn", [P, TILES, 6])
        raw = sb("raw", [P, 3, 2, P])
        b_t = sb("b_t", [P, CPAIRS])
        c_t = sb("c_t", [P, CPAIRS])
        abar = sb("abar", [P, CPAIRS])
        cb_two = sb("cb_two", [P, CPAIRS, 2])
        powers = [sb(f"powers{i}", [P, SPAIRS, CHUNK]) for i in range(2)]
        taps_t = sb("taps_t", [P, DIM])
        krow = sb("krow", [P, KC, KPAD])
        dcol = sb("dcol", [P, KC])
        tmp = sb("tmp", [P, TILES])
        tmp2 = sb("tmp2", [P, TILES])
        to_end = sb("to_end", [P, 1])
        steps_back = sb("steps_back", [P, CHUNK])
        ps_t = ps("ps_t", [P, 3, 4, P])
        ps_taps = [ps(f"ps_taps{i}", [P, 512]) for i in range(2)]
        ps_rows = ps("ps_rows", [P, KC, P])

        x_in = [sem(f"x_in{i}") for i in range(4)]
        par_in = sem("par_in")
        ident_made = sem("ident_made")
        iota_made = sem("iota_made")
        stats_done = sem("stats_done")
        par_turned = sem("par_turned")
        rates = sem("rates")
        act_chain = sem("act_chain")
        dve = sem("dve")
        cb_made = sem("cb_made")
        powers_made = sem("powers_made")
        taps_made = sem("taps_made")
        taps_kept = sem("taps_kept")
        rows_turned = sem("rows_turned")
        krow_made = sem("krow_made")
        sqrt_done = sem("sqrt_done")
        kpad_out = sem("kpad_out")

        mean, rstd, ea, cb = keep["mean"], keep["rstd"], keep["ea"], keep["cb"]
        ident, steps = keep["ident"], keep["steps"]

        with nc.Block() as block:

            @block.sync
            def _(sp):
                for n, a in enumerate((log_A, B_param, C)):
                    rows = a.rearrange("(h p two) n -> p h (two n)", p=P, two=2)
                    sp.dma_start(raw[:, n], rows).then_inc(par_in, 16)
                sp.dma_start(dcol[:, :], D.rearrange("(g p) -> p g", p=P),
                             allow_slow_non_contiguous=True).then_inc(par_in, 16)
                for t in range(loads):
                    if t >= 4:
                        sp.wait_ge(stats_done, (t - 3) * tiles_per_load)
                    sp.dma_start(xin[t % 4][:, :, :],
                                 x_rows[:, t * tiles_per_load:(t + 1) * tiles_per_load, :]).then_inc(x_in[t % 4], 16)
                sp.wait_ge(krow_made, 1)
                sp.dma_start(kpad.rearrange("(g p) k -> p g k", p=P), krow[:, :, :]).then_inc(kpad_out, 16)
                sp.wait_ge(kpad_out, 16)

            @block.gpsimd
            def _(pool):
                nc.gpsimd.memset(ident[:, :], 0.0).then_inc(ident_made, 1)
                pool.wait_ge(ident_made, 1)
                nc.gpsimd.affine_select(out=ident[:, :], in_=ident[:, :], compare_op=ALU.not_equal, fill=1.0,
                                        base=0, pattern=[[-1, P]], channel_multiplier=1).then_inc(ident_made, 1)
                nc.gpsimd.iota(steps[:, :], pattern=[[1, CHUNK + 1]], base=0, channel_multiplier=0,
                               allow_small_or_imprecise_dtypes=True).then_inc(iota_made, 1)
                nc.gpsimd.iota(to_end[:, :], pattern=[[0, 1]], base=CHUNK - 1, channel_multiplier=-1,
                               allow_small_or_imprecise_dtypes=True).then_inc(iota_made, 1)
                nc.gpsimd.iota(steps_back[:, :], pattern=[[-1, CHUNK]], base=CHUNK - 1, channel_multiplier=0,
                               allow_small_or_imprecise_dtypes=True).then_inc(iota_made, 1)
                nc.gpsimd.memset(cb_two[:, :, :], 0.0).then_inc(iota_made, 1)
                nc.gpsimd.memset(krow[:, :, :], 0.0).then_inc(iota_made, 1)

            @block.tensor
            def _(pe):
                pe.wait_ge(par_in, 64)
                pe.wait_ge(ident_made, 2)
                for n in range(3):
                    for h in range(2):
                        last = nc.tensor.transpose(ps_t[:, n, h, :], raw[:, n, h, :], ident[:, :])
                last.then_inc(par_turned, 1)
                pe.wait_ge(cb_made, 1)
                with pe.Fori(0, NSUB // 2) as s2:
                    for par in range(2):
                        pe.wait_ge(powers_made, s2 * 2 + par + 1)
                        pe.wait_ge(taps_kept, s2 * 2 + par)
                        for q in range(SPAIRS):
                            last = nc.tensor.matmul(ps_taps[par][:, 2 * q:2 * q + 2], powers[par][:, q, :],
                                                    cb_two[:, bass.ds((s2 * 2 + par) * SPAIRS + q, 1), :],
                                                    start=True, stop=True)
                        last.then_inc(taps_made, 1)
                pe.wait_ge(taps_kept, NSUB)
                for g in range(KC):
                    last = nc.tensor.transpose(ps_rows[:, g, :], taps_t[:, g * P:(g + 1) * P], ident[:, :])
                last.then_inc(rows_turned, 1)

            @block.scalar
            def _(act):
                act.wait_ge(par_turned, 1)
                nc.scalar.activation(ea[:, :], ps_t[:, 0, 0:2].rearrange("p h k -> p (h k)"), ACT.Exp).then_inc(act_chain, 1)
                act.wait_ge(act_chain, 1)
                nc.scalar.activation(abar[:, :], ea[:, :], ACT.Exp, scale=-DT).then_inc(rates, 1)
                act.wait_ge(dve, 3)
                act.wait_ge(iota_made, 3)
                with act.Fori(0, NSUB // 2) as s2:
                    for par in range(2):
                        act.wait_ge(taps_made, s2 * 2)
                        for q in range(SPAIRS):
                            last = nc.scalar.activation(
                                powers[par][:, q, :], steps_back[:, :], ACT.Exp,
                                scale=keep["log_abar"][:, bass.ds((s2 * 2 + par) * SPAIRS + q, 1)])
                        last.then_inc(powers_made, 1)
                act.wait_ge(sqrt_done, 1)
                nc.scalar.activation(tmp2[:, :], tmp[:, :], ACT.Sqrt).then_inc(sqrt_done, 1)

            @block.vector
            def _(v):
                v.wait_ge(par_turned, 1)
                nc.vector.tensor_copy(b_t[:, :], ps_t[:, 1, 0:2].rearrange("p h k -> p (h k)")).then_inc(dve, 1)
                nc.vector.tensor_copy(c_t[:, :], ps_t[:, 2, 0:2].rearrange("p h k -> p (h k)")).then_inc(dve, 1)
                v.wait_ge(rates, 1)
                nc.vector.tensor_scalar(keep["log_abar"][:, :], ea[:, :], -DT, None, ALU.mult).then_inc(dve, 1)
                nc.vector.tensor_scalar(abar[:, :], abar[:, :], -1.0, 1.0, ALU.mult, ALU.add).then_inc(dve, 1)
                nc.vector.reciprocal(cb[:, :], ea[:, :]).then_inc(dve, 1)
                v.wait_ge(dve, 5)
                nc.vector.tensor_tensor(cb[:, :], cb[:, :], abar[:, :], ALU.mult).then_inc(dve, 1)
                v.wait_ge(dve, 6)
                nc.vector.tensor_tensor(cb[:, :], cb[:, :], b_t[:, :], ALU.mult).then_inc(dve, 1)
                v.wait_ge(dve, 7)
                nc.vector.tensor_tensor(cb[:, :], cb[:, :], c_t[:, :], ALU.mult).then_inc(dve, 1)
                v.wait_ge(dve, 8)
                v.wait_ge(iota_made, 5)
                nc.vector.tensor_scalar(keep["to_end_rate"][:, :], to_end[:, :], -DT, None, ALU.mult).then_inc(dve, 1)
                nc.vector.tensor_copy(cb_two[0:STATE, :, 0], cb[0:STATE, :]).then_inc(dve, 1)
                nc.vector.tensor_copy(cb_two[STATE:P, :, 1], cb[STATE:P, :]).then_inc(cb_made, 1)
                v.wait_ge(dve, 10)
                with v.Fori(0, loads // 4) as t4:
                    for i in range(4):
                        v.wait_ge(x_in[i], t4 * 16 + 16)
                        for n in range(tiles_per_load):
                            nc.vector.bn_stats(bn[:, bass.ds(t4 * 16 + i * tiles_per_load + n, 1), :],
                                               xin[i][:, n, :]).then_inc(stats_done, 1)
                        v.wait_ge(taps_made, t4 * 4 + i + 1)
                        nc.vector.tensor_copy(taps_t[:, bass.ds((t4 * 4 + i) * SUB, SUB)],
                                              ps_taps[i % 2][:, 0:SUB]).then_inc(taps_kept, 1)
                v.wait_ge(stats_done, TILES)
                finish_stats(nc, v, dve, 10, bn, mean, rstd, tmp, tmp2, sqrt_done)
                v.wait_ge(rows_turned, 1)
                nc.vector.tensor_copy(krow[:, :, 0:CHUNK], ps_rows[:, :, :]).then_inc(dve, 1)
                v.wait_ge(dve, 10 + FINISH_STEPS + 1)
                nc.vector.tensor_tensor(krow[:, :, CHUNK - 1:CHUNK], krow[:, :, CHUNK - 1:CHUNK],
                                        spread(dcol[:, :], [1, KC], [1, 1]), ALU.add).then_inc(krow_made, 1)


FINISH_STEPS = 11


def finish_stats(nc, v, chain, n, bn, mean, rstd, tmp, tmp2, sqrt_done):
    half = DIM // 2

    def step(ins):
        nonlocal n
        n += 1
        ins.then_inc(chain, 1)
        v.wait_ge(chain, n)

    step(nc.vector.tensor_tensor(mean[:, :], bn[:, :, 1], bn[:, :, 4], ALU.add))
    step(nc.vector.tensor_scalar(mean[:, :], mean[:, :], 0.5, None, ALU.mult))
    step(nc.vector.tensor_tensor(tmp[:, :], bn[:, :, 1], bn[:, :, 4], ALU.subtract))
    step(nc.vector.scalar_tensor_tensor(out=tmp[:, :], in0=tmp[:, :], scalar=0.25, in1=tmp[:, :],
                                        op0=ALU.mult, op1=ALU.mult))
    step(nc.vector.tensor_tensor(tmp2[:, :], bn[:, :, 2], bn[:, :, 5], ALU.add))
    step(nc.vector.scalar_tensor_tensor(out=tmp[:, :], in0=tmp2[:, :], scalar=1.0 / (2 * half), in1=tmp[:, :],
                                        op0=ALU.mult, op1=ALU.add))
    nc.vector.tensor_scalar(tmp[:, :], tmp[:, :], EPS, None, ALU.add).then_inc(sqrt_done, 1)
    v.wait_ge(sqrt_done, 2)
    step(nc.vector.reciprocal(rstd[:, :], tmp2[:, :]))
    step(nc.vector.tensor_tensor(tmp2[:, :], rstd[:, :], rstd[:, :], ALU.mult))
    step(nc.vector.tensor_tensor(tmp2[:, :], tmp2[:, :], tmp[:, :], ALU.mult))
    step(nc.vector.tensor_scalar(tmp2[:, :], tmp2[:, :], -0.5, 1.5, ALU.mult, ALU.add))
    step(nc.vector.tensor_tensor(rstd[:, :], rstd[:, :], tmp2[:, :], ALU.mult))


def conv_phase(nc, x, log_A, keep, kpad, x2):
    COLS = NCH * BATCH
    x_v = x.rearrange("b (c p) d -> c p b d", p=P)
    x2_v = x2.rearrange("b (c p) d -> c p b d", p=P)
    groups = DIM // P
    SCAN = 2 * (NCH - 2)
    logA_flat = log_A.rearrange("d n -> (d n)")

    with ExitStack() as ctx:
        sb, ps, sem = open_tensors(nc, ctx)
        xg = [sb(f"xg{i}", [P, NCH, BATCH, P]) for i in range(2)]
        xn = [sb(f"xn{i}", [P, SUB, COLS]) for i in range(2)]
        toep_back = sb("toep_back", [P, SUB, CHUNK])
        toep = [sb(f"toep{i}", [P, SUB, CHUNK]) for i in range(2)]
        ea_all = sb("ea_all", [P, SUB * STATE])
        tail = [sb(f"tail{i}", [P, SUB * STATE]) for i in range(2)]
        powers = [sb(f"cpow{i}", [P, SPAIRS, CHUNK]) for i in range(2)]
        state = [sb(f"state{i}", [P, NCH, SPAIRS, BATCH]) for i in range(2)]
        decay = [sb(f"decay{i}", [P, SPAIRS]) for i in range(2)]
        carried = [sb(f"carried{i}", [P, SPAIRS, BATCH]) for i in range(2)]
        ps_state = [ps(f"ps_state{i}", [P, SPAIRS, COLS]) for i in range(2)]
        ps_y = [ps(f"ps_y{i}", [P, 4, COLS]) for i in range(4)]

        x_in = [sem(f"cx_in{i}") for i in range(2)]
        toep_in = sem("toep_in")
        toep_made = sem("toep_made")
        ea_in = sem("ea_in")
        ea_exp = sem("ea_exp")
        tails_made = sem("tails_made")
        powers_made = sem("cpowers_made")
        decay_made = sem("decay_made")
        normed = sem("normed")
        norm_step = sem("norm_step")
        states_summed = sem("states_summed")
        states_kept = sem("states_kept")
        carry = sem("carry")
        y_made = sem("y_made")
        y_added = sem("y_added")
        x2_out = sem("x2_out")

        mean, rstd, ea, cb = keep["mean"], keep["rstd"], keep["ea"], keep["cb"]

        def by_column(a):
            return spread(a[:, :], [0, SUB // 2], [1, NCH], [NCH, BATCH])

        with nc.Block() as block:

            @block.sync
            def _(sp):
                def load_group(g):
                    for c in range(NCH):
                        sp.dma_start(xg[g % 2][:, c], x_v[c, :, :, g * P:(g + 1) * P]).then_inc(x_in[g % 2], 16)

                def load_step(it):
                    if it >= 1:
                        sp.wait_ge(tails_made, it)
                    row = logA_flat[it * SUB * STATE:(it + 1) * SUB * STATE]
                    sp.dma_start(ea_all[:, :], bass.AP(tensor=row.tensor, offset=row.offset,
                                                       ap=[[0, P], [1, SUB * STATE]])).then_inc(ea_in, 16)
                    if it >= 1:
                        sp.wait_ge(toep_made, it)
                    sp.dma_start(toep_back[:, :, :],
                                 bass.AP(tensor=kpad.tensor, offset=kpad.offset + it * SUB * KPAD,
                                         ap=[[1, P], [KPAD, SUB], [1, CHUNK]])).then_inc(toep_in, 16)

                load_group(0)
                for it in range(NSUB):
                    load_step(it)
                    g = it // SUBS_PER_GROUP
                    if it == 1:
                        load_group(1)
                    if it % SUBS_PER_GROUP == 2 and g >= 1:
                        sp.wait_ge(y_added, 4 * SUBS_PER_GROUP * g)
                        for c in range(NCH):
                            sp.dma_start(x2_v[c, :, :, (g - 1) * P:g * P], xg[(g - 1) % 2][:, c]).then_inc(x2_out, 16)
                    if it % SUBS_PER_GROUP == 4 and 1 <= g < groups - 1:
                        sp.wait_ge(x2_out, 16 * NCH * g)
                        load_group(g + 1)
                sp.wait_ge(y_added, 4 * NSUB)
                for c in range(NCH):
                    sp.dma_start(x2_v[c, :, :, (groups - 1) * P:], xg[(groups - 1) % 2][:, c]).then_inc(x2_out, 16)
                sp.wait_ge(x2_out, 16 * NCH * groups)

            @block.vector
            def _(v):
                HALF = SUB // 2

                def normalise(g, sub, it, par, wait_y):
                    if wait_y is not None:
                        v.wait_ge(y_made, wait_y)
                    for h in range(2):
                        src = xg[g % 2][:, :, :, bass.ds(sub * SUB + h * HALF, HALF)].rearrange("p c b d -> p d c b")
                        dst = xn[par][:, h * HALF:(h + 1) * HALF, :].rearrange("p d (c b) -> p d c b", c=NCH)
                        nc.vector.tensor_tensor(dst, src, by_column(mean), ALU.subtract).then_inc(norm_step, 1)
                        v.wait_ge(norm_step, it * 2 + h + 1)
                        nc.vector.tensor_tensor(dst, dst, by_column(rstd), ALU.mult).then_inc(normed, 1)

                def add_y(g, sub, it):
                    for f in range(4):
                        v.wait_ge(y_made, it * 4 + f + 1)
                        at = xg[g % 2][:, :, :, bass.ds(sub * SUB, SUB)].rearrange(
                            "p c b (q two) -> p two q (c b)", two=2)[:, f // 2, f % 2 * 4:f % 2 * 4 + 4]
                        nc.vector.tensor_tensor(at, ps_y[f][:, :, :], at, ALU.add).then_inc(y_added, 1)

                v.wait_ge(x_in[0], 16 * NCH)
                normalise(0, 0, 0, 0, None)
                normalise(0, 1, 1, 1, None)
                for g in range(groups):
                    base = g * SUBS_PER_GROUP
                    with v.Fori(0, SUBS_PER_GROUP // 2 - 1) as s2:
                        for par in range(2):
                            sub = s2 * 2 + par
                            add_y(g, sub, sub + base)
                            normalise(g, sub + 2, sub + base + 2, par, (sub + base) * 4 + 4)
                    for par in range(2):
                        sub = SUBS_PER_GROUP - 2 + par
                        add_y(g, sub, base + sub)
                        if g + 1 < groups:
                            v.wait_ge(x_in[(g + 1) % 2], 16 * NCH * ((g + 1) // 2 + 1))
                            normalise(g + 1, par, base + sub + 2, par, (base + sub) * 4 + 4)

            @block.scalar
            def _(act):
                def make_tails(it, par):
                    act.wait_ge(ea_in, it * 16 + 16)
                    nc.scalar.activation(ea_all[:, :], ea_all[:, :], ACT.Exp).then_inc(ea_exp, 1)
                    act.wait_ge(ea_exp, it + 1)
                    nc.scalar.activation(tail[par][:, :], ea_all[:, :], ACT.Exp,
                                         scale=keep["to_end_rate"][:, :]).then_inc(tails_made, 1)

                def make_powers(it, par):
                    for q in range(SPAIRS):
                        last = nc.scalar.activation(powers[par][:, q, :], keep["steps"][:, 1:CHUNK + 1], ACT.Exp,
                                                    scale=keep["log_abar"][:, bass.ds(it * SPAIRS + q, 1)])
                    last.then_inc(powers_made, 1)

                def keep_states(it, par):
                    for q in range(SPAIRS):
                        if q % 4 == 0:
                            act.wait_ge(states_summed, it * 2 + q // 4 + 1)
                        last = nc.scalar.activation(state[par][:, :, q, :],
                                                    ps_state[par][:, q, :].rearrange("p (c b) -> p c b", c=NCH),
                                                    ACT.Identity, scale=cb[:, bass.ds(it * SPAIRS + q, 1)])
                    last.then_inc(states_kept, 1)

                def make_decay(it, par):
                    nc.scalar.activation(decay[par][:, :], ea[:, bass.ds(it * SPAIRS, SPAIRS)], ACT.Exp,
                                         scale=-DT * CHUNK).then_inc(decay_made, 1)

                def turn_toep(it, par):
                    act.wait_ge(toep_in, it * 16 + 16)
                    nc.scalar.activation(toep[par][:, :, :], toep_back[:, :, ::-1], ACT.Identity).then_inc(toep_made, 1)

                for it in range(2):
                    make_tails(it, it)
                make_powers(0, 0)
                make_decay(0, 0)
                turn_toep(0, 0)

                def act_step(it, par, tails_ahead, powers_ahead):
                    keep_states(it, par)
                    if tails_ahead:
                        make_tails(it + 2, par)
                    if powers_ahead:
                        act.wait_ge(y_made, it * 4)
                        make_powers(it + 1, 1 - par)
                        make_decay(it + 1, 1 - par)
                        turn_toep(it + 1, 1 - par)

                with act.Fori(0, NSUB // 2 - 1) as s2:
                    for par in range(2):
                        act_step(s2 * 2 + par, par, True, True)
                act_step(NSUB - 2, 0, False, True)
                act_step(NSUB - 1, 1, False, False)

            @block.gpsimd
            def _(pool):
                with pool.Fori(0, NSUB // 2) as s2:
                    for par in range(2):
                        it = s2 * 2 + par
                        by_seq = spread(decay[par][:, :], [1, SPAIRS], [0, BATCH])
                        pool.wait_ge(states_kept, it + 1)
                        for c in range(1, NCH - 1):
                            if c > 1:
                                pool.wait_ge(carry, it * SCAN + 2 * (c - 1))
                            nc.gpsimd.tensor_tensor(carried[par][:, :, :], state[par][:, c - 1], by_seq,
                                                    ALU.mult).then_inc(carry, 1)
                            pool.wait_ge(carry, it * SCAN + 2 * c - 1)
                            nc.gpsimd.tensor_tensor(state[par][:, c], state[par][:, c], carried[par][:, :, :],
                                                    ALU.add).then_inc(carry, 1)

            @block.tensor
            def _(pe):
                def sum_states(it, par):
                    pe.wait_ge(tails_made, it + 1)
                    for q in range(SPAIRS):
                        if q % 4 == 0:
                            pe.wait_ge(normed, it * 2 + q // 4 + 1)
                        for two in range(2):
                            ch = 2 * q + two
                            last = nc.tensor.matmul(ps_state[par][two * STATE:(two + 1) * STATE, q, :],
                                                    tail[par][:, ch * STATE:(ch + 1) * STATE], xn[par][:, ch, :],
                                                    start=True, stop=True)
                        if q % 4 == 3:
                            last.then_inc(states_summed, 1)

                def make_y(it, par):
                    pe.wait_ge(toep_made, it + 1)
                    pe.wait_ge(powers_made, it + 1)
                    pe.wait_ge(carry, it * SCAN + SCAN)
                    for f in range(4):
                        for i in range(4):
                            ch = 2 * (f % 2 * 4 + i) + f // 2
                            rows = slice(ch % 2 * STATE, (ch % 2 + 1) * STATE)
                            nc.tensor.matmul(ps_y[f][:, i, :], toep[par][:, ch, :], xn[par][:, ch, :],
                                             start=True, stop=False)
                            last = nc.tensor.matmul(ps_y[f][:, i, BATCH:], powers[par][rows, ch // 2, :],
                                                    state[par][rows, 0:NCH - 1, ch // 2, :],
                                                    start=False, stop=True)
                        last.then_inc(y_made, 1)

                sum_states(0, 0)
                with pe.Fori(0, NSUB // 2 - 1) as s2:
                    for par in range(2):
                        pe.wait_ge(states_kept, s2 * 2 + par)
                        sum_states(s2 * 2 + par + 1, 1 - par)
                        make_y(s2 * 2 + par, par)
                pe.wait_ge(states_kept, NSUB - 2)
                sum_states(NSUB - 1, 1)
                make_y(NSUB - 2, 0)
                pe.wait_ge(y_added, 4 * (NSUB - 1))
                make_y(NSUB - 1, 1)


def stats_phase(nc, x2, keep):
    tiles_per_load = 4
    loads = TILES // tiles_per_load
    rows = x2.rearrange("b (c p) d -> p (b c) d", p=P)
    with ExitStack() as ctx:
        sb, ps, sem = open_tensors(nc, ctx)
        xin = [sb(f"sxin{i}", [P, tiles_per_load, DIM]) for i in range(4)]
        bn = sb("sbn", [P, TILES, 6])
        tmp = sb("stmp", [P, TILES])
        tmp2 = sb("stmp2", [P, TILES])
        var2 = sb("svar2", [P, TILES])
        x_in = [sem(f"sx_in{i}") for i in range(4)]
        stats_done = sem("sstats_done")
        dve = sem("sdve")
        sqrt_done = sem("ssqrt_done")
        with nc.Block() as block:

            @block.sync
            def _(sp):
                for t in range(loads):
                    if t >= 4:
                        sp.wait_ge(stats_done, (t - 3) * tiles_per_load)
                    sp.dma_start(xin[t % 4][:, :, :],
                                 rows[:, t * tiles_per_load:(t + 1) * tiles_per_load, :]).then_inc(x_in[t % 4], 16)

            @block.scalar
            def _(act):
                for n in (1, 3, 5):
                    act.wait_ge(sqrt_done, n)
                    nc.scalar.activation(tmp2[:, :], tmp[:, :], ACT.Sqrt).then_inc(sqrt_done, 1)

            @block.vector
            def _(v):
                with v.Fori(0, loads // 4) as t4:
                    for i in range(4):
                        v.wait_ge(x_in[i], t4 * 16 + 16)
                        for n in range(tiles_per_load):
                            nc.vector.bn_stats(bn[:, bass.ds(t4 * 16 + i * tiles_per_load + n, 1), :],
                                               xin[i][:, n, :]).then_inc(stats_done, 1)
                v.wait_ge(stats_done, TILES)
                finish_stats(nc, v, dve, 0, bn, keep["mean2"], keep["rstd2"], tmp, tmp2, sqrt_done)
                nc_steps = FINISH_STEPS

                def step(ins):
                    nonlocal nc_steps
                    nc_steps += 1
                    ins.then_inc(dve, 1)
                    v.wait_ge(dve, nc_steps)

                def inverse_root(to, roots):
                    v.wait_ge(sqrt_done, roots)
                    step(nc.vector.reciprocal(to[:, :], tmp2[:, :]))
                    step(nc.vector.tensor_tensor(tmp2[:, :], to[:, :], to[:, :], ALU.mult))
                    step(nc.vector.tensor_tensor(tmp2[:, :], tmp2[:, :], tmp[:, :], ALU.mult))
                    step(nc.vector.tensor_scalar(tmp2[:, :], tmp2[:, :], -0.5, 1.5, ALU.mult, ALU.add))
                    step(nc.vector.tensor_tensor(to[:, :], to[:, :], tmp2[:, :], ALU.mult))

                rstd2, rstd3 = keep["rstd2"], keep["rstd3"]
                step(nc.vector.tensor_scalar(tmp[:, :], tmp[:, :], -EPS, None, ALU.add))
                step(nc.vector.tensor_tensor(tmp[:, :], tmp[:, :], rstd2[:, :], ALU.mult))
                step(nc.vector.tensor_tensor(tmp[:, :], tmp[:, :], rstd2[:, :], ALU.mult))
                step(nc.vector.tensor_copy(var2[:, :], tmp[:, :]))
                nc.vector.tensor_scalar(tmp[:, :], tmp[:, :], EPS, None, ALU.add).then_inc(sqrt_done, 1)
                inverse_root(rstd3, 4)
                nc.vector.tensor_scalar(tmp[:, :], var2[:, :], float(DIM), 1e-24, ALU.mult, ALU.max).then_inc(sqrt_done, 1)
                inverse_root(keep["rms_scale"], 6)
                step(nc.vector.scalar_tensor_tensor(out=keep["rms_scale"][:, :], in0=keep["rms_scale"][:, :],
                                                    scalar=float(np.float32(DIM ** 0.5)), in1=rstd2[:, :],
                                                    op0=ALU.mult, op1=ALU.mult))
                step(nc.vector.scalar_tensor_tensor(out=keep["shift2"][:, :], in0=keep["mean2"][:, :], scalar=-1.0,
                                                    in1=rstd2[:, :], op0=ALU.mult, op1=ALU.mult))
                step(nc.vector.tensor_tensor(keep["rstd23"][:, :], rstd2[:, :], rstd3[:, :], ALU.mult))
                step(nc.vector.tensor_tensor(keep["shift23"][:, :], keep["shift2"][:, :], rstd3[:, :], ALU.mult))
F32R = mybir.dt.float32r
QKV = 3 * HDH
MAIN, SIDE = P, WIN
RING = 4
XRING = 8


def wait(eng, sem, value):
    if not isinstance(value, int) or value > 0:
        eng.wait_ge(sem, value)


def light_weights_phase(nc, ln_g, ln_b, w_qkv, w_out, null_q, rt_q, rt_kv, w):
    with ExitStack() as ctx:
        sb, ps, sem = open_tensors(nc, ctx)
        raw = sb("lw_raw", [P, KC, QKV])
        raw_o = sb("lw_raw_o", [P, KC, DIM])
        g_col = sb("lw_g", [P, KC])
        b_col = sb("lw_b", [P, KC])
        bias_v = sb("lw_bias_v", [P, KC])
        wide = sb("lw_wide", [P, KC, P])
        null_row = sb("lw_null", [P, DIM])
        ps_bias = ps("lw_ps_bias", [P, QKV // P])
        ps_row = ps("lw_ps_row", [P, DIM])
        loaded, bias_made, dve, hi_made, row_made = (sem(f"lw_{n}") for n in ("loaded", "bias", "dve", "hi", "row"))
        spread_made = sem("lw_spread")
        LOADS = 7

        with nc.Block() as block:

            @block.sync
            def _(sp):
                sp.dma_start(raw[:, :, :], w_qkv.rearrange("(k p) n -> p k n", p=P)).then_inc(loaded, 16)
                sp.dma_start(raw_o[:, :, :], w_out.rearrange("(k p) n -> p k n", p=P)).then_inc(loaded, 16)
                for col, src in ((g_col, ln_g), (b_col, ln_b)):
                    sp.dma_start(col[:, :], src.rearrange("(k p) -> p k", p=P),
                                 allow_slow_non_contiguous=True).then_inc(loaded, 16)
                for row, src in ((null_row[:, :], null_q), (w["rt"][:, 0], rt_q[0]), (w["rt"][:, 1], rt_kv[0])):
                    sp.dma_start(row, bass.AP(tensor=src.tensor, offset=src.offset,
                                              ap=[[0, P], [1, DIM]])).then_inc(loaded, 16)

            @block.tensor
            def _(pe):
                pe.wait_ge(loaded, 16 * LOADS)
                for n in range(QKV // P):
                    for k in range(KC):
                        last = nc.tensor.matmul(ps_bias[:, n:n + 1], raw[:, k, n * P:(n + 1) * P], b_col[:, k:k + 1],
                                                start=(k == 0), stop=(k == KC - 1))
                last.then_inc(bias_made, 1)
                pe.wait_ge(spread_made, 1)
                for k in range(KC):
                    last = nc.tensor.matmul(ps_row[:, :], wide[:, k, :], raw_o[:, k, :],
                                            start=(k == 0), stop=(k == KC - 1))
                last.then_inc(row_made, 1)

            @block.vector
            def _(v):
                v.wait_ge(loaded, 16 * LOADS)
                v.wait_ge(bias_made, 1)
                nc.vector.tensor_scalar(w["bias_q"][:, :], ps_bias[:, 0:4], DH ** -0.5, None, ALU.mult)
                nc.vector.tensor_copy(w["bias_k"][:, :], ps_bias[:, 4:8])
                nc.vector.tensor_copy(bias_v[:, :], ps_bias[:, 8:12]).then_inc(dve, 1)
                v.wait_ge(dve, 1)
                nc.vector.tensor_copy(wide[:, :, :], spread(bias_v[:, :], [1, KC], [0, P])).then_inc(spread_made, 1)
                for k in range(KC):
                    nc.vector.tensor_scalar(raw[:, k, 0:HDH], raw[:, k, 0:HDH], g_col[:, k:k + 1], DH ** -0.5,
                                            ALU.mult, ALU.mult)
                    nc.vector.tensor_scalar(raw[:, k, HDH:], raw[:, k, HDH:], g_col[:, k:k + 1], None,
                                            ALU.mult).then_inc(dve, 1)
                v.wait_ge(hi_made, 2)
                nc.vector.tensor_tensor(w["qkv_lo"][:, :, :], raw[:, :, :], w["qkv_hi"][:, :, :].bitcast(F32), ALU.subtract)
                nc.vector.tensor_tensor(w["out_lo"][:, :, :], raw_o[:, :, :], w["out_hi"][:, :, :].bitcast(F32),
                                        ALU.subtract).then_inc(dve, 1)
                v.wait_ge(row_made, 1)
                nc.vector.tensor_tensor(w["row"][:, :], ps_row[:, :], null_row[:, :], ALU.add).then_inc(dve, 1)
                v.wait_ge(dve, 1 + KC + 2)

            @block.scalar
            def _(act):
                act.wait_ge(loaded, 16 * LOADS)
                nc.scalar.activation(w["out_hi"][:, :, :], raw_o[:, :, :], ACT.Identity).then_inc(hi_made, 1)
                act.wait_ge(dve, 1 + KC)
                nc.scalar.activation(w["qkv_hi"][:, :, :], raw[:, :, :], ACT.Identity).then_inc(hi_made, 1)


def product(nc, out, left, right, first=True, last=True):
    (lh, ll), (rh, rl) = left, right
    nc.tensor.matmul(out, lh, rh, start=first, stop=False)
    nc.tensor.matmul(out, lh, rl, start=False, stop=False)
    return nc.tensor.matmul(out, ll, rh, start=False, stop=last)


def light_phase(nc, x2, out, w, keep, s_all):
    x2_t = x2.rearrange("b (c p) d -> (b c) p d", p=P)
    out_t = out.rearrange("b (c p) d -> (b c) p d", p=P)

    with ExitStack() as ctx:
        sb, ps, sem = open_tensors(nc, ctx)
        xin = sb("l_xin", [P, XRING, DIM])
        x2n = sb("l_x2n", [P, 4, DIM])
        xn = sb("l_xn", [P, 2, DIM])
        dot_out = sb("l_dot_out", [P, DIM])
        dots = sb("l_dots", [P, 2, NCH])
        xt_hi = sb("l_xt_hi", [P, KC, P], F32R)
        xt_lo = sb("l_xt_lo", [P, KC, P], F32R)
        q_tok = sb("l_q_tok", [P, HDH])
        k_tok = sb("l_k_tok", [P, HDH])
        q_t = sb("l_q_t", [P, RING, PAIRS, 2, P])
        k_t = sb("l_k_t", [P, PAIRS, RING * P])
        val = sb("l_val", [P, RING, HDH])
        val_side = sb("l_val_side", [P, RING, HDH])
        prob = [sb(f"l_prob{i}", [P, 2, PAIRS, 2 * P]) for i in range(2)]
        neg_max = sb("l_neg_max", [P, 2, 2, PAIRS])
        total = sb("l_total", [P, 2, 2, PAIRS])
        inv = sb("l_inv", [P, 2, 2, PAIRS])
        pt_main = sb("l_pt_main", [P, HEADS, P])
        pt_side = sb("l_pt_side", [P, HEADS, P])
        att = sb("l_att", [P, HDH])
        at_hi = sb("l_at_hi", [P, KC, P], F32R)
        at_lo = sb("l_at_lo", [P, KC, P], F32R)
        res = sb("l_res", [P, 2, DIM])

        ps_s = ps("l_ps_s", [P, 2, PAIRS, 2 * P])
        ps_a = ps("l_ps_a", [P, 512])
        ps_b = ps("l_ps_b", [P, 512])
        ps_c = ps("l_ps_c", [P, 512])
        ps_d = ps("l_ps_d", [P, 512])

        x_in = [sem(f"l_x_in{i}") for i in range(XRING)]
        res_out = [sem(f"l_res_out{i}") for i in range(2)]
        (zeroed, x_normed, xt_made, xt_hi_kept, xt_kept, q_made, q_kept, k_made, k_kept, v_made, v_kept,
         qt_made, qt_kept, kt_made, kt_kept, s_made, max_made, exp_made, inv_made, dots_kept, dot_step,
         p_normed, v_moved, x_plus, pt_made, pt_kept_dve, pt_kept_act, o_made, o_kept, ot_made, ot_hi_kept, ot_kept,
         out_made, res_made) = (sem("l_" + n) for n in (
             "zeroed x_normed xt_made xt_hi_kept xt_kept q_made q_kept k_made k_kept v_made v_kept "
             "qt_made qt_kept kt_made kt_kept s_made max_made exp_made inv_made dots_kept dot_step "
             "p_normed v_moved x_plus pt_made pt_kept_dve pt_kept_act o_made o_kept ot_made ot_hi_kept ot_kept "
             "out_made res_made").split())
        ZEROED = 5

        ident = keep["ident"]

        def keys_of(j, win):
            if win == 0:
                return (SIDE if j == 0 else 0), MAIN + SIDE
            return 0, (MAIN if j == NCH - 1 else MAIN + SIDE)

        def key_runs(j, win):
            at = j % RING * P
            if win == 0:
                if j == 0:
                    return [(SIDE, at, MAIN)]
                if at == 0:
                    return [(0, RING * P - SIDE, SIDE), (SIDE, 0, MAIN)]
                return [(0, at - SIDE, MAIN + SIDE)]
            if j == NCH - 1:
                return [(0, at, MAIN)]
            if at == RING * P - P:
                return [(0, at, MAIN), (MAIN, 0, SIDE)]
            return [(0, at, MAIN + SIDE)]

        def steps(eng, body):
            for g in range(NCH):
                body(g, g, lambda k, g=g: g - k >= 0)
            with eng.Fori(1, BATCH - 1) as b:
                for j in range(NCH):
                    body(b * NCH + j, j, lambda k: True)
            for g in range(TILES - NCH, TILES + 4):
                body(g, g % NCH, lambda k, g=g: g - k < TILES)

        def by_head(buf, win):
            return buf[:, :, win * WIN:(win + 1) * WIN].rearrange("p (a h) q -> p a h q", h=2)

        def turned(bank):
            return bank[:, :].rearrange("p (a h q) -> p a h q", h=2, q=WIN)

        with nc.Block() as block:

            @block.sync
            def _(sp):
                for t in range(4):
                    sp.dma_start(xin[:, t, :], x2_t[t]).then_inc(x_in[t], 16)

                def body(g, j, live):
                    if live(4):
                        wait(sp, res_made, g - 3)
                        sp.dma_start(out_t[g - 4], res[:, j % 2, :]).then_inc(res_out[j % 2], 16)
                    if live(-4):
                        sp.dma_start(xin[:, (j + 4) % XRING, :], x2_t[g + 4]).then_inc(x_in[(j + 4) % XRING], 16)

                steps(sp, body)
                for i in range(2):
                    sp.wait_ge(res_out[i], 16 * TILES // 2)

            @block.tensor
            def _(pe):
                def transpose_x(g, j):
                    wait(pe, x_normed, g + 1)
                    wait(pe, qt_kept, g)
                    for k in range(KC):
                        last = nc.tensor.transpose(ps_a[:, k * P:(k + 1) * P], xn[:, j % 2, k * P:(k + 1) * P],
                                                   ident[:, :])
                    last.then_inc(xt_made, 1)

                def project(bank, part, done):
                    for k in range(KC):
                        cols = slice(part * HDH, (part + 1) * HDH)
                        last = product(nc, bank[:, :], (xt_hi[:, k, :], xt_lo[:, k, :]),
                                       (w["qkv_hi"][:, k, cols], w["qkv_lo"][:, k, cols]), k == 0, k == KC - 1)
                    last.then_inc(done, 1)

                def turn(bank, src, done):
                    for k in range(KC):
                        last = nc.tensor.transpose(bank[:, k * P:(k + 1) * P], src[:, k * P:(k + 1) * P], ident[:, :])
                    last.then_inc(done, 1)

                def scores(t, j):
                    wait(pe, qt_kept, t + 1)
                    wait(pe, kt_kept, t + 1 if j == NCH - 1 else t + 2)
                    for win in range(2):
                        wait(pe, exp_made, 2 * t + win - 1)
                        for pair in range(PAIRS):
                            for col, key, n in key_runs(j, win):
                                last = nc.tensor.matmul(ps_s[:, win, pair, col:col + n], q_t[:, j % RING, pair, win, :],
                                                        k_t[:, pair, key:key + n], start=True, stop=True)
                        last.then_inc(s_made, 1)

                def turn_probs(bank, j, win, col):
                    for pair in range(PAIRS):
                        last = nc.tensor.transpose(bank[:, pair * P:(pair + 1) * P],
                                                   prob[j % 2][:, win, pair, col:col + P], ident[:, :])
                    last.then_inc(pt_made, 1)

                def attend(t, j):
                    wait(pe, pt_kept_dve, 2 * t + 2)
                    wait(pe, pt_kept_act, 2 * t + 2)
                    wait(pe, v_kept, t + 1)
                    wait(pe, v_moved, t + 1 if j == NCH - 1 else t + 2)
                    for h in range(HEADS):
                        cols = slice(h * DH, (h + 1) * DH)
                        nc.tensor.matmul(ps_c[:, cols], pt_main[:, h, :], val[:, j % RING, cols], start=True, stop=False)
                        last = nc.tensor.matmul(ps_c[:, cols], pt_side[:, h, :], val_side[:, j % RING, cols],
                                                start=False, stop=True)
                    last.then_inc(o_made, 1)

                pe.wait_ge(zeroed, ZEROED)
                transpose_x(0, 0)

                def body(g, j, live):
                    if live(2):
                        scores(g - 2, (j - 2) % NCH)
                    if live(4):
                        wait(pe, ot_kept, g - 3)
                        wait(pe, o_kept, g - 3)
                        for k in range(KC):
                            last = product(nc, ps_c[:, :], (at_hi[:, k, :], at_lo[:, k, :]),
                                           (w["out_hi"][:, k, :], w["out_lo"][:, k, :]), k == 0, k == KC - 1)
                        last.then_inc(out_made, 1)
                    if live(0):
                        wait(pe, xt_kept, g + 1)
                        wait(pe, kt_kept, g)
                        project(ps_b, 0, q_made)
                    if live(3):
                        t, jt = g - 3, (j - 3) % NCH
                        wait(pe, p_normed, 2 * t + 2)
                        wait(pe, res_made, g - 3)
                        turn_probs(ps_c, jt, 0, P)
                    if live(0):
                        project(ps_a, 1, k_made)
                    if live(3):
                        wait(pe, ot_kept, t)
                        turn_probs(ps_d, jt, 1, 0)
                    if live(0):
                        wait(pe, q_kept, g + 1)
                        project(ps_b, 2, v_made)
                    if live(3):
                        wait(pe, pt_kept_dve, 2 * t + 1)
                        turn_probs(ps_c, jt, 0, 0)
                    if live(0):
                        wait(pe, k_kept, g + 1)
                        turn(ps_a, q_tok, qt_made)
                    if live(3):
                        wait(pe, pt_kept_act, 2 * t + 1)
                        turn_probs(ps_d, jt, 1, P)
                    if live(0):
                        wait(pe, v_kept, g + 1)
                        turn(ps_b, k_tok, kt_made)
                    if live(3):
                        attend(t, jt)
                    if live(-1):
                        transpose_x(g + 1, j + 1)
                    if live(3):
                        wait(pe, o_kept, t + 1)
                        turn(ps_d, att, ot_made)

                steps(pe, body)

            @block.scalar
            def _(act):
                def layernorms(g, j, passes):
                    one = slice(g, g + 1) if isinstance(g, int) else bass.ds(g, 1)
                    wait(act, x_in[j % XRING], passes)
                    wait(act, dot_step, 2 * g - 6)
                    nc.scalar.activation(x2n[:, j % 4, :], xin[:, j % XRING, :], ACT.Identity,
                                         scale=keep["rstd2"][:, one], bias=keep["shift2"][:, one])
                    nc.scalar.activation(xn[:, j % 2, :], xin[:, j % XRING, :], ACT.Identity,
                                         scale=keep["rstd23"][:, one], bias=keep["shift23"][:, one]).then_inc(x_normed, 1)

                def keep_xt(g):
                    wait(act, xt_made, g + 1)
                    nc.scalar.activation(xt_hi[:, :, :].rearrange("p k t -> p (k t)"), ps_a[:, :],
                                         ACT.Identity).then_inc(xt_hi_kept, 1)

                layernorms(0, 0, 16)
                layernorms(1, 1, 16)
                keep_xt(0)

                def body(g, j, live):
                    if live(2):
                        t, jt = g - 2, (j - 2) % NCH
                        for win in range(2):
                            wait(act, max_made, 2 * t + win + 1)
                            lo, hi = keys_of(jt, win)
                            at = SIDE * (1 - win)
                            for pair in range(PAIRS):
                                last = nc.scalar.activation(
                                    prob[jt % 2][:, win, pair, at + lo:at + hi], ps_s[:, win, pair, lo:hi], ACT.Exp,
                                    bias=neg_max[:, jt % 2, win, pair:pair + 1],
                                    accum_out=total[:, jt % 2, win, pair:pair + 1])
                            last.then_inc(exp_made, 1)
                    if live(0):
                        wait(act, q_made, g + 1)
                        nc.scalar.activation(q_tok[:, :], ps_b[:, :], ACT.Identity).then_inc(q_kept, 1)
                        wait(act, k_made, g + 1)
                        nc.scalar.activation(k_tok[:, :], ps_a[:, :], ACT.Identity).then_inc(k_kept, 1)
                    if live(1):
                        wait(act, v_kept, g)
                        lo, hi = slice(0, WIN), slice(WIN, P)
                        if (j - 1) % NCH != 0:
                            last = nc.scalar.activation(val_side[lo, (j - 2) % RING, :], val[lo, (j - 1) % RING, :],
                                                        ACT.Identity)
                        if (j - 1) % NCH != NCH - 1:
                            last = nc.scalar.activation(val_side[hi, j % RING, :], val[hi, (j - 1) % RING, :],
                                                        ACT.Identity)
                        last.then_inc(v_moved, 1)
                    if live(3):
                        t, jt = g - 3, (j - 3) % NCH
                        wait(act, pt_made, 4 * t + 2)
                        nc.scalar.activation(by_head(pt_main, 1), turned(ps_d), ACT.Identity).then_inc(pt_kept_act, 1)
                    if live(0):
                        wait(act, v_made, g + 1)
                        nc.scalar.activation(val[:, j % RING, :], ps_b[:, :], ACT.Identity).then_inc(v_kept, 1)
                    if live(3):
                        wait(act, pt_made, 4 * t + 4)
                        nc.scalar.activation(by_head(pt_side, 1), turned(ps_d), ACT.Identity).then_inc(pt_kept_act, 1)
                    if live(-2):
                        layernorms(g + 2, (j + 2) % NCH, (g - j) * (16 // XRING) + 16 * ((j + 2) // XRING + 1))
                    if live(-1):
                        keep_xt(g + 1)
                    if live(3):
                        wait(act, ot_made, t + 1)
                        nc.scalar.activation(at_hi[:, :, :].rearrange("p k t -> p (k t)"), ps_d[:, :],
                                             ACT.Identity).then_inc(ot_hi_kept, 1)

                steps(act, body)

            @block.vector
            def _(v):
                nc.vector.memset(q_t[:, :, :, :, :].rearrange("p r a w q -> p (r a w q)"), 0.0).then_inc(zeroed, 1)
                nc.vector.memset(prob[0][:, :, :, :].rearrange("p w a k -> p (w a k)"), 0.0).then_inc(zeroed, 1)
                nc.vector.memset(prob[1][:, :, :, :].rearrange("p w a k -> p (w a k)"), 0.0).then_inc(zeroed, 1)
                nc.vector.memset(val_side[:, :, :].rearrange("p r n -> p (r n)"), 0.0).then_inc(zeroed, 1)
                nc.vector.memset(dots[:, :, :].rearrange("p r n -> p (r n)"), 0.0).then_inc(zeroed, 1)
                v.wait_ge(zeroed, ZEROED)

                def keep_xt_lo(g):
                    wait(v, xt_hi_kept, g + 1)
                    nc.vector.tensor_tensor(xt_lo[:, :, :].rearrange("p k t -> p (k t)"), ps_a[:, :],
                                            xt_hi[:, :, :].bitcast(F32).rearrange("p k t -> p (k t)"),
                                            ALU.subtract).then_inc(xt_kept, 1)

                keep_xt_lo(0)

                def body(g, j, live):
                    if live(2):
                        t, jt = g - 2, (j - 2) % NCH
                        for win in range(2):
                            wait(v, s_made, 2 * t + win + 1)
                            lo, hi = keys_of(jt, win)
                            if hi - lo == MAIN:
                                edge = SIDE if win == 0 else MAIN
                                nc.vector.memset(prob[jt % 2][:, win, :, edge:edge + SIDE], 0.0)
                            nc.vector.tensor_reduce(neg_max[:, jt % 2, win, :], ps_s[:, win, :, lo:hi], AX_X, ALU.max,
                                                    negate=True).then_inc(max_made, 1)
                    if live(4):
                        t4 = g - 4
                        wait(v, out_made, g - 3)
                        wait(v, x_plus, g - 3)
                        wait(v, res_out[j % 2], (g - j) * 8 + 16 * ((j - 4) // 2))
                        nc.vector.tensor_tensor(res[:, j % 2, :], ps_c[:, :], xin[:, (j - 4) % XRING, :],
                                                ALU.add).then_inc(res_made, 1)
                    if live(3):
                        t3 = g - 3
                        wait(v, pt_made, 4 * t3 + 1)
                        nc.vector.tensor_copy(by_head(pt_main, 0), turned(ps_c)).then_inc(pt_kept_dve, 1)
                    if live(2):
                        wait(v, exp_made, 2 * t + 2)
                        nc.vector.reciprocal(inv[:, jt % 2], total[:, jt % 2]).then_inc(inv_made, 1)
                    if live(3):
                        wait(v, pt_made, 4 * t3 + 3)
                        nc.vector.tensor_copy(by_head(pt_side, 0), turned(ps_c)).then_inc(pt_kept_dve, 1)
                    if live(0):
                        wait(v, qt_made, g + 1)
                        for h in range(2):
                            rows = slice(h * DH, (h + 1) * DH)
                            last = nc.vector.tensor_tensor(
                                q_t[rows, j % RING, :, :, h * WIN:(h + 1) * WIN],
                                ps_a[rows, :].rearrange("p (a w q) -> p a w q", a=PAIRS, w=2),
                                spread(w["bias_q"][rows, :], [1, PAIRS], [0, 2], [0, WIN]), ALU.add)
                        last.then_inc(qt_kept, 1)
                        wait(v, kt_made, g + 1)
                        nc.vector.tensor_tensor(k_t[:, :, j % RING * P:(j % RING + 1) * P],
                                                ps_b[:, :].rearrange("p (a t) -> p a t", a=PAIRS),
                                                spread(w["bias_k"][:, :], [1, PAIRS], [0, P]), ALU.add).then_inc(kt_kept, 1)
                    if live(3):
                        wait(v, o_made, t3 + 1)
                        nc.vector.tensor_copy(att[:, :], ps_c[:, :]).then_inc(o_kept, 1)
                    if live(-1):
                        keep_xt_lo(g + 1)
                    if live(0):
                        wait(v, x_normed, g + 1)
                        for r in range(2):
                            wait(v, dot_step, 2 * g + r)
                            last = nc.vector.tensor_tensor_reduce(dot_out[:, :], x2n[:, j % 4, :], w["rt"][:, r], 1.0, 0.0,
                                                                  ALU.mult, ALU.add, dots[:, r, j:j + 1])
                            last.then_inc(dot_step, 1)
                        if j == NCH - 1:
                            first = g - j
                            at = slice(first, first + NCH) if isinstance(g, int) else bass.ds(first, NCH)
                            wait(v, dot_step, 2 * g + 2)
                            nc.vector.tensor_copy(s_all[:, :, at], dots[:, :, :]).then_inc(dots_kept, 1)
                    if live(3):
                        wait(v, ot_hi_kept, t3 + 1)
                        nc.vector.tensor_tensor(at_lo[:, :, :].rearrange("p k t -> p (k t)"), ps_d[:, :],
                                                at_hi[:, :, :].bitcast(F32).rearrange("p k t -> p (k t)"),
                                                ALU.subtract).then_inc(ot_kept, 1)

                steps(v, body)

            @block.gpsimd
            def _(pool):
                pool.wait_ge(zeroed, ZEROED)

                def body(g, j, live):
                    if live(2):
                        t, jt = g - 2, (j - 2) % NCH
                        for win in range(2):
                            if win == 0:
                                wait(pool, inv_made, t + 1)
                            at = SIDE * (1 - win)
                            mine = prob[jt % 2][:, win, :, at:at + MAIN + SIDE]
                            nc.gpsimd.tensor_tensor(mine, mine, spread(inv[:, jt % 2, win, :], [1, PAIRS], [0, MAIN + SIDE]),
                                                    ALU.mult).then_inc(p_normed, 1)
                    if live(0):
                        wait(pool, x_normed, g + 1)
                        nc.gpsimd.tensor_tensor(xin[:, j % XRING, :], xin[:, j % XRING, :], w["row"][:, :],
                                                ALU.add).then_inc(x_plus, 1)

                steps(pool, body)


ROUTES = 2
ROWS = ROUTES * BATCH
QB, KVB = NQ // P, NKV // P
BIG_BIT = 30


def routing_phase(nc, s_all, keep, lists):
    COLS = ROWS * NCH
    HI = max(QB, KVB)
    PARTS = 2 + 3 * 3
    with ExitStack() as ctx:
        sb, ps, sem = open_tensors(nc, ctx)
        blocks = sb("r_blocks", [P, P])
        ones = sb("r_ones", [P, P])
        before = sb("r_before", [P, P])
        s_t = sb("r_s_t", [P, ROUTES, P])
        gap = sb("r_gap", [P, ROUTES, P])
        score = sb("r_score", [P, ROUTES, P])
        part_max = sb("r_part_max", [P, ROUTES])
        row_max = sb("r_row_max", [ROUTES, BATCH])
        row_wide = sb("r_row_wide", [ROUTES, P])
        s_max = sb("r_s_max", [P, ROUTES])
        neg_a = sb("r_neg_a", [P, ROUTES])
        top = sb("r_top", [P, ROUTES])
        sums = sb("r_sums", [P, ROUTES])
        log_sum = sb("r_log_sum", [P, ROUTES])
        log_k = sb("r_log_k", [P, ROUTES])
        take = sb("r_take", [P, ROUTES])
        cut = sb("r_cut", [P, ROUTES], U32)
        cand = sb("r_cand", [P, ROUTES], U32)
        bit = sb("r_bit", [P, 1], U32)
        gain = sb("r_gain", [P, ROUTES], U32)
        over = sb("r_over", [P, ROUTES, P])
        equal = sb("r_equal", [P, ROUTES, P])
        over_c = sb("r_over_c", [P, ROUTES, BATCH, NCH])
        equal_c = sb("r_equal_c", [P, ROUTES, BATCH, NCH])
        score_c = sb("r_score_c", [P, COLS])
        count = sb("r_count", [P, ROWS, NCH])
        offset = sb("r_offset", [P, ROWS, NCH])
        place = sb("r_place", [P, COLS])
        place_i = sb("r_place_i", [P, COLS], I32)
        block_i = sb("r_block_i", [P, COLS], I32)
        room = sb("r_room", [P, ROWS])
        chosen = sb("r_chosen", [P, COLS])
        column = sb("r_column", [P, COLS])
        block_no = sb("r_block_no", [P, COLS])
        token_row = sb("r_token_row", [P, COLS])
        token_tile = sb("r_token_tile", [P, COLS])
        first_token = sb("r_first_token", [P, BATCH])
        total_no = sb("r_total_no", [P, ROWS, HI])
        in_block = sb("r_in_block", [P, COLS, HI], BF16)
        rest = sb("r_rest", [P, COLS])
        parts = sb("r_parts", [P, COLS, PARTS], BF16)
        what = sb("r_what", [P, COLS, PARTS, HI], BF16)
        row_what = [sb(f"r_row_what{i}", [P, NCH, PARTS, HI], BF16) for i in range(2)]
        one_hot = [sb(f"r_one_hot{i}", [P, NCH, P], BF16) for i in range(2)]
        listed = sb("r_listed", [P, ROWS, PARTS, HI])

        ps_turn = ps("r_ps_turn", [P, 4, P])
        ps_small = ps("r_ps_small", [P, 512])
        ps_sums = ps("r_ps_sums", [P, 512])
        ps_back = ps("r_ps_back", [P, 3, ROUTES, P])
        ps_before = ps("r_ps_before", [P, 512])
        ps_list = [ps(f"r_ps_list{i}", [P, 512]) for i in range(2)]

        (made, turned, max_made, max_turned, wide_made, wide_turned, gap_made, exp_made, total_made, log_made,
         dve, counted, count_made, masks_made, back, tie_in, tie_counts, mask_in, places, what_made, what_moved, hot_made, list_made,
         list_kept) = (sem("r_" + n) for n in (
             "made turned max_made max_turned wide_made wide_turned gap_made exp_made total_made log_made "
             "dve counted count_made masks_made back tie_in tie_counts mask_in places what_made what_moved hot_made list_made "
             "list_kept").split())
        ident, steps = keep["ident"], keep["steps"]
        MADE = 14
        ITER_STEPS = 3
        BIT_STEPS = 4
        scores_over = float(np.float32(np.log(np.float32(SEQ))))

        with nc.Block() as block:

            @block.gpsimd
            def _(pool):
                nc.gpsimd.memset(ones[:, :], 1.0).then_inc(made, 1)
                nc.gpsimd.memset(blocks[:, :], 1.0).then_inc(made, 1)
                nc.gpsimd.memset(before[:, :], 1.0).then_inc(made, 1)
                for a, pattern, mult in ((token_row, [[0, COLS]], 1), (token_tile, [[0, ROWS], [1, NCH]], 0),
                                         (first_token, [[SEQ, BATCH]], 0)):
                    nc.gpsimd.iota(a[:, :], pattern=pattern, base=0, channel_multiplier=mult,
                                   allow_small_or_imprecise_dtypes=True).then_inc(made, 1)
                for r, (k_eff, k) in enumerate(((K_EFF_Q, NQ), (K_EFF_KV, NKV))):
                    nc.gpsimd.memset(log_k[:, r:r + 1], float(np.float32(np.log(np.float32(k_eff))))).then_inc(made, 1)
                    nc.gpsimd.memset(take[:, r:r + 1], float(k)).then_inc(made, 1)
                pool.wait_ge(made, 10)
                by_seq = blocks[:, :].rearrange("p (b t) -> p b t", t=NCH)
                nc.gpsimd.affine_select(out=by_seq, in_=by_seq, compare_op=ALU.is_ge, fill=0.0, base=0,
                                        pattern=[[-NCH, BATCH], [0, NCH]], channel_multiplier=1).then_inc(made, 1)
                nc.gpsimd.affine_select(out=before[:, :], in_=before[:, :], compare_op=ALU.is_ge, fill=0.0, base=-1,
                                        pattern=[[1, P]], channel_multiplier=-1).then_inc(made, 1)
                pool.wait_ge(made, 12)
                nc.gpsimd.affine_select(out=by_seq, in_=by_seq, compare_op=ALU.is_ge, fill=0.0, base=NCH - 1,
                                        pattern=[[NCH, BATCH], [0, NCH]], channel_multiplier=-1).then_inc(made, 2)

            @block.tensor
            def _(pe):
                for r in range(ROUTES):
                    last = nc.tensor.transpose(ps_turn[:, r, :], s_all[:, r, :], ident[:, :])
                last.then_inc(turned, 1)
                pe.wait_ge(max_made, 1)
                nc.tensor.transpose(ps_small[0:ROUTES, 0:P], part_max[:, :], ident[:, :]).then_inc(max_turned, 1)
                pe.wait_ge(wide_made, 1)
                nc.tensor.transpose(ps_small[:, P:P + ROUTES], row_wide[:, :],
                                    ident[0:ROUTES, 0:ROUTES]).then_inc(wide_turned, 1)
                pe.wait_ge(made, MADE)
                with pe.Fori(0, N_ITERS - 1) as i:
                    pe.wait_ge(exp_made, i + 1)
                    nc.tensor.matmul(ps_sums[:, 0:ROUTES], blocks[:, :], sums[:, :], start=True,
                                     stop=True).then_inc(total_made, 1)
                with pe.Fori(0, BIG_BIT) as i:
                    pe.wait_ge(counted, i + 1)
                    nc.tensor.matmul(ps_sums[:, 0:ROUTES], blocks[:, :], sums[:, :], start=True,
                                     stop=True).then_inc(count_made, 1)
                pe.wait_ge(masks_made, 1)
                for n, src in enumerate((over, equal, score)):
                    for r in range(ROUTES):
                        last = nc.tensor.transpose(ps_back[:, n, r, :], src[:, r, :], ident[:, :])
                last.then_inc(back, 1)
                pe.wait_ge(tie_in, 1)
                nc.tensor.matmul(ps_before[:, 0:COLS], before[:, :], equal_c[:, :, :, :].rearrange("p r b t -> p (r b t)"),
                                 start=True, stop=True)
                nc.tensor.matmul(ps_turn[:, 0:2, :].rearrange("p a t -> p (a t)"), ones[:, :],
                                 equal_c[:, :, :, :].rearrange("p r b t -> p (r b t)"), start=True, stop=True)
                nc.tensor.matmul(ps_turn[:, 2:4, :].rearrange("p a t -> p (a t)"), ones[:, :],
                                 over_c[:, :, :, :].rearrange("p r b t -> p (r b t)"), start=True,
                                 stop=True).then_inc(tie_counts, 1)
                pe.wait_ge(mask_in, 1)
                nc.tensor.matmul(ps_before[:, 0:COLS], before[:, :], chosen[:, :], start=True, stop=True)
                nc.tensor.matmul(ps_turn[:, 0:2, :].rearrange("p a t -> p (a t)"), ones[:, :], chosen[:, :],
                                 start=True, stop=True).then_inc(places, 1)
                with pe.Fori(0, ROWS // 2) as r2:
                    for par in range(2):
                        pe.wait_ge(hot_made, r2 * 2 + par + 1)
                        pe.wait_ge(what_moved, r2 * 2 + par + 1)
                        pe.wait_ge(list_kept, r2 * 2 + par)
                        for t in range(NCH):
                            last = nc.tensor.matmul(ps_list[par][:, 0:PARTS * HI], one_hot[par][:, t, :],
                                                    row_what[par][:, t, :, :], start=(t == 0), stop=(t == NCH - 1))
                        last.then_inc(list_made, 1)

            @block.scalar
            def _(act):
                act.wait_ge(made, 1)
                nc.scalar.preload_act_table_set("natural_log_exp_and_others")
                nc.scalar.activation(log_sum[0:1, :], ones[0:1, 0:ROUTES], ACT.Exp).then_inc(log_made, 1)
                with act.Fori(0, N_ITERS - 1) as i:
                    act.wait_ge(gap_made, i + 1)
                    for r in range(ROUTES):
                        last = nc.scalar.activation(score[:, r, :], gap[:, r, :], ACT.Exp, accum_out=sums[:, r:r + 1])
                    last.then_inc(exp_made, 1)
                    act.wait_ge(total_made, i + 1)
                    nc.scalar.activation(log_sum[:, :], ps_sums[:, 0:ROUTES], ACT.Ln).then_inc(log_made, 1)
                act.wait_ge(gap_made, N_ITERS)
                nc.scalar.activation(score[:, :, :], gap[:, :, :], ACT.Exp).then_inc(exp_made, 1)
                act.wait_ge(what_made, 1)
                with act.Fori(0, ROWS // 2) as r2:
                    for par in range(2):
                        row = r2 * 2 + par
                        act.wait_ge(list_made, r2 * 2)
                        nc.scalar.activation(row_what[par][:, :, :, :],
                                             what[:, bass.ds(row * NCH, NCH), :, :], ACT.Identity).then_inc(what_moved, 1)
                    for par in range(2):
                        row = r2 * 2 + par
                        act.wait_ge(list_made, row + 1)
                        nc.scalar.activation(listed[:, bass.ds(row, 1), :, :].rearrange("p o w h -> p (o w h)"),
                                             ps_list[par][:, 0:PARTS * HI], ACT.Identity).then_inc(list_kept, 1)

            @block.vector
            def _(v):
                done = 0

                def step(ins, at=None):
                    nonlocal done
                    done += 1
                    ins.then_inc(dve, 1)
                    v.wait_ge(dve, done if at is None else at + done)

                def gap_to(last_step, at=None):
                    for r in range(ROUTES):
                        last = nc.vector.tensor_scalar(gap[:, r, :], s_t[:, r, :], last_step[:, r:r + 1], 0.0,
                                                       ALU.subtract, ALU.min)
                    last.then_inc(gap_made, 1)

                v.wait_ge(turned, 1)
                step(nc.vector.tensor_copy(s_t[:, :, :], ps_turn[:, 0:2, :]))
                nc.vector.tensor_reduce(part_max[:, :], s_t[:, :, :], AX_X, ALU.max).then_inc(max_made, 1)
                v.wait_ge(max_turned, 1)
                step(nc.vector.tensor_reduce(row_max[:, :], ps_small[0:ROUTES, 0:P].rearrange("r (b t) -> r b t", t=NCH),
                                             AX_X, ALU.max))
                nc.vector.tensor_copy(row_wide[:, :].rearrange("r (b t) -> r b t", t=NCH),
                                      spread(row_max[:, :], [1, BATCH], [0, NCH])).then_inc(wide_made, 1)
                v.wait_ge(wide_turned, 1)
                step(nc.vector.tensor_copy(s_max[:, :], ps_small[:, P:P + ROUTES]))
                v.wait_ge(made, MADE)
                step(nc.vector.tensor_scalar(neg_a[:, :], log_k[:, :], -1.0, scores_over, ALU.mult, ALU.add))
                v.wait_ge(log_made, 1)
                before_loop, done = done, 0
                with v.Fori(0, N_ITERS - 1) as i:
                    at = i * ITER_STEPS + before_loop
                    done = 0
                    step(nc.vector.tensor_tensor(top[:, :], s_max[:, :], neg_a[:, :], ALU.min), at)
                    for r in range(ROUTES):
                        last = nc.vector.tensor_scalar(gap[:, r, :], s_t[:, r, :], neg_a[:, r:r + 1], top[:, r:r + 1],
                                                       ALU.min, ALU.subtract)
                    last.then_inc(gap_made, 1)
                    v.wait_ge(log_made, i + 2)
                    step(nc.vector.tensor_tensor(top[:, :], top[:, :], log_sum[:, :], ALU.add), at)
                    step(nc.vector.tensor_tensor(neg_a[:, :], top[:, :], log_k[:, :], ALU.subtract), at)
                assert done == ITER_STEPS
                done = before_loop + done * (N_ITERS - 1)
                gap_to(neg_a)
                step(nc.vector.memset(cut[:, :], 0))
                step(nc.vector.memset(bit[:, :], 1 << BIG_BIT))
                v.wait_ge(exp_made, N_ITERS)
                before_loop = done
                with v.Fori(0, BIG_BIT) as i:
                    at = i * BIT_STEPS + before_loop
                    done = 0
                    step(nc.vector.tensor_scalar(bit[:, :], bit[:, :], 1, None, ALU.logical_shift_right), at)
                    step(nc.vector.tensor_tensor(cand[:, :], cut[:, :], spread(bit[:, :], [0, ROUTES]), ALU.bitwise_or), at)
                    for r in range(ROUTES):
                        last = nc.vector.tensor_scalar(over[:, r, :], score[:, r, :], cand[:, r:r + 1].bitcast(F32), 0.0,
                                                       ALU.is_ge, ALU.add, accum_out=sums[:, r:r + 1])
                    last.then_inc(counted, 1)
                    v.wait_ge(count_made, i + 1)
                    for r, k in enumerate((NQ, NKV)):
                        last = nc.vector.scalar_tensor_tensor(out=gain[:, r:r + 1], in0=ps_sums[:, r:r + 1], scalar=float(k),
                                                              in1=bit[:, :], op0=ALU.is_ge, op1=ALU.mult)
                    step(last, at)
                    step(nc.vector.tensor_tensor(cut[:, :], cut[:, :], gain[:, :], ALU.bitwise_or), at)
                done = before_loop + done * BIG_BIT
                for r in range(ROUTES):
                    nc.vector.tensor_scalar(equal[:, r, :], score[:, r, :], cut[:, r:r + 1].bitcast(F32), None, ALU.is_equal)
                    last = nc.vector.tensor_scalar(over[:, r, :], score[:, r, :], cut[:, r:r + 1].bitcast(F32), None,
                                                   ALU.is_gt)
                last.then_inc(masks_made, 1)
                v.wait_ge(back, 1)
                nc.vector.tensor_copy(over_c[:, :, :, :].rearrange("p r b t -> p r (b t)"), ps_back[:, 0])
                nc.vector.tensor_copy(equal_c[:, :, :, :].rearrange("p r b t -> p r (b t)"), ps_back[:, 1]).then_inc(tie_in, 1)
                step(nc.vector.tensor_copy(score_c[:, :].rearrange("p (r c) -> p r c", r=ROUTES), ps_back[:, 2]))

                def tiles_before():
                    step(nc.vector.tensor_copy(count[:, :, :].rearrange("p r t -> p (r t)"),
                                               ps_turn[:, 0:2, :].rearrange("p a t -> p (a t)")))
                    step(nc.vector.memset(offset[:, :, 0:1], 0.0))
                    for t in range(1, NCH):
                        step(nc.vector.tensor_tensor(offset[:, :, t], offset[:, :, t - 1], count[:, :, t - 1], ALU.add))
                    step(nc.vector.tensor_tensor(place[:, :], ps_before[:, 0:COLS],
                                                 offset[:, :, :].rearrange("p r t -> p (r t)"), ALU.add))

                v.wait_ge(tie_counts, 1)
                step(nc.vector.tensor_reduce(room[:, :], ps_turn[:, 2:4, :].rearrange("p a (b t) -> p (a b) t", t=NCH), AX_X,
                                             ALU.add))
                step(nc.vector.tensor_tensor(room[:, :].rearrange("p (r b) -> p r b", b=BATCH),
                                             spread(take[:, :], [1, ROUTES], [0, BATCH]),
                                             room[:, :].rearrange("p (r b) -> p r b", b=BATCH), ALU.subtract))
                tiles_before()
                step(nc.vector.tensor_tensor(chosen[:, :].rearrange("p (r t) -> p r t", t=NCH),
                                             place[:, :].rearrange("p (r t) -> p r t", t=NCH),
                                             spread(room[:, :], [1, ROWS], [0, NCH]), ALU.is_lt))
                step(nc.vector.tensor_tensor(chosen[:, :], chosen[:, :],
                                             equal_c[:, :, :, :].rearrange("p r b t -> p (r b t)"), ALU.mult))
                step(nc.vector.tensor_tensor(chosen[:, :], chosen[:, :],
                                             over_c[:, :, :, :].rearrange("p r b t -> p (r b t)"), ALU.add))
                mask_made = nc.vector.tensor_copy(block_no[:, :], chosen[:, :])
                mask_made.then_inc(mask_in, 1)
                v.wait_ge(places, 1)
                tiles_before()
                step(nc.vector.tensor_copy(place_i[:, :], place[:, :]))
                step(nc.vector.tensor_scalar(block_i[:, :], place_i[:, :], P.bit_length() - 1, None, ALU.logical_shift_right))
                step(nc.vector.tensor_scalar(place_i[:, :], place_i[:, :], P - 1, None, ALU.bitwise_and))
                step(nc.vector.tensor_copy(block_no[:, :], block_i[:, :]))
                step(nc.vector.tensor_copy(column[:, :], place_i[:, :]))
                step(nc.vector.scalar_tensor_tensor(out=column[:, :], in0=column[:, :], scalar=1.0, in1=chosen[:, :],
                                                    op0=ALU.add, op1=ALU.mult))
                step(nc.vector.tensor_scalar(column[:, :], column[:, :], -1.0, None, ALU.add))
                step(nc.vector.tensor_tensor(in_block[:, :, :], spread(block_no[:, :], [1, COLS], [0, HI]),
                                             spread(steps[:, 0:HI], [0, COLS], [1, HI]), ALU.is_equal))
                step(nc.vector.tensor_copy(parts[:, :, 0], token_row[:, :]))
                step(nc.vector.tensor_copy(parts[:, :, 1], token_tile[:, :]))

                def by_route(a):
                    return a.rearrange("p (r c) -> p r c", r=ROUTES)

                values = (score_c[:, :], *(spread(keep[n][:, :], [0, ROUTES], [1, TILES]) for n in ("mean2", "rms_scale")))
                for n, value in enumerate(values):
                    left = rest[:, :] if n == 0 else by_route(rest[:, :])
                    for m in range(3):
                        part = parts[:, :, 2 + 3 * n + m]
                        part = part if n == 0 else by_route(part)
                        step(nc.vector.tensor_copy(part, value if m == 0 else left))
                        if m < 2:
                            step(nc.vector.tensor_tensor(left, value if m == 0 else left, part, ALU.subtract))
                for m in range(PARTS):
                    step(nc.vector.tensor_tensor(what[:, :, m, :], in_block[:, :, :],
                                                 spread(parts[:, :, m:m + 1], [PARTS, COLS], [0, HI]), ALU.mult))
                what_ready = nc.vector.memset(offset[:, :, 0:1], 0.0)
                what_ready.then_inc(what_made, 1)
                with v.Fori(0, ROWS // 2) as r2:
                    for par in range(2):
                        row = r2 * 2 + par
                        v.wait_ge(list_made, r2 * 2)
                        nc.vector.tensor_tensor(one_hot[par][:, :, :],
                                                spread(column[:, bass.ds(row * NCH, NCH)], [1, NCH], [0, P]),
                                                spread(steps[:, 0:P], [0, NCH], [1, P]), ALU.is_equal).then_inc(hot_made, 1)
                v.wait_ge(list_kept, ROWS)
                step(nc.vector.scalar_tensor_tensor(out=total_no[:, :, :], in0=listed[:, :, 1, :], scalar=float(P),
                                                    in1=listed[:, :, 0, :], op0=ALU.mult, op1=ALU.add))
                step(nc.vector.tensor_tensor(lists["token"][:, :, :].rearrange("p (r b) h -> p r b h", r=ROUTES),
                                             total_no[:, :, :].rearrange("p (r b) h -> p r b h", r=ROUTES),
                                             spread(first_token[:, :], [0, ROUTES], [1, BATCH], [0, HI]), ALU.add))
                for n, name in enumerate(("factor", "mean", "scale")):
                    step(nc.vector.tensor_tensor(lists[name][:, :, :], listed[:, :, 2 + 3 * n, :], listed[:, :, 3 + 3 * n, :],
                                                 ALU.add))
                    step(nc.vector.tensor_tensor(lists[name][:, :, :], lists[name][:, :, :], listed[:, :, 4 + 3 * n, :],
                                                 ALU.add))
                step(nc.vector.tensor_scalar(total_no[:, :, :], lists["factor"][:, :, :], -1.0, 1.0, ALU.mult, ALU.add))
                step(nc.vector.tensor_tensor(lists["factor"][:, :, :], total_no[:, :, :], lists["factor"][:, :, :], ALU.add))


def heavy_weights_phase(nc, rms_g, w_q, w_kv, null_kv, w_out, null_q, w):
    with ExitStack() as ctx:
        sb, ps, sem = open_tensors(nc, ctx)
        raw_q = sb("hw_raw_q", [P, KC, HDH])
        raw_kv = sb("hw_raw_kv", [P, KC, HEADS, 2, DH])
        raw_parts = sb("hw_raw_parts", [P, 2, KC, HDH])
        raw_null = sb("hw_raw_null", [P, HEADS])
        g_col = sb("hw_g", [P, KC])
        loaded, scaled, hi_made, lo_made = (sem(f"hw_{n}") for n in ("loaded", "scaled", "hi", "lo"))
        LOADS = 8

        with nc.Block() as block:

            @block.sync
            def _(sp):
                sp.dma_start(raw_q[:, :, :], w_q.rearrange("(k p) n -> p k n", p=P)).then_inc(loaded, 16)
                sp.dma_start(raw_kv[:, :, :, :, :].rearrange("p k h w d -> p k (h w d)"),
                             w_kv.rearrange("(k p) h n -> p k (h n)", p=P)).then_inc(loaded, 16)
                sp.dma_start(w["out"][:, :, :], w_out.rearrange("(k p) n -> p k n", p=P)).then_inc(loaded, 16)
                sp.dma_start(g_col[:, :], rms_g.rearrange("(k p) -> p k", p=P),
                             allow_slow_non_contiguous=True).then_inc(loaded, 16)
                for half in range(2):
                    sp.dma_start(raw_null[half * DH:(half + 1) * DH, :], null_kv[0].rearrange("h d -> d h"),
                                 allow_slow_non_contiguous=True).then_inc(loaded, 16)
                for row, src in ((w["null_v"][:, :], null_kv[1]), (w["null_row"][:, :], null_q)):
                    sp.dma_start(row, bass.AP(tensor=src.tensor, offset=src.offset,
                                              ap=[[0, P], [1, DIM]])).then_inc(loaded, 16)

            @block.vector
            def _(v):
                v.wait_ge(loaded, 16 * LOADS)
                for k in range(KC):
                    nc.vector.tensor_scalar(raw_q[:, k, :], raw_q[:, k, :], g_col[:, k:k + 1], DH ** -0.5,
                                            ALU.mult, ALU.mult)
                    for n in range(2):
                        nc.vector.tensor_scalar(raw_parts[:, n, k, :].rearrange("p (h d) -> p h d", h=HEADS),
                                                raw_kv[:, k, :, n, :], g_col[:, k:k + 1], None,
                                                ALU.mult).then_inc(scaled, 1)
                v.wait_ge(hi_made, 4)
                for hi, lo, raw in ((w["q_hi"], w["q_lo"], raw_q[:, :, :]), (w["k_hi"], w["k_lo"], raw_parts[:, 0]),
                                    (w["v_hi"], w["v_lo"], raw_parts[:, 1])):
                    nc.vector.tensor_tensor(lo[:, :, :], raw, hi[:, :, :].bitcast(F32), ALU.subtract).then_inc(lo_made, 1)
                nc.vector.tensor_tensor(w["null_k"][:, :, 1], raw_null[:, :], w["null_k"][:, :, 0].bitcast(F32),
                                        ALU.subtract).then_inc(lo_made, 1)
                v.wait_ge(lo_made, 4)

            @block.scalar
            def _(act):
                act.wait_ge(loaded, 16 * LOADS)
                nc.scalar.activation(w["null_k"][:, :, 0], raw_null[:, :], ACT.Identity).then_inc(hi_made, 1)
                act.wait_ge(scaled, 2 * KC)
                nc.scalar.activation(w["q_hi"][:, :, :], raw_q[:, :, :], ACT.Identity).then_inc(hi_made, 1)
                nc.scalar.activation(w["k_hi"][:, :, :], raw_parts[:, 0], ACT.Identity).then_inc(hi_made, 1)
                nc.scalar.activation(w["v_hi"][:, :, :], raw_parts[:, 1], ACT.Identity).then_inc(hi_made, 1)


def heavy_phase(nc, x2, out, w, keep, lists):
    out_rows = out.rearrange("b n d -> (b n) d")
    x2_rows = x2.rearrange("b n d -> (b n) d")
    GT = 4
    GROUPS = 1 + NKV // (GT * P)
    ROWT = GT * GROUPS
    KVG = GROUPS - 1
    KT = NKV // P
    SLOTS = 3
    STEPS = QB * HEADS
    LAST = BATCH * QB - 1

    with ExitStack() as ctx:
        sb, ps, sem = open_tensors(nc, ctx)
        rows_in = [sb(f"h_rows{i}", [P, DIM]) for i in range(SLOTS)]
        xt_hi = sb("h_xt_hi", [P, KC, GT * P], F32R)
        xt_lo = sb("h_xt_lo", [P, KC, GT * P], F32R)
        q2 = sb("h_q2", [P, HEADS, NQ], F32R)
        k2_hi = sb("h_k2_hi", [P, HEADS, NKV], F32R)
        k2_lo = sb("h_k2_lo", [P, HEADS, NKV], F32R)
        val = sb("h_val", [P, KT, HDH])
        neg_null = sb("h_neg_null", [P, QB, HEADS])
        prob = [sb(f"h_prob{i}", [P, NKV]) for i in range(2)]
        probs_t = [sb(f"h_probs_t{i}", [P, KT, P]) for i in range(2)]
        neg_max = sb("h_neg_max", [P, 2, HEADS])
        total = sb("h_total", [P, 2, HEADS])
        null_gap = sb("h_null_gap", [P, 2, HEADS])
        null_exp = sb("h_null_exp", [P, 2, HEADS])
        inv = sb("h_inv", [P, 2, HEADS])
        att = sb("h_att", [P, HEADS, DH])
        att_t = sb("h_att_t", [P, KC, P])
        res = [sb(f"h_res{i}", [P, DIM]) for i in range(2)]

        ps_s = [ps(f"h_ps_s{i}", [P, 2, 512]) for i in range(2)]
        ps_t = [ps(f"h_ps_t{i}", [P, KT // 2, P]) for i in range(2)]
        ps_o = ps("h_ps_o", [P, HEADS, DH])
        ps_x = ps("h_ps_x", [P, 512])

        gathered = [sem(f"h_gathered{i}") for i in range(SLOTS)]
        res_out = [sem(f"h_res_out{i}") for i in range(2)]
        (normed, xt_turned, xt_hi_kept, xt_kept, projected, hi_kept, lo_kept, v_kept, group_used, doubled, null_made,
         null_kept, s_made, max_step, max_made, exp_made, pt_made, pt_kept_dve, pt_kept_act, o_made, gap_made,
         null_exp_made, null_part_made, inv_step, o_read, att_made, att_turned, att_kept, out_made, res_made) = (
             sem("h_" + n) for n in (
                 "normed xt_turned xt_hi_kept xt_kept projected hi_kept lo_kept v_kept group_used doubled null_made "
                 "null_kept s_made max_step max_made exp_made pt_made pt_kept_dve pt_kept_act o_made gap_made "
                 "null_exp_made null_part_made inv_step o_read att_made att_turned att_kept out_made res_made").split())
        ident = keep["ident"]

        def entry(name, b, n):
            at = b * KVB + n if n < QB else (b + BATCH) * KVB + n - QB
            flat = lists[name][:, :, :].rearrange("p r h -> p (r h)")
            return flat[:, at:at + 1] if isinstance(at, int) else flat[:, bass.ds(at, 1)]

        def bank(m):
            return ps_s[m % 4 // 2][:, m % 2, :]

        with nc.Block() as block:

            @block.sync
            def _(sp):
                with sp.Fori(0, BATCH) as b:
                    for g in range(KVG):
                        cols = slice(g * GT * P, (g + 1) * GT * P)
                        sp.wait_ge(lo_kept, b * ROWT + GT * (g + 2))
                        for odd in range(2):
                            for k2 in (k2_hi, k2_lo):
                                mine, other = slice(odd * DH, odd * DH + DH), slice(DH - odd * DH, P - odd * DH)
                                sp.dma_start(k2[other, odd::2, cols].bitcast(F32), k2[mine, odd::2, cols].bitcast(F32)).then_inc(doubled, 16)

            def scatter(pool, t):
                pool.wait_ge(res_made, t + 1)
                nc.gpsimd.indirect_dma_start(
                    out=out_rows, out_offset=bass.IndirectOffsetOnAxis(ap=entry("token", t // QB, t % QB), axis=0),
                    in_=res[t % 2][:, :], in_offset=None, compute_op=ALU.add).then_inc(res_out[t % 2], 16)

            @block.gpsimd
            def _(pool):
                def gather(n):
                    if n >= SLOTS:
                        pool.wait_ge(xt_turned, n - SLOTS + 1)
                    b, t = n // ROWT, n % ROWT
                    nc.gpsimd.indirect_dma_start(
                        out=rows_in[n % SLOTS][:, :], out_offset=None, in_=x2_rows,
                        in_offset=bass.IndirectOffsetOnAxis(ap=entry("token", b, t), axis=0)).then_inc(gathered[n % SLOTS], 16)

                for n in range(SLOTS):
                    gather(n)
                for b in range(BATCH):
                    for n in range(b * ROWT + SLOTS, min((b + 1) * ROWT + SLOTS, BATCH * ROWT)):
                        gather(n)
                    for qt in range(QB):
                        t = b * QB + qt
                        pool.wait_ge(null_exp_made, t + 1)
                        pool.wait_ge(att_turned, t)
                        nc.gpsimd.tensor_tensor(att[:, :, :], w["null_v"][:, :].rearrange("p (h d) -> p h d", h=HEADS),
                                                spread(null_exp[:, qt % 2, :], [1, HEADS], [0, DH]),
                                                ALU.mult).then_inc(null_part_made, 1)
                        if t >= 1:
                            scatter(pool, t - 1)
                scatter(pool, LAST)
                for i in range(2):
                    pool.wait_ge(res_out[i], 16 * BATCH * QB // 2)

            @block.tensor
            def _(pe):
                def turn_rows(b, n):
                    pe.wait_ge(normed, b * ROWT + n + 1)
                    if n >= 2:
                        pe.wait_ge(xt_kept, b * ROWT + n - 1)
                    for k in range(KC):
                        last = nc.tensor.transpose(ps_t[n % 2][:, k, :], rows_in[n % SLOTS][:, k * P:(k + 1) * P], ident[:, :])
                    last.then_inc(xt_turned, 1)

                def project_t(b, m, hi, lo, a):
                    for k in range(KC):
                        cols = slice(a * P, (a + 1) * P)
                        last = product(nc, bank(m), (hi[:, k, cols], lo[:, k, cols]), (xt_hi[:, k, :], xt_lo[:, k, :]),
                                       k == 0, k == KC - 1)
                    last.then_inc(projected, 1)

                def project_v(b, m, t):
                    for k in range(KC):
                        cols = slice(t * P, (t + 1) * P)
                        last = product(nc, bank(m), (xt_hi[:, k, cols], xt_lo[:, k, cols]),
                                       (w["v_hi"][:, k, :], w["v_lo"][:, k, :]), k == 0, k == KC - 1)
                    return last

                def null_scores(b):
                    pe.wait_ge(res_made, b * QB)
                    for qt in range(QB):
                        for h in range(HEADS):
                            at = (qt * HEADS + h) * 2
                            last = nc.tensor.matmul(ps_x[:, at:at + 2], q2[:, h, qt * P:(qt + 1) * P], w["null_k"][:, h, :],
                                                    start=True, stop=True)
                    last.then_inc(null_made, 1)

                def scores(b, i):
                    qt, h = i // HEADS, i % HEADS
                    if i == 0:
                        pe.wait_ge(v_kept, b * KT + KT)
                        pe.wait_ge(doubled, b * KVG * 64 + KVG * 64)
                    if i >= 2:
                        pe.wait_ge(exp_made, b * STEPS + i - 1)
                    for half in range(2):
                        cols = slice(half * 512, half * 512 + 512)
                        left = q2[:, h, qt * P:(qt + 1) * P]
                        nc.tensor.matmul(ps_s[i % 2][:, half, :], left, k2_hi[:, h, cols], start=True, stop=False)
                        last = nc.tensor.matmul(ps_s[i % 2][:, half, :], left, k2_lo[:, h, cols], start=False, stop=True)
                    last.then_inc(s_made, 1)

                def turn_probs(b, i):
                    pe.wait_ge(exp_made, b * STEPS + i + 1)
                    for half in range(2):
                        if i >= 1:
                            pe.wait_ge((pt_kept_dve, pt_kept_act)[half], b * STEPS + i)
                        for n in range(KT // 2):
                            at = (half * (KT // 2) + n) * P
                            last = nc.tensor.transpose(ps_t[half][:, n, :], prob[i % 2][:, at:at + P], ident[:, :])
                        last.then_inc(pt_made, 1)

                def attend(b, i):
                    qt, h = i // HEADS, i % HEADS
                    pe.wait_ge(pt_kept_dve, b * STEPS + i + 1)
                    pe.wait_ge(pt_kept_act, b * STEPS + i + 1)
                    if h == 0:
                        pe.wait_ge(o_read, b * QB + qt)
                    for n in range(KT):
                        last = nc.tensor.matmul(ps_o[:, h, :], probs_t[i % 2][:, n, :], val[:, n, h * DH:(h + 1) * DH],
                                                start=(n == 0), stop=(n == KT - 1))
                    last.then_inc(o_made, 1)

                def turn_att(b, qt):
                    pe.wait_ge(att_made, b * QB + qt + 1)
                    pe.wait_ge(null_kept, b + 1)
                    pe.wait_ge(res_made, b * QB + qt)
                    for k in range(KC):
                        last = nc.tensor.transpose(ps_x[:, k * P:(k + 1) * P],
                                                   att[:, 2 * k:2 * k + 2, :].rearrange("p h d -> p (h d)"), ident[:, :])
                    last.then_inc(att_turned, 1)

                def project_out(b, qt):
                    pe.wait_ge(att_kept, b * QB + qt + 1)
                    for k in range(KC):
                        last = nc.tensor.matmul(ps_x[:, :], att_t[:, k, :], w["out"][:, k, :],
                                                start=(k == 0), stop=(k == KC - 1))
                    last.then_inc(out_made, 1)

                with pe.Fori(0, BATCH) as b:
                    for n in range(GT):
                        turn_rows(b, n)
                    pe.wait_ge(xt_kept, b * ROWT + GT)
                    for a in range(PAIRS):
                        project_t(b, a, w["q_hi"], w["q_lo"], a)
                    for g in range(1, GROUPS):
                        for n in range(g * GT, (g + 1) * GT):
                            turn_rows(b, n)
                        pe.wait_ge(xt_kept, b * ROWT + (g + 1) * GT)
                        for a in range(PAIRS):
                            if g == 1:
                                pe.wait_ge(lo_kept, b * ROWT + a + 1)
                            else:
                                pe.wait_ge(v_kept, b * KT + (g - 2) * GT + a + 1)
                            project_t(b, g * 8 - 4 + a, w["k_hi"], w["k_lo"], a)
                        if g == 1:
                            null_scores(b)
                        for t in range(GT):
                            pe.wait_ge(lo_kept, b * ROWT + g * GT + t + 1)
                            last = project_v(b, g * 8 + t, t)
                            last.then_inc(projected, 1)
                    for i in range(2):
                        scores(b, i)
                    for i in range(STEPS + 3):
                        if i < STEPS:
                            turn_probs(b, i)
                        if i + 2 < STEPS:
                            scores(b, i + 2)
                        if 1 <= i <= STEPS:
                            attend(b, i - 1)
                        if i % HEADS == 1 and i > HEADS:
                            turn_att(b, i // HEADS - 1)
                        if i % HEADS == 2 and i > HEADS:
                            project_out(b, i // HEADS - 1)

            @block.scalar
            def _(act):
                def keep_rows(b, n):
                    act.wait_ge(xt_turned, b * ROWT + n + 1)
                    if n % GT == 0:
                        act.wait_ge(projected, b * 20 + (0, 4, 12)[n // GT])
                    nc.scalar.activation(xt_hi[:, :, n % GT * P:(n % GT + 1) * P], ps_t[n % 2][:, :, :],
                                         ACT.Identity).then_inc(xt_hi_kept, 1)

                def keep_hi(b, m, dst, cols, n):
                    act.wait_ge(projected, b * 20 + m + 1)
                    for odd in range(2):
                        mine = slice(odd * DH, odd * DH + DH)
                        last = nc.scalar.activation(dst[mine, 2 * (m % 4) + odd, cols], bank(m)[mine, :], ACT.Identity)
                    last.then_inc(hi_kept, 1)

                def exponential(b, i):
                    qt, h = i // HEADS, i % HEADS
                    act.wait_ge(max_made, b * STEPS + i + 1)
                    if i >= 2:
                        act.wait_ge(pt_made, 2 * (b * STEPS + i) - 2)
                    nc.scalar.activation(prob[i % 2][:, :].rearrange("p (a k) -> p a k", a=2), ps_s[i % 2][:, :, :], ACT.Exp,
                                         bias=neg_max[:, qt % 2, h:h + 1],
                                         accum_out=total[:, qt % 2, h:h + 1]).then_inc(exp_made, 1)

                nc.scalar.preload_act_table_set("natural_log_exp_and_others")
                with act.Fori(0, BATCH) as b:
                    for g in range(GROUPS):
                        for n in range(g * GT, (g + 1) * GT):
                            keep_rows(b, n)
                        if g == 0:
                            for a in range(PAIRS):
                                keep_hi(b, a, q2, slice(0, NQ), a)
                            continue
                        for a in range(PAIRS):
                            keep_hi(b, g * 8 - 4 + a, k2_hi, slice((g - 1) * GT * P, g * GT * P), a)
                        for t in range(GT):
                            m = g * 8 + t
                            act.wait_ge(projected, b * 20 + m + 1)
                            nc.scalar.activation(val[:, (g - 1) * GT + t, :], bank(m), ACT.Identity,
                                                 scale=entry("factor", b, g * GT + t)).then_inc(v_kept, 1)
                    exponential(b, 0)
                    for i in range(STEPS + 3):
                        if i + 1 < STEPS:
                            exponential(b, i + 1)
                        if i < STEPS:
                            act.wait_ge(pt_made, 2 * (b * STEPS + i) + 2)
                            nc.scalar.activation(probs_t[i % 2][:, KT // 2:, :], ps_t[1][:, :, :],
                                                 ACT.Identity).then_inc(pt_kept_act, 1)
                        if i % HEADS == HEADS - 2 and i < STEPS:
                            qt = i // HEADS
                            act.wait_ge(gap_made, b * QB + qt + 1)
                            nc.scalar.activation(null_exp[:, qt % 2, :], null_gap[:, qt % 2, :], ACT.Exp).then_inc(null_exp_made, 1)
                        if i % HEADS == 1 and i > HEADS:
                            act.wait_ge(att_turned, b * QB + i // HEADS)
                            nc.scalar.activation(att_t[:, :, :].rearrange("p k t -> p (k t)"), ps_x[:, :],
                                                 ACT.Identity).then_inc(att_kept, 1)

            @block.vector
            def _(v):
                def normalise(b, n):
                    slot = n % SLOTS
                    v.wait_ge(gathered[slot], (b * (ROWT // SLOTS) + n // SLOTS + 1) * 16)
                    nc.vector.tensor_scalar(rows_in[slot][:, :], rows_in[slot][:, :], entry("mean", b, n), entry("scale", b, n),
                                            ALU.subtract, ALU.mult).then_inc(normed, 1)

                def keep_rows_lo(b, n):
                    v.wait_ge(xt_hi_kept, b * ROWT + n + 1)
                    at = slice(n % GT * P, (n % GT + 1) * P)
                    nc.vector.tensor_tensor(xt_lo[:, :, at], ps_t[n % 2][:, :, :], xt_hi[:, :, at].bitcast(F32),
                                            ALU.subtract).then_inc(xt_kept, 1)

                def keep_lo(b, m, n):
                    v.wait_ge(hi_kept, b * ROWT + n + 1)
                    for odd in range(2):
                        mine, other = slice(odd * DH, odd * DH + DH), slice(DH - odd * DH, P - odd * DH)
                        h = 2 * (m % 4) + odd
                        if n < GT:
                            last = nc.vector.tensor_tensor(q2[other, h, :], bank(m)[mine, :], q2[mine, h, :].bitcast(F32),
                                                           ALU.subtract)
                        else:
                            cols = slice((n // GT - 1) * GT * P, n // GT * GT * P)
                            last = nc.vector.tensor_tensor(k2_lo[mine, h, cols], bank(m)[mine, :],
                                                           k2_hi[mine, h, cols].bitcast(F32), ALU.subtract)
                    last.then_inc(lo_kept, 1)

                def maximum(b, i):
                    qt, h = i // HEADS, i % HEADS
                    at = neg_max[:, qt % 2, h:h + 1]
                    v.wait_ge(s_made, b * STEPS + i + 1)
                    nc.vector.tensor_reduce(at, ps_s[i % 2][:, :, :].rearrange("p a k -> p (a k)"), AX_X, ALU.max,
                                            negate=True).then_inc(max_step, 1)
                    v.wait_ge(max_step, b * STEPS + i + 1)
                    nc.vector.tensor_tensor(at, at, neg_null[:, qt, h:h + 1], ALU.min).then_inc(max_made, 1)

                with v.Fori(0, BATCH) as b:
                    normalise(b, 0)
                    for g in range(GROUPS):
                        for n in range(g * GT, (g + 1) * GT):
                            if n + 1 < ROWT:
                                normalise(b, n + 1)
                            keep_rows_lo(b, n)
                        for a in range(PAIRS):
                            keep_lo(b, a if g == 0 else g * 8 - 4 + a, g * GT + a)
                        if g == 1:
                            v.wait_ge(null_made, b + 1)
                            pairs = ps_x[:, 0:2 * STEPS].rearrange("p (i w) -> p i w", w=2)
                            nc.vector.tensor_reduce(neg_null[:, :, :].rearrange("p q h -> p (q h)"), pairs, AX_X, ALU.add,
                                                    negate=True).then_inc(null_kept, 1)
                            v.wait_ge(null_kept, b + 1)
                    for i in range(2):
                        maximum(b, i)
                    for i in range(STEPS + 3):
                        if i < STEPS:
                            v.wait_ge(pt_made, 2 * (b * STEPS + i) + 1)
                            if i >= 2:
                                v.wait_ge(o_made, b * STEPS + i - 1)
                            nc.vector.tensor_copy(probs_t[i % 2][:, 0:KT // 2, :], ps_t[0][:, :, :]).then_inc(pt_kept_dve, 1)
                        if i + 2 < STEPS:
                            maximum(b, i + 2)
                        qt = i // HEADS
                        if i % HEADS == HEADS - 3 and i < STEPS:
                            v.wait_ge(max_made, b * STEPS + i + 3)
                            nc.vector.tensor_tensor(null_gap[:, qt % 2, :], neg_max[:, qt % 2, :], neg_null[:, qt, :],
                                                    ALU.subtract).then_inc(gap_made, 1)
                        if i % HEADS == HEADS - 1 and i < STEPS:
                            v.wait_ge(null_exp_made, b * QB + qt + 1)
                            v.wait_ge(exp_made, b * STEPS + i + 1)
                            nc.vector.tensor_tensor(inv[:, qt % 2, :], total[:, qt % 2, :], null_exp[:, qt % 2, :],
                                                    ALU.add).then_inc(inv_step, 1)
                            v.wait_ge(inv_step, (b * QB + qt) * 2 + 1)
                            nc.vector.reciprocal(inv[:, qt % 2, :], inv[:, qt % 2, :]).then_inc(inv_step, 1)
                        if i % HEADS == 0 and i > 0:
                            qt -= 1
                            v.wait_ge(o_made, b * STEPS + i)
                            v.wait_ge(null_part_made, b * QB + qt + 1)
                            nc.vector.tensor_tensor(att[:, :, :], ps_o[:, :, :], att[:, :, :], ALU.add).then_inc(o_read, 1)
                            v.wait_ge(o_read, b * QB + qt + 1)
                            v.wait_ge(inv_step, (b * QB + qt) * 2 + 2)
                            nc.vector.tensor_tensor(att[:, :, :], att[:, :, :], spread(inv[:, qt % 2, :], [1, HEADS], [0, DH]),
                                                    ALU.mult).then_inc(att_made, 1)
                        if i % HEADS == 2 and i > HEADS:
                            qt -= 1
                            v.wait_ge(out_made, b * QB + qt + 1)
                            v.wait_ge(res_out[qt % 2], (b * (QB // 2) + qt // 2) * 16)
                            nc.vector.scalar_tensor_tensor(out=res[qt % 2][:, :], in0=ps_x[:, :], scalar=entry("factor", b, qt),
                                                           in1=w["null_row"][:, :], op0=ALU.mult,
                                                           op1=ALU.subtract).then_inc(res_made, 1)


def ssm_then_routed_attention(nc, x, log_A, B_param, C, D, ln_g, ln_b, w_qkv, w_out, null_q, rt_q, rt_kv,
                              rms_g, w_q_h, w_kv_h, null_kv, w_out_h, out):
    kpad = nc.dram_tensor("taps_padded", (DIM, KPAD), F32, kind="Internal").ap()
    x2 = nc.dram_tensor("x2", (BATCH, SEQ, DIM), F32, kind="Internal").ap()

    with ExitStack() as whole:
        sb, _, _ = open_tensors(nc, whole)
        keep = {"ident": sb("ident", [P, P]), "steps": sb("steps", [P, P + 1])}
        lists = {n: sb(f"list_{n}", [P, ROWS, max(QB, KVB)], I32 if n == "token" else F32)
                 for n in ("token", "factor", "mean", "scale")}

        with ExitStack() as convolution:
            sb, _, _ = open_tensors(nc, convolution)
            keep |= {n: sb(n, [P, CPAIRS]) for n in ("ea", "cb", "log_abar")}
            keep |= {n: sb(n, [P, TILES]) for n in ("mean", "rstd")}
            keep["to_end_rate"] = sb("to_end_rate", [P, 1])
            prepare_phase(nc, x, log_A, B_param, C, D, keep, kpad)
            conv_phase(nc, x, log_A, keep, kpad, x2)

        with ExitStack() as scores:
            sb, _, _ = open_tensors(nc, scores)
            keep |= {n: sb(n, [P, TILES]) for n in ("mean2", "rms_scale")}
            s_all = sb("s_all", [P, ROUTES, TILES])
            with ExitStack() as light:
                sb, _, _ = open_tensors(nc, light)
                keep |= {n: sb(n, [P, TILES]) for n in ("rstd2", "rstd3", "shift2", "rstd23", "shift23")}
                w = {"rt": sb("w_rt", [P, ROUTES, DIM]), "row": sb("w_row", [P, DIM])}
                w |= {n: sb(f"w_{n}", [P, PAIRS]) for n in ("bias_q", "bias_k")}
                w |= {n: sb(f"w_{n}", [P, KC, QKV], F32R) for n in ("qkv_hi", "qkv_lo")}
                w |= {n: sb(f"w_{n}", [P, KC, DIM], F32R) for n in ("out_hi", "out_lo")}
                stats_phase(nc, x2, keep)
                light_weights_phase(nc, ln_g, ln_b, w_qkv, w_out, null_q, rt_q, rt_kv, w)
                light_phase(nc, x2, out, w, keep, s_all)
            routing_phase(nc, s_all, keep, lists)

        with ExitStack() as heavy:
            sb, _, _ = open_tensors(nc, heavy)
            w = {n: sb(f"hw_{n}", [P, KC, HDH], F32R) for n in ("q_hi", "q_lo", "k_hi", "k_lo", "v_hi", "v_lo")}
            w |= {"out": sb("hw_out", [P, KC, DIM]), "null_k": sb("hw_null_k", [P, HEADS, 2], F32R)}
            w |= {n: sb(f"hw_{n}", [P, DIM]) for n in ("null_v", "null_row")}
            heavy_weights_phase(nc, rms_g, w_q_h, w_kv_h, null_kv, w_out_h, null_q, w)
            heavy_phase(nc, x2, out, w, keep, lists)


_INS = ["L0_attn_x", "L0_attn_log_A", "L0_attn_B_param", "L0_attn_C", "L0_attn_D", "L0_ffn_ln_g", "L0_ffn_ln_b",
        "L0_ffn_w_qkv_l", "L0_ffn_w_out_l", "L0_ffn_null_q", "L0_ffn_rt_q", "L0_ffn_rt_kv", "L0_ffn_rms_g",
        "L0_ffn_w_q_h", "L0_ffn_w_kv_h", "L0_ffn_null_kv", "L0_ffn_w_out_h"]
_OUT = (BATCH, SEQ, DIM)


def kernel(**inputs):
    import numpy as _np
    import concourse.bacc as _bacc
    from concourse import mybir as _mybir
    from concourse.bass_utils import run_bass_kernel_spmd as _run

    nc = _bacc.Bacc("TRN2", target_bir_lowering=False, num_devices=1)
    arrays, args = {}, []
    for name in _INS:
        a = _np.ascontiguousarray(inputs[name])
        arrays[f"in_{name}_dram"] = a
        args.append(nc.dram_tensor(f"in_{name}_dram", a.shape, _mybir.dt.from_np(a.dtype), kind="ExternalInput").ap())
    args.append(nc.dram_tensor("out_dram", _OUT, _mybir.dt.float32, kind="ExternalOutput").ap())
    ssm_then_routed_attention(nc, *args)
    return _run(nc, [arrays], core_ids=[0]).results[0]["out_dram"]
```

```python
from contextlib import ExitStack

import numpy as np

import concourse.bass as bass
import concourse.mybir as mybir

F32 = mybir.dt.float32
I32 = mybir.dt.int32
U32 = mybir.dt.uint32
BF16 = mybir.dt.bfloat16
F32R = mybir.dt.float32r
ALU = mybir.AluOpType
ACT = mybir.ActivationFunctionType
AX_X = mybir.AxisListType.X

P = 128
BATCH, SEQ, DIM, STATE = 8, 2048, 512, 64
HEADS, DH = 8, 64
HDH = HEADS * DH
QKV = 3 * HDH
WIN = 64
PAIRS = HEADS // 2
CHUNK = P
NCH = SEQ // CHUNK
TILES = BATCH * NCH
KC = DIM // P
DT = 0.1
EPS = 1e-5
N_ITERS = 50
NQ, NKV = 512, 1024
K_EFF_Q, K_EFF_KV = 576.0, 1152.0

CPAIRS = DIM // 2
SUB = 16
SPAIRS = SUB // 2
NSUB = DIM // SUB
SUBS_PER_GROUP = P // SUB
KPAD = 2 * CHUNK - 1


def open_tensors(nc, ctx, dtype=F32):
    def sb(name, shape, dt=dtype):
        return ctx.enter_context(nc.sbuf_tensor(name, shape, dt))

    def ps(name, shape, dt=dtype):
        return ctx.enter_context(nc.psum_tensor(name, shape, dt))

    def sem(name):
        return ctx.enter_context(nc.semaphore(name))

    return sb, ps, sem


def spread(ap, *dims):
    return bass.AP(tensor=ap.tensor, offset=ap.offset, ap=[list(ap.ap[0])] + [list(d) for d in dims])


def wait(eng, sem, value):
    if not isinstance(value, int) or value > 0:
        eng.wait_ge(sem, value)


def each(eng, count, body):
    body(0)
    with eng.Fori(1, count) as i:
        body(i)


def columns(at, n):
    return slice(at, at + n) if isinstance(at, int) else bass.ds(at, n)


def prepare_phase(nc, x, log_A, B_param, C, D, keep, kpad):
    tiles_per_load = 4
    loads = TILES // tiles_per_load
    x_rows = x.rearrange("b (c p) d -> p (b c) d", p=P)

    with ExitStack() as ctx:
        sb, ps, sem = open_tensors(nc, ctx)
        xin = [sb(f"xin{i}", [P, tiles_per_load, DIM]) for i in range(4)]
        bn = sb("bn", [P, TILES, 6])
        raw = sb("raw", [P, 3, 2, P])
        b_t = sb("b_t", [P, CPAIRS])
        c_t = sb("c_t", [P, CPAIRS])
        abar = sb("abar", [P, CPAIRS])
        cb_two = sb("cb_two", [P, CPAIRS, 2])
        powers = [sb(f"powers{i}", [P, SPAIRS, CHUNK]) for i in range(2)]
        taps_t = sb("taps_t", [P, DIM])
        krow = sb("krow", [P, KC, KPAD])
        dcol = sb("dcol", [P, KC])
        tmp = sb("tmp", [P, TILES])
        tmp2 = sb("tmp2", [P, TILES])
        to_end = sb("to_end", [P, 1])
        steps_back = sb("steps_back", [P, CHUNK])
        ps_t = ps("ps_t", [P, 3, 4, P])
        ps_taps = [ps(f"ps_taps{i}", [P, 512]) for i in range(2)]
        ps_rows = ps("ps_rows", [P, KC, P])

        x_in = [sem(f"x_in{i}") for i in range(4)]
        par_in = sem("par_in")
        ident_made = sem("ident_made")
        iota_made = sem("iota_made")
        stats_done = sem("stats_done")
        par_turned = sem("par_turned")
        rates = sem("rates")
        act_chain = sem("act_chain")
        dve = sem("dve")
        cb_made = sem("cb_made")
        powers_made = sem("powers_made")
        taps_made = sem("taps_made")
        taps_kept = sem("taps_kept")
        rows_turned = sem("rows_turned")
        krow_made = sem("krow_made")
        sqrt_done = sem("sqrt_done")
        kpad_out = sem("kpad_out")

        ea = sb("ea", [P, CPAIRS])
        mean, rstd, cb = keep["mean"], keep["rstd"], keep["cb"]
        ident, steps = keep["ident"], keep["steps"]

        with nc.Block() as block:

            @block.sync
            def _(sp):
                for n, a in enumerate((log_A, B_param, C)):
                    rows = a.rearrange("(h p two) n -> p h (two n)", p=P, two=2)
                    sp.dma_start(raw[:, n], rows).then_inc(par_in, 16)
                sp.dma_start(dcol[:, :], D.rearrange("(g p) -> p g", p=P),
                             allow_slow_non_contiguous=True).then_inc(par_in, 16)
                for t in range(loads):
                    if t >= 4:
                        sp.wait_ge(stats_done, (t - 3) * tiles_per_load)
                    sp.dma_start(xin[t % 4][:, :, :],
                                 x_rows[:, t * tiles_per_load:(t + 1) * tiles_per_load, :]).then_inc(x_in[t % 4], 16)
                sp.wait_ge(krow_made, 1)
                sp.dma_start(kpad.rearrange("(g p) k -> p g k", p=P), krow[:, :, :]).then_inc(kpad_out, 16)
                sp.wait_ge(kpad_out, 16)

            @block.gpsimd
            def _(pool):
                nc.gpsimd.memset(ident[:, :], 0.0).then_inc(ident_made, 1)
                pool.wait_ge(ident_made, 1)
                nc.gpsimd.affine_select(out=ident[:, :], in_=ident[:, :], compare_op=ALU.not_equal, fill=1.0,
                                        base=0, pattern=[[-1, P]], channel_multiplier=1).then_inc(ident_made, 1)
                nc.gpsimd.iota(steps[:, :], pattern=[[1, CHUNK + 1]], base=0, channel_multiplier=0,
                               allow_small_or_imprecise_dtypes=True).then_inc(iota_made, 1)
                nc.gpsimd.iota(to_end[:, :], pattern=[[0, 1]], base=CHUNK - 1, channel_multiplier=-1,
                               allow_small_or_imprecise_dtypes=True).then_inc(iota_made, 1)
                nc.gpsimd.iota(steps_back[:, :], pattern=[[-1, CHUNK]], base=CHUNK - 1, channel_multiplier=0,
                               allow_small_or_imprecise_dtypes=True).then_inc(iota_made, 1)
                nc.gpsimd.memset(cb_two[:, :, :], 0.0).then_inc(iota_made, 1)
                nc.gpsimd.memset(krow[:, :, :], 0.0).then_inc(iota_made, 1)

            @block.tensor
            def _(pe):
                pe.wait_ge(par_in, 64)
                pe.wait_ge(ident_made, 2)
                for n in range(3):
                    for h in range(2):
                        last = nc.tensor.transpose(ps_t[:, n, h, :], raw[:, n, h, :], ident[:, :])
                last.then_inc(par_turned, 1)
                pe.wait_ge(cb_made, 1)
                def taps_of_two(s2):
                    for par in range(2):
                        pe.wait_ge(powers_made, s2 * 2 + par + 1)
                        wait(pe, taps_kept, s2 * 2 + par)
                        for q in range(SPAIRS):
                            last = nc.tensor.matmul(ps_taps[par][:, 2 * q:2 * q + 2], powers[par][:, q, :],
                                                    cb_two[:, columns((s2 * 2 + par) * SPAIRS + q, 1), :],
                                                    start=True, stop=True)
                        last.then_inc(taps_made, 1)

                each(pe, NSUB // 2, taps_of_two)
                pe.wait_ge(taps_kept, NSUB)
                for g in range(KC):
                    last = nc.tensor.transpose(ps_rows[:, g, :], taps_t[:, g * P:(g + 1) * P], ident[:, :])
                last.then_inc(rows_turned, 1)

            @block.scalar
            def _(act):
                act.wait_ge(par_turned, 1)
                nc.scalar.activation(ea[:, :], ps_t[:, 0, 0:2].rearrange("p h k -> p (h k)"), ACT.Exp).then_inc(act_chain, 1)
                act.wait_ge(act_chain, 1)
                nc.scalar.activation(abar[:, :], ea[:, :], ACT.Exp, scale=-DT).then_inc(rates, 1)
                act.wait_ge(dve, 3)
                act.wait_ge(iota_made, 3)
                def powers_of_two(s2):
                    for par in range(2):
                        wait(act, taps_made, s2 * 2)
                        for q in range(SPAIRS):
                            last = nc.scalar.activation(
                                powers[par][:, q, :], steps_back[:, :], ACT.Exp,
                                scale=keep["log_abar"][:, columns((s2 * 2 + par) * SPAIRS + q, 1)])
                        last.then_inc(powers_made, 1)

                each(act, NSUB // 2, powers_of_two)
                act.wait_ge(sqrt_done, 1)
                nc.scalar.activation(tmp2[:, :], tmp[:, :], ACT.Sqrt).then_inc(sqrt_done, 1)

            @block.vector
            def _(v):
                v.wait_ge(par_turned, 1)
                nc.vector.tensor_copy(b_t[:, :], ps_t[:, 1, 0:2].rearrange("p h k -> p (h k)")).then_inc(dve, 1)
                nc.vector.tensor_copy(c_t[:, :], ps_t[:, 2, 0:2].rearrange("p h k -> p (h k)")).then_inc(dve, 1)
                v.wait_ge(rates, 1)
                nc.vector.tensor_scalar(keep["log_abar"][:, :], ea[:, :], -DT, None, ALU.mult).then_inc(dve, 1)
                nc.vector.tensor_scalar(abar[:, :], abar[:, :], -1.0, 1.0, ALU.mult, ALU.add).then_inc(dve, 1)
                nc.vector.reciprocal(cb[:, :], ea[:, :]).then_inc(dve, 1)
                v.wait_ge(dve, 5)
                nc.vector.tensor_tensor(cb[:, :], cb[:, :], abar[:, :], ALU.mult).then_inc(dve, 1)
                v.wait_ge(dve, 6)
                nc.vector.tensor_tensor(cb[:, :], cb[:, :], b_t[:, :], ALU.mult).then_inc(dve, 1)
                v.wait_ge(dve, 7)
                nc.vector.tensor_tensor(cb[:, :], cb[:, :], c_t[:, :], ALU.mult).then_inc(dve, 1)
                v.wait_ge(dve, 8)
                v.wait_ge(iota_made, 5)
                nc.vector.tensor_scalar(keep["to_end_rate"][:, :], to_end[:, :], -DT, None, ALU.mult).then_inc(dve, 1)
                nc.vector.tensor_copy(cb_two[0:STATE, :, 0], cb[0:STATE, :]).then_inc(dve, 1)
                nc.vector.tensor_copy(cb_two[STATE:P, :, 1], cb[STATE:P, :]).then_inc(cb_made, 1)
                v.wait_ge(dve, 10)
                with v.Fori(0, loads // 4) as t4:
                    for i in range(4):
                        v.wait_ge(x_in[i], t4 * 16 + 16)
                        for n in range(tiles_per_load):
                            nc.vector.bn_stats(bn[:, bass.ds(t4 * 16 + i * tiles_per_load + n, 1), :],
                                               xin[i][:, n, :]).then_inc(stats_done, 1)
                        v.wait_ge(taps_made, t4 * 4 + i + 1)
                        nc.vector.tensor_copy(taps_t[:, bass.ds((t4 * 4 + i) * SUB, SUB)],
                                              ps_taps[i % 2][:, 0:SUB]).then_inc(taps_kept, 1)
                v.wait_ge(stats_done, TILES)
                finish_stats(nc, v, dve, 10, bn, mean, rstd, tmp, tmp2, sqrt_done)
                v.wait_ge(rows_turned, 1)
                nc.vector.tensor_copy(krow[:, :, 0:CHUNK], ps_rows[:, :, :]).then_inc(dve, 1)
                v.wait_ge(dve, 10 + FINISH_STEPS + 1)
                nc.vector.tensor_tensor(krow[:, :, CHUNK - 1:CHUNK], krow[:, :, CHUNK - 1:CHUNK],
                                        spread(dcol[:, :], [1, KC], [1, 1]), ALU.add).then_inc(krow_made, 1)


FINISH_STEPS = 11


def finish_stats(nc, v, chain, n, bn, mean, rstd, tmp, tmp2, sqrt_done):
    half = DIM // 2

    def step(ins):
        nonlocal n
        n += 1
        ins.then_inc(chain, 1)
        v.wait_ge(chain, n)

    step(nc.vector.tensor_tensor(mean[:, :], bn[:, :, 1], bn[:, :, 4], ALU.add))
    step(nc.vector.tensor_scalar(mean[:, :], mean[:, :], 0.5, None, ALU.mult))
    step(nc.vector.tensor_tensor(tmp[:, :], bn[:, :, 1], bn[:, :, 4], ALU.subtract))
    step(nc.vector.scalar_tensor_tensor(out=tmp[:, :], in0=tmp[:, :], scalar=0.25, in1=tmp[:, :],
                                        op0=ALU.mult, op1=ALU.mult))
    step(nc.vector.tensor_tensor(tmp2[:, :], bn[:, :, 2], bn[:, :, 5], ALU.add))
    step(nc.vector.scalar_tensor_tensor(out=tmp[:, :], in0=tmp2[:, :], scalar=1.0 / (2 * half), in1=tmp[:, :],
                                        op0=ALU.mult, op1=ALU.add))
    nc.vector.tensor_scalar(tmp[:, :], tmp[:, :], EPS, None, ALU.add).then_inc(sqrt_done, 1)
    v.wait_ge(sqrt_done, 2)
    step(nc.vector.reciprocal(rstd[:, :], tmp2[:, :]))
    step(nc.vector.tensor_tensor(tmp2[:, :], rstd[:, :], rstd[:, :], ALU.mult))
    step(nc.vector.tensor_tensor(tmp2[:, :], tmp2[:, :], tmp[:, :], ALU.mult))
    step(nc.vector.tensor_scalar(tmp2[:, :], tmp2[:, :], -0.5, 1.5, ALU.mult, ALU.add))
    step(nc.vector.tensor_tensor(rstd[:, :], rstd[:, :], tmp2[:, :], ALU.mult))


def conv_phase(nc, x, log_A, keep, kpad, x2):
    COLS = NCH * BATCH
    x_v = x.rearrange("b (c p) d -> c p b d", p=P)
    x2_v = x2.rearrange("b (c p) d -> c p b d", p=P)
    groups = DIM // P
    SCAN = 2 * (NCH - 2)
    logA_flat = log_A.rearrange("d n -> (d n)")
    NEVER = -1e4
    BANKS = (0, 2, 1, 3)

    with ExitStack() as ctx:
        sb, ps, sem = open_tensors(nc, ctx)
        xg = [sb(f"xg{i}", [P, NCH, BATCH, P]) for i in range(2)]
        xn = [sb(f"xn{i}", [P, SUB, COLS]) for i in range(2)]
        toep_back = sb("toep_back", [P, SUB, CHUNK])
        toep = [sb(f"toep{i}", [P, SUB, CHUNK]) for i in range(2)]
        ea_all = sb("ea_all", [P, SUB * STATE])
        tail = sb("tail", [P, SUB * STATE])
        powers = [sb(f"cpow{i}", [P, SUB, CHUNK]) for i in range(2)]
        log_own = sb("log_own", [P, CPAIRS, 2])
        state = [sb(f"state{i}", [P, NCH, SPAIRS, BATCH]) for i in range(2)]
        decay = [sb(f"decay{i}", [P, SPAIRS]) for i in range(2)]
        carried = [sb(f"carried{i}", [P, SPAIRS, BATCH]) for i in range(2)]
        ps_state = [ps(f"ps_state{i}", [P, SPAIRS, COLS]) for i in range(2)]
        ps_y = [ps(f"ps_y{i}", [P, 4, COLS]) for i in range(4)]

        x_in = [sem(f"cx_in{i}") for i in range(2)]
        toep_in = sem("toep_in")
        toep_made = sem("toep_made")
        ea_in = sem("ea_in")
        ea_exp = sem("ea_exp")
        own_made = sem("own_made")
        tails_made = sem("tails_made")
        powers_made = sem("cpowers_made")
        normed = sem("normed")
        norm_step = sem("norm_step")
        states_summed = sem("states_summed")
        states_kept = sem("states_kept")
        carry = sem("carry")
        y_made = sem("y_made")
        y_added = sem("y_added")
        x2_out = [sem(f"x2_out{k}") for k in range(4)]

        mean, rstd, cb = keep["mean"], keep["rstd"], keep["cb"]

        def by_column(a):
            return spread(a[:, :], [0, SUB // 2], [1, NCH], [NCH, BATCH])

        with nc.Block() as block:

            @block.sync
            def _(sp):
                def quarter(k):
                    return range(k * NCH // 4, (k + 1) * NCH // 4)

                def load_quarter(g, k):
                    if g >= 2:
                        sp.wait_ge(x2_out[k], 16 * NCH // 4 * (g - 1))
                    for c in quarter(k):
                        sp.dma_start(xg[g % 2][:, c], x_v[c, :, :, g * P:(g + 1) * P]).then_inc(x_in[g % 2], 16)

                def store_quarter(g, k):
                    sp.wait_ge(y_added, 4 * SUBS_PER_GROUP * (g + 1))
                    for c in quarter(k):
                        sp.dma_start(x2_v[c, :, :, g * P:(g + 1) * P], xg[g % 2][:, c]).then_inc(x2_out[k], 16)

                def load_step(it):
                    if it >= 1:
                        sp.wait_ge(tails_made, it)
                    row = logA_flat[it * SUB * STATE:(it + 1) * SUB * STATE]
                    sp.dma_start(ea_all[:, :], bass.AP(tensor=row.tensor, offset=row.offset,
                                                       ap=[[0, P], [1, SUB * STATE]])).then_inc(ea_in, 16)
                    if it >= 1:
                        sp.wait_ge(toep_made, it)
                    sp.dma_start(toep_back[:, :, :],
                                 bass.AP(tensor=kpad.tensor, offset=kpad.offset + it * SUB * KPAD,
                                         ap=[[1, P], [KPAD, SUB], [1, CHUNK]])).then_inc(toep_in, 16)

                for k in range(4):
                    load_quarter(0, k)
                for it in range(NSUB):
                    load_step(it)
                    g, k = it // SUBS_PER_GROUP, it % SUBS_PER_GROUP - 1
                    if 0 <= k < 4 and g >= 1:
                        store_quarter(g - 1, k)
                    if 0 <= k - 1 < 4 and g + 1 < groups:
                        load_quarter(g + 1, k - 1)
                for k in range(4):
                    store_quarter(groups - 1, k)
                for k in range(4):
                    sp.wait_ge(x2_out[k], 16 * NCH // 4 * groups)

            @block.vector
            def _(v):
                HALF = SUB // 2

                def normalise(g, sub, it, par, h):
                    src = xg[g % 2][:, :, :, columns(sub * SUB + h * HALF, HALF)].rearrange("p c b d -> p d c b")
                    dst = xn[par][:, h * HALF:(h + 1) * HALF, :].rearrange("p d (c b) -> p d c b", c=NCH)
                    nc.vector.tensor_tensor(dst, src, by_column(mean), ALU.subtract).then_inc(norm_step, 1)
                    v.wait_ge(norm_step, it * 2 + h + 1)
                    nc.vector.tensor_tensor(dst, dst, by_column(rstd), ALU.mult).then_inc(normed, 1)

                def add_y(g, sub, f):
                    at = xg[g % 2][:, :, :, columns(sub * SUB, SUB)].rearrange(
                        "p c b (q two) -> p two q (c b)", two=2)[:, f // 2, f % 2 * 4:f % 2 * 4 + 4]
                    nc.vector.tensor_tensor(at, ps_y[f][:, :, :], at, ALU.add).then_inc(y_added, 1)

                def step(g, sub, it, par, g_next, sub_next):
                    for h in range(2):
                        v.wait_ge(y_made, it * 4 + 2 * h + 2)
                        if g_next is not None:
                            normalise(g_next, sub_next, it + 2, par, h)
                        for f in BANKS[2 * h:2 * h + 2]:
                            add_y(g, sub, f)

                nc.vector.memset(log_own[:, :, :], NEVER).then_inc(own_made, 1)
                v.wait_ge(own_made, 1)
                nc.vector.tensor_copy(log_own[0:STATE, :, 0], keep["log_abar"][0:STATE, :])
                nc.vector.tensor_copy(log_own[STATE:P, :, 1], keep["log_abar"][STATE:P, :]).then_inc(own_made, 1)
                v.wait_ge(x_in[0], 16 * NCH)
                for it in range(2):
                    for h in range(2):
                        normalise(0, it, it, it, h)
                for g in range(groups):
                    base = g * SUBS_PER_GROUP
                    with v.Fori(0, SUBS_PER_GROUP // 2 - 1) as s2:
                        for par in range(2):
                            sub = s2 * 2 + par
                            step(g, sub, sub + base, par, g, sub + 2)
                    for par in range(2):
                        sub = SUBS_PER_GROUP - 2 + par
                        if g + 1 < groups:
                            v.wait_ge(x_in[(g + 1) % 2], 16 * NCH * ((g + 1) // 2 + 1))
                            step(g, sub, base + sub, par, g + 1, par)
                        else:
                            step(g, sub, base + sub, par, None, None)

            @block.scalar
            def _(act):
                log_flat = log_own[:, :, :].rearrange("p q two -> p (q two)")

                def make_tails(it):
                    act.wait_ge(ea_in, it * 16 + 16)
                    nc.scalar.activation(ea_all[:, :], ea_all[:, :], ACT.Exp).then_inc(ea_exp, 1)
                    act.wait_ge(ea_exp, it + 1)
                    wait(act, states_summed, it * 2)
                    nc.scalar.activation(tail[:, :], ea_all[:, :], ACT.Exp,
                                         scale=keep["to_end_rate"][:, :]).then_inc(tails_made, 1)

                def make_powers(it, par):
                    for ch in range(SUB):
                        last = nc.scalar.activation(powers[par][:, ch, :], keep["steps"][:, 1:CHUNK + 1], ACT.Exp,
                                                    scale=log_flat[:, columns(it * SUB + ch, 1)])
                    last.then_inc(powers_made, 1)

                def keep_states(it, par):
                    for q in range(SPAIRS):
                        if q % 4 == 0:
                            act.wait_ge(states_summed, it * 2 + q // 4 + 1)
                        last = nc.scalar.activation(state[par][:, :, q, :],
                                                    ps_state[par][:, q, :].rearrange("p (c b) -> p c b", c=NCH),
                                                    ACT.Identity, scale=cb[:, columns(it * SPAIRS + q, 1)])
                    last.then_inc(states_kept, 1)

                def make_decay(it, par):
                    nc.scalar.activation(decay[par][:, :], keep["log_abar"][:, columns(it * SPAIRS, SPAIRS)], ACT.Exp,
                                         scale=float(CHUNK))

                def turn_toep(it, par):
                    act.wait_ge(toep_in, it * 16 + 16)
                    nc.scalar.activation(toep[par][:, :, :], toep_back[:, :, ::-1], ACT.Identity).then_inc(toep_made, 1)

                act.wait_ge(own_made, 2)
                make_tails(0)
                make_powers(0, 0)
                make_decay(0, 0)

                def act_step(it, par, ahead):
                    keep_states(it, par)
                    turn_toep(it, par)
                    if ahead:
                        make_tails(it + 1)
                        wait(act, y_made, it * 4)
                        make_powers(it + 1, 1 - par)
                        make_decay(it + 1, 1 - par)

                def act_steps(s2):
                    for par in range(2):
                        act_step(s2 * 2 + par, par, True)

                each(act, NSUB // 2 - 1, act_steps)
                act_step(NSUB - 2, 0, True)
                act_step(NSUB - 1, 1, False)

            @block.gpsimd
            def _(pool):
                with pool.Fori(0, NSUB // 2) as s2:
                    for par in range(2):
                        it = s2 * 2 + par
                        by_seq = spread(decay[par][:, :], [1, SPAIRS], [0, BATCH])
                        pool.wait_ge(states_kept, it + 1)
                        for c in range(1, NCH - 1):
                            if c > 1:
                                pool.wait_ge(carry, it * SCAN + 2 * (c - 1))
                            nc.gpsimd.tensor_tensor(carried[par][:, :, :], state[par][:, c - 1], by_seq,
                                                    ALU.mult).then_inc(carry, 1)
                            pool.wait_ge(carry, it * SCAN + 2 * c - 1)
                            nc.gpsimd.tensor_tensor(state[par][:, c], state[par][:, c], carried[par][:, :, :],
                                                    ALU.add).then_inc(carry, 1)

            @block.tensor
            def _(pe):
                def sum_states(it, par):
                    pe.wait_ge(tails_made, it + 1)
                    for q in range(SPAIRS):
                        if q % 4 == 0:
                            pe.wait_ge(normed, it * 2 + q // 4 + 1)
                        for two in range(2):
                            ch = 2 * q + two
                            last = nc.tensor.matmul(ps_state[par][two * STATE:(two + 1) * STATE, q, :],
                                                    tail[:, ch * STATE:(ch + 1) * STATE], xn[par][:, ch, :],
                                                    start=True, stop=True)
                        if q % 4 == 3:
                            last.then_inc(states_summed, 1)

                def make_y(it, par):
                    pe.wait_ge(toep_made, it + 1)
                    pe.wait_ge(powers_made, it + 1)
                    pe.wait_ge(carry, it * SCAN + SCAN)
                    for n, f in enumerate(BANKS):
                        wait(pe, y_added, (it - 1) * 4 + n + 1)
                        for i in range(4):
                            ch = 2 * (f % 2 * 4 + i) + f // 2
                            nc.tensor.matmul(ps_y[f][:, i, :], toep[par][:, ch, :], xn[par][:, ch, :],
                                             start=True, stop=False)
                            last = nc.tensor.matmul(ps_y[f][:, i, BATCH:], powers[par][:, ch, :],
                                                    state[par][:, 0:NCH - 1, ch // 2, :],
                                                    start=False, stop=True)
                        last.then_inc(y_made, 1)

                sum_states(0, 0)
                def pe_steps(s2):
                    for par in range(2):
                        wait(pe, states_kept, s2 * 2 + par)
                        sum_states(s2 * 2 + par + 1, 1 - par)
                        make_y(s2 * 2 + par, par)

                each(pe, NSUB // 2 - 1, pe_steps)
                pe.wait_ge(states_kept, NSUB - 2)
                sum_states(NSUB - 1, 1)
                make_y(NSUB - 2, 0)
                make_y(NSUB - 1, 1)


def light_weights(nc, ctx, ln_g, ln_b, w_qkv, w_out, null_q, rt_q, rt_kv, w):
    sb, ps, sem = open_tensors(nc, ctx)
    raw = sb("lw_raw", [P, KC, QKV])
    raw_o = sb("lw_raw_o", [P, KC, DIM])
    g_col = sb("lw_g", [P, KC])
    b_col = sb("lw_b", [P, KC])
    bias_v = sb("lw_bias_v", [P, KC])
    wide = sb("lw_wide", [P, KC, P])
    null_row = sb("lw_null", [P, DIM])
    ps_bias = ps("lw_ps_bias", [P, QKV // P])
    ps_row = ps("lw_ps_row", [P, DIM])
    loaded, bias_made, dve, hi_made, row_made = (sem(f"lw_{n}") for n in ("loaded", "bias", "dve", "hi", "row"))
    spread_made = sem("lw_spread")
    LOADS = 7

    def on_sync(sp):
        sp.dma_start(raw[:, :, :], w_qkv.rearrange("(k p) n -> p k n", p=P)).then_inc(loaded, 16)
        sp.dma_start(raw_o[:, :, :], w_out.rearrange("(k p) n -> p k n", p=P)).then_inc(loaded, 16)
        for col, src in ((g_col, ln_g), (b_col, ln_b)):
            sp.dma_start(col[:, :], src.rearrange("(k p) -> p k", p=P),
                         allow_slow_non_contiguous=True).then_inc(loaded, 16)
        for row, src in ((null_row[:, :], null_q), (w["rt"][:, 0], rt_q[0]), (w["rt"][:, 1], rt_kv[0])):
            sp.dma_start(row, bass.AP(tensor=src.tensor, offset=src.offset,
                                      ap=[[0, P], [1, DIM]])).then_inc(loaded, 16)

    def on_tensor(pe):
        pe.wait_ge(loaded, 16 * LOADS)
        for n in range(QKV // P):
            for k in range(KC):
                last = nc.tensor.matmul(ps_bias[:, n:n + 1], raw[:, k, n * P:(n + 1) * P], b_col[:, k:k + 1],
                                        start=(k == 0), stop=(k == KC - 1))
        last.then_inc(bias_made, 1)
        pe.wait_ge(spread_made, 1)
        for k in range(KC):
            last = nc.tensor.matmul(ps_row[:, :], wide[:, k, :], raw_o[:, k, :],
                                    start=(k == 0), stop=(k == KC - 1))
        last.then_inc(row_made, 1)

    def on_vector(v):
        v.wait_ge(loaded, 16 * LOADS)
        v.wait_ge(bias_made, 1)
        nc.vector.tensor_scalar(w["bias_q"][:, :], ps_bias[:, 0:4], DH ** -0.5, None, ALU.mult)
        nc.vector.tensor_copy(w["bias_k"][:, :], ps_bias[:, 4:8])
        nc.vector.tensor_copy(bias_v[:, :], ps_bias[:, 8:12]).then_inc(dve, 1)
        v.wait_ge(dve, 1)
        nc.vector.tensor_copy(wide[:, :, :], spread(bias_v[:, :], [1, KC], [0, P])).then_inc(spread_made, 1)
        for k in range(KC):
            nc.vector.tensor_scalar(raw[:, k, 0:HDH], raw[:, k, 0:HDH], g_col[:, k:k + 1], DH ** -0.5,
                                    ALU.mult, ALU.mult)
            nc.vector.tensor_scalar(raw[:, k, HDH:], raw[:, k, HDH:], g_col[:, k:k + 1], None,
                                    ALU.mult).then_inc(dve, 1)
        v.wait_ge(hi_made, 2)
        nc.vector.tensor_tensor(w["qkv_lo"][:, :, :], raw[:, :, :], w["qkv_hi"][:, :, :].bitcast(F32), ALU.subtract)
        nc.vector.tensor_tensor(w["out_lo"][:, :, :], raw_o[:, :, :], w["out_hi"][:, :, :].bitcast(F32),
                                ALU.subtract).then_inc(dve, 1)
        v.wait_ge(row_made, 1)
        nc.vector.tensor_tensor(w["row"][:, :], ps_row[:, :], null_row[:, :], ALU.add).then_inc(dve, 1)
        v.wait_ge(dve, 1 + KC + 2)

    def on_scalar(act):
        act.wait_ge(loaded, 16 * LOADS)
        nc.scalar.activation(w["out_hi"][:, :, :], raw_o[:, :, :], ACT.Identity).then_inc(hi_made, 1)
        act.wait_ge(dve, 1 + KC)
        nc.scalar.activation(w["qkv_hi"][:, :, :], raw[:, :, :], ACT.Identity).then_inc(hi_made, 1)

    return on_sync, on_tensor, on_vector, on_scalar


def stats_phase(nc, x2, keep, weights):
    tiles_per_load = 4
    loads = TILES // tiles_per_load
    rows = x2.rearrange("b (c p) d -> p (b c) d", p=P)
    with ExitStack() as ctx:
        sb, ps, sem = open_tensors(nc, ctx)
        xin = [sb(f"sxin{i}", [P, tiles_per_load, DIM]) for i in range(4)]
        bn = sb("sbn", [P, TILES, 6])
        tmp = sb("stmp", [P, TILES])
        tmp2 = sb("stmp2", [P, TILES])
        var2 = sb("svar2", [P, TILES])
        x_in = [sem(f"sx_in{i}") for i in range(4)]
        stats_done = sem("sstats_done")
        dve = sem("sdve")
        sqrt_done = sem("ssqrt_done")
        load_weights, multiply_weights, combine_weights, round_weights = light_weights(nc, ctx, *weights)
        with nc.Block() as block:

            @block.sync
            def _(sp):
                load_weights(sp)
                for t in range(loads):
                    if t >= 4:
                        sp.wait_ge(stats_done, (t - 3) * tiles_per_load)
                    sp.dma_start(xin[t % 4][:, :, :],
                                 rows[:, t * tiles_per_load:(t + 1) * tiles_per_load, :]).then_inc(x_in[t % 4], 16)

            @block.scalar
            def _(act):
                round_weights(act)
                for n in (1, 3, 5):
                    act.wait_ge(sqrt_done, n)
                    nc.scalar.activation(tmp2[:, :], tmp[:, :], ACT.Sqrt).then_inc(sqrt_done, 1)

            @block.tensor
            def _(pe):
                multiply_weights(pe)

            @block.vector
            def _(v):
                def statistics(first, end):
                    with v.Fori(first, end) as t4:
                        for i in range(4):
                            v.wait_ge(x_in[i], t4 * 16 + 16)
                            for n in range(tiles_per_load):
                                nc.vector.bn_stats(bn[:, bass.ds(t4 * 16 + i * tiles_per_load + n, 1), :],
                                                   xin[i][:, n, :]).then_inc(stats_done, 1)

                statistics(0, loads // 8)
                combine_weights(v)
                statistics(loads // 8, loads // 4)
                v.wait_ge(stats_done, TILES)
                finish_stats(nc, v, dve, 0, bn, keep["mean2"], keep["rstd2"], tmp, tmp2, sqrt_done)
                nc_steps = FINISH_STEPS

                def step(ins):
                    nonlocal nc_steps
                    nc_steps += 1
                    ins.then_inc(dve, 1)
                    v.wait_ge(dve, nc_steps)

                def inverse_root(to, roots):
                    v.wait_ge(sqrt_done, roots)
                    step(nc.vector.reciprocal(to[:, :], tmp2[:, :]))
                    step(nc.vector.tensor_tensor(tmp2[:, :], to[:, :], to[:, :], ALU.mult))
                    step(nc.vector.tensor_tensor(tmp2[:, :], tmp2[:, :], tmp[:, :], ALU.mult))
                    step(nc.vector.tensor_scalar(tmp2[:, :], tmp2[:, :], -0.5, 1.5, ALU.mult, ALU.add))
                    step(nc.vector.tensor_tensor(to[:, :], to[:, :], tmp2[:, :], ALU.mult))

                rstd2, rstd3 = keep["rstd2"], keep["rstd3"]
                step(nc.vector.tensor_scalar(tmp[:, :], tmp[:, :], -EPS, None, ALU.add))
                step(nc.vector.tensor_tensor(tmp[:, :], tmp[:, :], rstd2[:, :], ALU.mult))
                step(nc.vector.tensor_tensor(tmp[:, :], tmp[:, :], rstd2[:, :], ALU.mult))
                step(nc.vector.tensor_copy(var2[:, :], tmp[:, :]))
                nc.vector.tensor_scalar(tmp[:, :], tmp[:, :], EPS, None, ALU.add).then_inc(sqrt_done, 1)
                inverse_root(rstd3, 4)
                nc.vector.tensor_scalar(tmp[:, :], var2[:, :], float(DIM), 1e-24, ALU.mult, ALU.max).then_inc(sqrt_done, 1)
                inverse_root(keep["rms_scale"], 6)
                step(nc.vector.scalar_tensor_tensor(out=keep["rms_scale"][:, :], in0=keep["rms_scale"][:, :],
                                                    scalar=float(np.float32(DIM ** 0.5)), in1=rstd2[:, :],
                                                    op0=ALU.mult, op1=ALU.mult))
                step(nc.vector.scalar_tensor_tensor(out=keep["shift2"][:, :], in0=keep["mean2"][:, :], scalar=-1.0,
                                                    in1=rstd2[:, :], op0=ALU.mult, op1=ALU.mult))
                step(nc.vector.tensor_tensor(keep["rstd23"][:, :], rstd2[:, :], rstd3[:, :], ALU.mult))
                step(nc.vector.tensor_tensor(keep["shift23"][:, :], keep["shift2"][:, :], rstd3[:, :], ALU.mult))


MAIN, SIDE = P, WIN
RING = 4
XRING = 8


def product(nc, out, left, right, first=True, last=True):
    (lh, ll), (rh, rl) = left, right
    nc.tensor.matmul(out, lh, rh, start=first, stop=False)
    nc.tensor.matmul(out, lh, rl, start=False, stop=False)
    return nc.tensor.matmul(out, ll, rh, start=False, stop=last)


def light_phase(nc, x2, out, w, keep, s_all):
    x2_t = x2.rearrange("b (c p) d -> (b c) p d", p=P)
    out_t = out.rearrange("b (c p) d -> (b c) p d", p=P)

    with ExitStack() as ctx:
        sb, ps, sem = open_tensors(nc, ctx)
        xin = sb("l_xin", [P, XRING, DIM])
        x2n = sb("l_x2n", [P, 4, DIM])
        xn = sb("l_xn", [P, 2, DIM])
        dot_out = sb("l_dot_out", [P, DIM])
        dots = sb("l_dots", [P, 2, NCH])
        xt_hi = sb("l_xt_hi", [P, KC, P], F32R)
        xt_lo = sb("l_xt_lo", [P, KC, P], F32R)
        q_tok = sb("l_q_tok", [P, HDH])
        k_tok = sb("l_k_tok", [P, HDH])
        q_t = sb("l_q_t", [P, RING, PAIRS, 2, P])
        k_t = sb("l_k_t", [P, PAIRS, RING * P])
        val = sb("l_val", [P, RING, HDH])
        val_side = sb("l_val_side", [P, RING, HDH])
        prob = [sb(f"l_prob{i}", [P, PAIRS, 2 * (MAIN + SIDE)]) for i in range(2)]
        neg_max = sb("l_neg_max", [P, 2, 2, PAIRS])
        total = sb("l_total", [P, 2, 2, PAIRS])
        inv = sb("l_inv", [P, 2, 2, PAIRS])
        pt_main = sb("l_pt_main", [P, HEADS, P])
        pt_side = sb("l_pt_side", [P, HEADS, P])
        at_hi = sb("l_at_hi", [P, KC, P], F32R)
        at_lo = sb("l_at_lo", [P, KC, P], F32R)
        res = sb("l_res", [P, 2, DIM])

        ps_s = ps("l_ps_s", [P, 2, PAIRS, 2 * P])
        ps_a = ps("l_ps_a", [P, 512])
        ps_b = ps("l_ps_b", [P, 512])
        ps_c = ps("l_ps_c", [P, 512])
        ps_d = ps("l_ps_d", [P, 512])

        x_in = [sem(f"l_x_in{i}") for i in range(4)]
        res_out = [sem(f"l_res_out{i}") for i in range(2)]
        (zeroed, x_normed, xt_made, xt_hi_kept, xt_kept, q_made, q_kept, k_made, k_kept, v_made, v_kept,
         qt_made, qt_kept, kt_made, kt_kept, s_made, max_made, exp_made, inv_made, dot_step,
         p_normed, v_moved, x_plus, pt_made, pt_kept_dve, pt_kept_act, o_made, o_hi_kept, o_kept,
         out_made, res_made) = (sem("l_" + n) for n in (
             "zeroed x_normed xt_made xt_hi_kept xt_kept q_made q_kept k_made k_kept v_made v_kept "
             "qt_made qt_kept kt_made kt_kept s_made max_made exp_made inv_made dot_step "
             "p_normed v_moved x_plus pt_made pt_kept_dve pt_kept_act o_made o_hi_kept o_kept "
             "out_made res_made").split())
        ZEROED = 4

        ident = keep["ident"]

        def keys_of(j, win):
            if win == 0:
                return (SIDE if j == 0 else 0), MAIN + SIDE
            return 0, (MAIN if j == NCH - 1 else MAIN + SIDE)

        def key_runs(j, win):
            at = j % RING * P
            if win == 0:
                if j == 0:
                    return [(SIDE, at, MAIN)]
                if at == 0:
                    return [(0, RING * P - SIDE, SIDE), (SIDE, 0, MAIN)]
                return [(0, at - SIDE, MAIN + SIDE)]
            if j == NCH - 1:
                return [(0, at, MAIN)]
            if at == RING * P - P:
                return [(0, at, MAIN), (MAIN, 0, SIDE)]
            return [(0, at, MAIN + SIDE)]

        def steps(eng, body):
            for g in range(NCH):
                body(g, g, lambda k, g=g: g - k >= 0)
            with eng.Fori(1, BATCH - 1) as b:
                for j in range(NCH):
                    body(b * NCH + j, j, lambda k: True)
            for g in range(TILES - NCH, TILES + 4):
                body(g, g % NCH, lambda k, g=g: g - k < TILES)

        AT = (MAIN + SIDE, 0)
        ALL, NEXT, BEFORE = slice(0, P), slice(0, WIN), slice(WIN, P)

        def by_head(buf, keys, win):
            return buf[keys, :, win * WIN:(win + 1) * WIN].rearrange("p (a h) q -> p a h q", h=2)

        def turned(bank, keys):
            return bank[keys, :].rearrange("p (a h q) -> p a h q", h=2, q=WIN)

        with nc.Block() as block:

            @block.sync
            def _(sp):
                for t in range(4):
                    sp.dma_start(xin[:, t, :], x2_t[t]).then_inc(x_in[t], 16)

                def body(g, j, live):
                    if live(4):
                        wait(sp, res_made, g - 3)
                        sp.dma_start(out_t[g - 4], res[:, j % 2, :]).then_inc(res_out[j % 2], 16)
                    elif g < 4:
                        sp.wait_ge(x_normed, g + 1)
                    if live(-4):
                        sp.dma_start(xin[:, (j + 4) % XRING, :], x2_t[g + 4]).then_inc(x_in[j % 4], 16)

                steps(sp, body)
                for i in range(2):
                    sp.wait_ge(res_out[i], 16 * TILES // 2)

            @block.tensor
            def _(pe):
                def transpose_x(g, j):
                    wait(pe, x_normed, g + 1)
                    wait(pe, qt_kept, g)
                    for k in range(KC):
                        last = nc.tensor.transpose(ps_a[:, k * P:(k + 1) * P], xn[:, j % 2, k * P:(k + 1) * P],
                                                   ident[:, :])
                    last.then_inc(xt_made, 1)

                def project(bank, part, done):
                    for k in range(KC):
                        cols = slice(part * HDH, (part + 1) * HDH)
                        last = product(nc, bank[:, :], (xt_hi[:, k, :], xt_lo[:, k, :]),
                                       (w["qkv_hi"][:, k, cols], w["qkv_lo"][:, k, cols]), k == 0, k == KC - 1)
                    last.then_inc(done, 1)

                def turn(bank, src, done):
                    for k in range(KC):
                        last = nc.tensor.transpose(bank[:, k * P:(k + 1) * P], src[:, k * P:(k + 1) * P], ident[:, :])
                    last.then_inc(done, 1)

                def scores(t, j):
                    wait(pe, qt_kept, t + 1)
                    wait(pe, kt_kept, t + 1 if j == NCH - 1 else t + 2)
                    for win in range(2):
                        wait(pe, exp_made, 2 * t + win - 1)
                        for pair in range(PAIRS):
                            for col, key, n in key_runs(j, win):
                                last = nc.tensor.matmul(ps_s[:, win, pair, col:col + n], q_t[:, j % RING, pair, win, :],
                                                        k_t[:, pair, key:key + n], start=True, stop=True)
                        last.then_inc(s_made, 1)

                def turn_probs(bank, j, col):
                    for pair in range(PAIRS):
                        last = nc.tensor.transpose(bank[:, pair * P:(pair + 1) * P],
                                                   prob[j % 2][:, pair, col:col + P], ident[:, :])
                    last.then_inc(pt_made, 1)

                def attend(t, j):
                    wait(pe, pt_kept_dve, 2 * t + 2)
                    wait(pe, pt_kept_act, 2 * t + 2)
                    wait(pe, v_kept, t + 1)
                    wait(pe, v_moved, t + 1 if j == NCH - 1 else t + 2)
                    for h in range(HEADS):
                        cols = slice(h * DH, (h + 1) * DH)
                        to = ps_d[h % 2 * DH:(h % 2 + 1) * DH, h // 2 * P:(h // 2 + 1) * P]
                        nc.tensor.matmul(to, val[:, j % RING, cols], pt_main[:, h, :], start=True, stop=False)
                        last = nc.tensor.matmul(to, val_side[:, j % RING, cols], pt_side[:, h, :], start=False, stop=True)
                    last.then_inc(o_made, 1)

                pe.wait_ge(zeroed, ZEROED)
                transpose_x(0, 0)

                def body(g, j, live):
                    if live(2):
                        scores(g - 2, (j - 2) % NCH)
                    if live(4):
                        wait(pe, o_kept, g - 3)
                        wait(pe, kt_kept, g if live(0) else TILES)
                        for k in range(KC):
                            last = product(nc, ps_c[:, :], (at_hi[:, k, :], at_lo[:, k, :]),
                                           (w["out_hi"][:, k, :], w["out_lo"][:, k, :]), k == 0, k == KC - 1)
                        last.then_inc(out_made, 1)
                    if live(0):
                        wait(pe, xt_kept, g + 1)
                        wait(pe, v_kept, g)
                        project(ps_b, 0, q_made)
                    if live(3):
                        t, jt = g - 3, (j - 3) % NCH
                        wait(pe, p_normed, 2 * t + 2)
                        wait(pe, res_made, g - 3)
                        turn_probs(ps_c, jt, AT[0] + SIDE)
                        turn_probs(ps_d, jt, AT[1])
                    if live(0):
                        project(ps_a, 1, k_made)
                    if live(3):
                        wait(pe, pt_kept_dve, 2 * t + 1)
                        turn_probs(ps_c, jt, MAIN)
                    if live(0):
                        wait(pe, q_kept, g + 1)
                        project(ps_b, 2, v_made)
                        wait(pe, k_kept, g + 1)
                        turn(ps_a, q_tok, qt_made)
                    if live(3):
                        wait(pe, pt_kept_dve, 2 * t + 2)
                        wait(pe, pt_kept_act, 2 * t + 2)
                    if live(0):
                        turn(ps_c, k_tok, kt_made)
                    if live(3):
                        attend(t, jt)
                    if live(-1):
                        transpose_x(g + 1, j + 1)

                steps(pe, body)

            @block.scalar
            def _(act):
                def layernorms(g, j, passes):
                    one = slice(g, g + 1) if isinstance(g, int) else bass.ds(g, 1)
                    wait(act, x_in[j % 4], passes)
                    wait(act, dot_step, 2 * g - 6)
                    nc.scalar.activation(x2n[:, j % 4, :], xin[:, j % XRING, :], ACT.Identity,
                                         scale=keep["rstd2"][:, one], bias=keep["shift2"][:, one])
                    nc.scalar.activation(xn[:, j % 2, :], xin[:, j % XRING, :], ACT.Identity,
                                         scale=keep["rstd23"][:, one], bias=keep["shift23"][:, one]).then_inc(x_normed, 1)

                def keep_xt(g):
                    wait(act, xt_made, g + 1)
                    nc.scalar.activation(xt_hi[:, :, :].rearrange("p k t -> p (k t)"), ps_a[:, :],
                                         ACT.Identity).then_inc(xt_hi_kept, 1)

                layernorms(0, 0, 16)
                layernorms(1, 1, 16)
                keep_xt(0)

                def body(g, j, live):
                    if live(2):
                        t, jt = g - 2, (j - 2) % NCH
                        for win in range(2):
                            wait(act, max_made, 2 * t + win + 1)
                            lo, hi = keys_of(jt, win)
                            for pair in range(PAIRS):
                                last = nc.scalar.activation(
                                    prob[jt % 2][:, pair, AT[win] + lo:AT[win] + hi], ps_s[:, win, pair, lo:hi], ACT.Exp,
                                    bias=neg_max[:, jt % 2, win, pair:pair + 1],
                                    accum_out=total[:, jt % 2, win, pair:pair + 1])
                            last.then_inc(exp_made, 1)
                    if live(0):
                        wait(act, q_made, g + 1)
                        nc.scalar.activation(q_tok[:, :], ps_b[:, :], ACT.Identity).then_inc(q_kept, 1)
                    if live(1):
                        wait(act, v_kept, g)
                        lo, hi = slice(0, WIN), slice(WIN, P)
                        if (j - 1) % NCH != 0:
                            last = nc.scalar.activation(val_side[lo, (j - 2) % RING, :], val[lo, (j - 1) % RING, :],
                                                        ACT.Identity)
                        if (j - 1) % NCH != NCH - 1:
                            last = nc.scalar.activation(val_side[hi, j % RING, :], val[hi, (j - 1) % RING, :],
                                                        ACT.Identity)
                        last.then_inc(v_moved, 1)
                    if live(3):
                        t, jt = g - 3, (j - 3) % NCH
                        wait(act, pt_made, 3 * t + 2)
                        nc.scalar.activation(by_head(pt_main, ALL, 1), turned(ps_d, ALL), ACT.Identity).then_inc(pt_kept_act, 1)
                    if live(0):
                        wait(act, k_made, g + 1)
                        nc.scalar.activation(k_tok[:, :], ps_a[:, :], ACT.Identity).then_inc(k_kept, 1)
                    if live(3):
                        wait(act, pt_made, 3 * t + 3)
                        nc.scalar.activation(by_head(pt_side, NEXT, 1), turned(ps_c, NEXT),
                                             ACT.Identity).then_inc(pt_kept_act, 1)
                    if live(0):
                        wait(act, v_made, g + 1)
                        nc.scalar.activation(val[:, j % RING, :], ps_b[:, :], ACT.Identity).then_inc(v_kept, 1)
                    if live(-2):
                        layernorms(g + 2, (j + 2) % NCH, (g - j) * 4 + 16 * ((j + 2) // 4 + 1))
                    if live(3):
                        wait(act, o_made, t + 1)
                        nc.scalar.activation(at_hi[:, :, :].rearrange("p k t -> p (k t)"), ps_d[:, :],
                                             ACT.Identity).then_inc(o_hi_kept, 1)
                    if live(-1):
                        keep_xt(g + 1)

                steps(act, body)

            @block.vector
            def _(v):
                nc.vector.memset(q_t[:, :, :, :, :].rearrange("p r a w q -> p (r a w q)"), 0.0).then_inc(zeroed, 1)
                nc.vector.memset(pt_side[:, :, :].rearrange("p h q -> p (h q)"), 0.0).then_inc(zeroed, 1)
                nc.vector.memset(val_side[:, :, :].rearrange("p r n -> p (r n)"), 0.0).then_inc(zeroed, 1)
                nc.vector.memset(dots[:, :, :].rearrange("p r n -> p (r n)"), 0.0).then_inc(zeroed, 1)
                v.wait_ge(zeroed, ZEROED)

                def keep_xt_lo(g):
                    wait(v, xt_hi_kept, g + 1)
                    nc.vector.tensor_tensor(xt_lo[:, :, :].rearrange("p k t -> p (k t)"), ps_a[:, :],
                                            xt_hi[:, :, :].bitcast(F32).rearrange("p k t -> p (k t)"),
                                            ALU.subtract).then_inc(xt_kept, 1)

                keep_xt_lo(0)

                def body(g, j, live):
                    if live(2):
                        t, jt = g - 2, (j - 2) % NCH
                        for win in range(2):
                            wait(v, s_made, 2 * t + win + 1)
                            lo, hi = keys_of(jt, win)
                            if hi - lo == MAIN:
                                edge = AT[0] if win == 0 else MAIN
                                nc.vector.memset(prob[jt % 2][:, :, edge:edge + SIDE], 0.0)
                            nc.vector.tensor_reduce(neg_max[:, jt % 2, win, :], ps_s[:, win, :, lo:hi], AX_X, ALU.max,
                                                    negate=True).then_inc(max_made, 1)
                    if live(4):
                        t4 = g - 4
                        wait(v, out_made, g - 3)
                        wait(v, x_plus, g - 3)
                        wait(v, res_out[j % 2], (g - j) * 8 + 16 * ((j - 4) // 2))
                        nc.vector.tensor_tensor(res[:, j % 2, :], ps_c[:, :], xin[:, (j - 4) % XRING, :],
                                                ALU.add).then_inc(res_made, 1)
                    if live(3):
                        t3 = g - 3
                        wait(v, pt_made, 3 * t3 + 1)
                        nc.vector.tensor_copy(by_head(pt_main, ALL, 0), turned(ps_c, ALL)).then_inc(pt_kept_dve, 1)
                    if live(2):
                        wait(v, exp_made, 2 * t + 2)
                        nc.vector.reciprocal(inv[:, jt % 2], total[:, jt % 2]).then_inc(inv_made, 1)
                    if live(3):
                        wait(v, pt_made, 3 * t3 + 3)
                        nc.vector.tensor_copy(by_head(pt_side, BEFORE, 0), turned(ps_c, BEFORE)).then_inc(pt_kept_dve, 1)
                    if live(0):
                        wait(v, qt_made, g + 1)
                        for h in range(2):
                            rows = slice(h * DH, (h + 1) * DH)
                            last = nc.vector.tensor_tensor(
                                q_t[rows, j % RING, :, :, h * WIN:(h + 1) * WIN],
                                ps_a[rows, :].rearrange("p (a w q) -> p a w q", a=PAIRS, w=2),
                                spread(w["bias_q"][rows, :], [1, PAIRS], [0, 2], [0, WIN]), ALU.add)
                        last.then_inc(qt_kept, 1)
                        wait(v, kt_made, g + 1)
                        nc.vector.tensor_tensor(k_t[:, :, j % RING * P:(j % RING + 1) * P],
                                                ps_c[:, :].rearrange("p (a t) -> p a t", a=PAIRS),
                                                spread(w["bias_k"][:, :], [1, PAIRS], [0, P]), ALU.add).then_inc(kt_kept, 1)
                    if live(3):
                        wait(v, o_hi_kept, t3 + 1)
                        nc.vector.tensor_tensor(at_lo[:, :, :].rearrange("p k t -> p (k t)"), ps_d[:, :],
                                                at_hi[:, :, :].bitcast(F32).rearrange("p k t -> p (k t)"),
                                                ALU.subtract).then_inc(o_kept, 1)
                    if live(-1):
                        keep_xt_lo(g + 1)
                    if live(0):
                        wait(v, x_normed, g + 1)
                        for r in range(2):
                            wait(v, dot_step, 2 * g + r)
                            last = nc.vector.tensor_tensor_reduce(dot_out[:, :], x2n[:, j % 4, :], w["rt"][:, r], 1.0, 0.0,
                                                                  ALU.mult, ALU.add, dots[:, r, j:j + 1])
                            last.then_inc(dot_step, 1)
                        if j == NCH - 1:
                            first = g - j
                            at = slice(first, first + NCH) if isinstance(g, int) else bass.ds(first, NCH)
                            wait(v, dot_step, 2 * g + 2)
                            nc.vector.tensor_copy(s_all[:, :, at], dots[:, :, :])

                steps(v, body)

            @block.gpsimd
            def _(pool):
                pool.wait_ge(zeroed, ZEROED)

                def body(g, j, live):
                    if live(2):
                        t, jt = g - 2, (j - 2) % NCH
                        for win in range(2):
                            if win == 0:
                                wait(pool, inv_made, t + 1)
                            mine = prob[jt % 2][:, :, AT[win]:AT[win] + MAIN + SIDE]
                            nc.gpsimd.tensor_tensor(mine, mine, spread(inv[:, jt % 2, win, :], [1, PAIRS], [0, MAIN + SIDE]),
                                                    ALU.mult).then_inc(p_normed, 1)
                    if live(0):
                        wait(pool, x_normed, g + 1)
                        nc.gpsimd.tensor_tensor(xin[:, j % XRING, :], xin[:, j % XRING, :], w["row"][:, :],
                                                ALU.add).then_inc(x_plus, 1)

                steps(pool, body)


ROUTES = 2
ROWS = ROUTES * BATCH
QB, KVB = NQ // P, NKV // P
BIG_BIT = 30


def heavy_weights(nc, ctx, rms_g, w_q, w_kv, null_kv, w_out, null_q, w):
    sb, _, sem = open_tensors(nc, ctx)
    raw_q = sb("hw_raw_q", [P, KC, HDH])
    raw_kv = sb("hw_raw_kv", [P, KC, HEADS, 2, DH])
    raw_parts = sb("hw_raw_parts", [P, 2, KC, HDH])
    raw_null = sb("hw_raw_null", [P, HEADS])
    g_col = sb("hw_g", [P, KC])
    loaded, scaled, hi_made, lo_made = (sem(f"hw_{n}") for n in ("loaded", "scaled", "hi", "lo"))
    LOADS = 8

    def on_sync(sp):
        sp.dma_start(raw_q[:, :, :], w_q.rearrange("(k p) n -> p k n", p=P)).then_inc(loaded, 16)
        sp.dma_start(raw_kv[:, :, :, :, :].rearrange("p k h w d -> p k (h w d)"),
                     w_kv.rearrange("(k p) h n -> p k (h n)", p=P)).then_inc(loaded, 16)
        sp.dma_start(w["out"][:, :, :], w_out.rearrange("(k p) n -> p k n", p=P)).then_inc(loaded, 16)
        sp.dma_start(g_col[:, :], rms_g.rearrange("(k p) -> p k", p=P),
                     allow_slow_non_contiguous=True).then_inc(loaded, 16)
        for half in range(2):
            sp.dma_start(raw_null[half * DH:(half + 1) * DH, :], null_kv[0].rearrange("h d -> d h"),
                         allow_slow_non_contiguous=True).then_inc(loaded, 16)
        for row, src in ((w["null_v"][:, :], null_kv[1]), (w["null_row"][:, :], null_q)):
            sp.dma_start(row, bass.AP(tensor=src.tensor, offset=src.offset,
                                      ap=[[0, P], [1, DIM]])).then_inc(loaded, 16)

    def on_gpsimd(pool):
        pool.wait_ge(loaded, 16 * LOADS)
        for k in range(KC):
            nc.gpsimd.tensor_scalar(raw_q[:, k, :], raw_q[:, k, :], g_col[:, k:k + 1], DH ** -0.5,
                                    ALU.mult, ALU.mult).then_inc(scaled, 1)
            for n in range(2):
                nc.gpsimd.tensor_scalar(raw_parts[:, n, k, :].rearrange("p (h d) -> p h d", h=HEADS),
                                        raw_kv[:, k, :, n, :], g_col[:, k:k + 1], None, ALU.mult).then_inc(scaled, 1)
        pool.wait_ge(scaled, 3 * KC)
        pool.wait_ge(hi_made, 4)
        for hi, lo, raw in ((w["q_hi"], w["q_lo"], raw_q[:, :, :]), (w["k_hi"], w["k_lo"], raw_parts[:, 0]),
                            (w["v_hi"], w["v_lo"], raw_parts[:, 1])):
            nc.gpsimd.tensor_tensor(lo[:, :, :], raw, hi[:, :, :].bitcast(F32), ALU.subtract).then_inc(lo_made, 1)
        nc.gpsimd.tensor_tensor(w["null_k"][:, :, 1], raw_null[:, :], w["null_k"][:, :, 0].bitcast(F32),
                                ALU.subtract).then_inc(lo_made, 1)
        pool.wait_ge(lo_made, 4)

    def on_scalar(act):
        act.wait_ge(loaded, 16 * LOADS)
        nc.scalar.activation(w["null_k"][:, :, 0], raw_null[:, :], ACT.Identity).then_inc(hi_made, 1)
        act.wait_ge(scaled, 3 * KC)
        nc.scalar.activation(w["q_hi"][:, :, :], raw_q[:, :, :], ACT.Identity).then_inc(hi_made, 1)
        nc.scalar.activation(w["k_hi"][:, :, :], raw_parts[:, 0], ACT.Identity).then_inc(hi_made, 1)
        nc.scalar.activation(w["v_hi"][:, :, :], raw_parts[:, 1], ACT.Identity).then_inc(hi_made, 1)

    return on_sync, on_gpsimd, on_scalar


def routing_phase(nc, s_all, keep, lists, weights):
    COLS = ROWS * NCH
    HI = max(QB, KVB)
    PARTS = 2 + 3 * 3
    with ExitStack() as ctx:
        sb, ps, sem = open_tensors(nc, ctx)
        blocks = sb("r_blocks", [P, P])
        ones = sb("r_ones", [P, P])
        before = sb("r_before", [P, P])
        s_t = sb("r_s_t", [P, ROUTES, P])
        gap = sb("r_gap", [P, ROUTES, P])
        score = sb("r_score", [P, ROUTES, P])
        part_max = sb("r_part_max", [P, ROUTES])
        row_max = sb("r_row_max", [ROUTES, BATCH])
        row_wide = sb("r_row_wide", [ROUTES, P])
        s_max = sb("r_s_max", [P, ROUTES])
        neg_a = sb("r_neg_a", [P, ROUTES])
        top = sb("r_top", [P, ROUTES])
        sums = sb("r_sums", [P, ROUTES])
        log_sum = sb("r_log_sum", [P, ROUTES])
        take = sb("r_take", [P, ROUTES])
        cut = sb("r_cut", [P, ROUTES], U32)
        cand = sb("r_cand", [P, ROUTES], U32)
        bit = sb("r_bit", [P, ROUTES], U32)
        gain = sb("r_gain", [P, ROUTES], U32)
        over = sb("r_over", [P, ROUTES, P])
        equal = sb("r_equal", [P, ROUTES, P])
        over_c = sb("r_over_c", [P, ROUTES, BATCH, NCH])
        equal_c = sb("r_equal_c", [P, ROUTES, BATCH, NCH])
        score_c = sb("r_score_c", [P, COLS])
        count = sb("r_count", [P, ROWS, NCH])
        offset = sb("r_offset", [P, ROWS, NCH])
        place = sb("r_place", [P, COLS])
        place_i = sb("r_place_i", [P, COLS], I32)
        block_i = sb("r_block_i", [P, COLS], I32)
        room = sb("r_room", [P, ROWS])
        chosen = sb("r_chosen", [P, COLS])
        column = sb("r_column", [P, COLS])
        block_no = sb("r_block_no", [P, COLS])
        token_row = sb("r_token_row", [P, COLS])
        token_tile = sb("r_token_tile", [P, COLS])
        first_token = sb("r_first_token", [P, BATCH])
        total_no = sb("r_total_no", [P, ROWS, HI])
        in_block = sb("r_in_block", [P, COLS, HI], BF16)
        rest = sb("r_rest", [P, COLS])
        parts = sb("r_parts", [P, COLS, PARTS], BF16)
        what = sb("r_what", [P, COLS, PARTS, HI], BF16)
        row_what = [sb(f"r_row_what{i}", [P, NCH, PARTS, HI], BF16) for i in range(2)]
        one_hot = [sb(f"r_one_hot{i}", [P, NCH, P], BF16) for i in range(2)]
        listed = sb("r_listed", [P, ROWS, PARTS, HI])

        ps_turn = ps("r_ps_turn", [P, 4, P])
        ps_small = ps("r_ps_small", [P, 512])
        ps_sums = ps("r_ps_sums", [P, 512])
        ps_back = ps("r_ps_back", [P, 3, ROUTES, P])
        ps_before = ps("r_ps_before", [P, 512])
        total = [ps_sums[:, 0:1], ps_before[:, 0:1]]
        ps_list = [ps(f"r_ps_list{i}", [P, 512]) for i in range(2)]

        SCORES_TURNED, MAX_TURNED, MAX_SPREAD, MASKS_TURNED, TIES_COUNTED, PLACES_COUNTED = range(1, 7)
        MAX_MADE, MAX_WIDE, MASKS_MADE, TIES_IN, CHOSEN_IN, WHAT_MADE = range(1, 7)
        (made, turned, handed, scores_made, dve, what_moved, hot_made, list_made, list_kept) = (
            sem("r_" + n) for n in "made turned handed scores_made dve what_moved hot_made list_made list_kept".split())
        gap_made, exp_made, total_made, log_made, counted, count_made = (
            [sem(f"r_{n}{r}") for r in range(ROUTES)]
            for n in ("gap_made", "exp_made", "total_made", "log_made", "counted", "count_made"))
        ident, steps = keep["ident"], keep["steps"]
        MADE = 12
        ITER_STEPS = 2 * ROUTES
        BIT_STEPS = 4 * ROUTES
        LOG_K = [float(np.float32(np.log(np.float32(k)))) for k in (K_EFF_Q, K_EFF_KV)]

        load_weights, combine_weights, round_weights = heavy_weights(nc, ctx, *weights)
        with nc.Block() as block:

            @block.sync
            def _(sp):
                load_weights(sp)

            @block.gpsimd
            def _(pool):
                nc.gpsimd.memset(ones[:, :], 1.0).then_inc(made, 1)
                nc.gpsimd.memset(blocks[:, :], 1.0).then_inc(made, 1)
                nc.gpsimd.memset(before[:, :], 1.0).then_inc(made, 1)
                for a, pattern, mult in ((token_row, [[0, COLS]], 1), (token_tile, [[0, ROWS], [1, NCH]], 0),
                                         (first_token, [[SEQ, BATCH]], 0)):
                    nc.gpsimd.iota(a[:, :], pattern=pattern, base=0, channel_multiplier=mult,
                                   allow_small_or_imprecise_dtypes=True).then_inc(made, 1)
                for r, k in enumerate((NQ, NKV)):
                    nc.gpsimd.memset(take[:, r:r + 1], float(k)).then_inc(made, 1)
                pool.wait_ge(made, 8)
                by_seq = blocks[:, :].rearrange("p (b t) -> p b t", t=NCH)
                nc.gpsimd.affine_select(out=by_seq, in_=by_seq, compare_op=ALU.is_ge, fill=0.0, base=0,
                                        pattern=[[-NCH, BATCH], [0, NCH]], channel_multiplier=1).then_inc(made, 1)
                nc.gpsimd.affine_select(out=before[:, :], in_=before[:, :], compare_op=ALU.is_ge, fill=0.0, base=-1,
                                        pattern=[[1, P]], channel_multiplier=-1).then_inc(made, 1)
                pool.wait_ge(made, 10)
                nc.gpsimd.affine_select(out=by_seq, in_=by_seq, compare_op=ALU.is_ge, fill=0.0, base=NCH - 1,
                                        pattern=[[NCH, BATCH], [0, NCH]], channel_multiplier=-1).then_inc(made, 2)
                combine_weights(pool)

            @block.tensor
            def _(pe):
                for r in range(ROUTES):
                    last = nc.tensor.transpose(ps_turn[:, r, :], s_all[:, r, :], ident[:, :])
                last.then_inc(turned, 1)
                pe.wait_ge(handed, MAX_MADE)
                nc.tensor.transpose(ps_small[0:ROUTES, 0:P], part_max[:, :], ident[:, :]).then_inc(turned, 1)
                pe.wait_ge(handed, MAX_WIDE)
                nc.tensor.transpose(ps_small[:, P:P + ROUTES], row_wide[:, :],
                                    ident[0:ROUTES, 0:ROUTES]).then_inc(turned, 1)
                pe.wait_ge(made, MADE)
                with pe.Fori(0, N_ITERS - 1) as i:
                    for r in range(ROUTES):
                        pe.wait_ge(exp_made[r], i + 1)
                        nc.tensor.matmul(total[r], blocks[:, :], sums[:, r:r + 1], start=True,
                                         stop=True).then_inc(total_made[r], 1)
                with pe.Fori(0, BIG_BIT) as i:
                    for r in range(ROUTES):
                        pe.wait_ge(counted[r], i + 1)
                        nc.tensor.matmul(total[r], blocks[:, :], sums[:, r:r + 1], start=True,
                                         stop=True).then_inc(count_made[r], 1)
                pe.wait_ge(handed, MASKS_MADE)
                for n, src in enumerate((over, equal, score)):
                    for r in range(ROUTES):
                        last = nc.tensor.transpose(ps_back[:, n, r, :], src[:, r, :], ident[:, :])
                last.then_inc(turned, 1)
                pe.wait_ge(handed, TIES_IN)
                nc.tensor.matmul(ps_before[:, 0:COLS], before[:, :], equal_c[:, :, :, :].rearrange("p r b t -> p (r b t)"),
                                 start=True, stop=True)
                nc.tensor.matmul(ps_turn[:, 0:2, :].rearrange("p a t -> p (a t)"), ones[:, :],
                                 equal_c[:, :, :, :].rearrange("p r b t -> p (r b t)"), start=True, stop=True)
                nc.tensor.matmul(ps_turn[:, 2:4, :].rearrange("p a t -> p (a t)"), ones[:, :],
                                 over_c[:, :, :, :].rearrange("p r b t -> p (r b t)"), start=True,
                                 stop=True).then_inc(turned, 1)
                pe.wait_ge(handed, CHOSEN_IN)
                nc.tensor.matmul(ps_before[:, 0:COLS], before[:, :], chosen[:, :], start=True, stop=True)
                nc.tensor.matmul(ps_turn[:, 0:2, :].rearrange("p a t -> p (a t)"), ones[:, :], chosen[:, :],
                                 start=True, stop=True).then_inc(turned, 1)
                def lists_of_two(r2):
                    for par in range(2):
                        pe.wait_ge(hot_made, r2 * 2 + par + 1)
                        pe.wait_ge(what_moved, r2 * 2 + par + 1)
                        wait(pe, list_kept, r2 * 2)
                        for t in range(NCH):
                            last = nc.tensor.matmul(ps_list[par][:, 0:PARTS * HI], one_hot[par][:, t, :],
                                                    row_what[par][:, t, :, :], start=(t == 0), stop=(t == NCH - 1))
                        last.then_inc(list_made, 1)

                each(pe, ROWS // 2, lists_of_two)

            @block.scalar
            def _(act):
                act.wait_ge(made, 1)
                nc.scalar.preload_act_table_set("natural_log_exp_and_others")
                nc.scalar.activation(log_sum[0:1, :], ones[0:1, 0:ROUTES], ACT.Exp).then_inc(scores_made, 1)
                with act.Fori(0, N_ITERS - 1) as i:
                    for r in range(ROUTES):
                        act.wait_ge(gap_made[r], i + 1)
                        nc.scalar.activation(score[:, r, :], gap[:, r, :], ACT.Exp,
                                             accum_out=sums[:, r:r + 1]).then_inc(exp_made[r], 1)
                    for r in range(ROUTES):
                        act.wait_ge(total_made[r], i + 1)
                        nc.scalar.activation(log_sum[:, r:r + 1], total[r], ACT.Ln).then_inc(log_made[r], 1)
                for r in range(ROUTES):
                    act.wait_ge(gap_made[r], N_ITERS)
                    nc.scalar.activation(score[:, r, :], gap[:, r, :], ACT.Exp).then_inc(scores_made, 1)
                round_weights(act)
                act.wait_ge(handed, WHAT_MADE)
                def lists_of_two(r2):
                    for par in range(2):
                        row = r2 * 2 + par
                        wait(act, list_made, r2 * 2)
                        nc.scalar.activation(row_what[par][:, :, :, :],
                                             what[:, columns(row * NCH, NCH), :, :], ACT.Identity).then_inc(what_moved, 1)
                    for par in range(2):
                        row = r2 * 2 + par
                        act.wait_ge(list_made, row + 1)
                        nc.scalar.activation(listed[:, columns(row, 1), :, :].rearrange("p o w h -> p (o w h)"),
                                             ps_list[par][:, 0:PARTS * HI], ACT.Identity).then_inc(list_kept, 1)

                each(act, ROWS // 2, lists_of_two)

            @block.vector
            def _(v):
                done = 0

                def step(ins, at=None):
                    nonlocal done
                    done += 1
                    ins.then_inc(dve, 1)
                    v.wait_ge(dve, done if at is None else at + done)

                def start_step(r, at=None):
                    step(nc.vector.tensor_tensor(top[:, r:r + 1], s_max[:, r:r + 1], neg_a[:, r:r + 1], ALU.min), at)
                    nc.vector.tensor_scalar(gap[:, r, :], s_t[:, r, :], neg_a[:, r:r + 1], top[:, r:r + 1],
                                            ALU.min, ALU.subtract).then_inc(gap_made[r], 1)

                def end_step(r, n, at=None):
                    v.wait_ge(log_made[r], n)
                    step(nc.vector.tensor_scalar(neg_a[:, r:r + 1], log_sum[:, r:r + 1], top[:, r:r + 1], LOG_K[r],
                                                 ALU.add, ALU.subtract), at)

                def try_bit(r, at=None):
                    step(nc.vector.tensor_scalar(bit[:, r:r + 1], bit[:, r:r + 1], 1, None, ALU.logical_shift_right), at)
                    step(nc.vector.tensor_tensor(cand[:, r:r + 1], cut[:, r:r + 1], bit[:, r:r + 1], ALU.bitwise_or), at)
                    nc.vector.tensor_scalar(over[:, r, :], score[:, r, :], cand[:, r:r + 1].bitcast(F32), 0.0,
                                            ALU.is_ge, ALU.add, accum_out=sums[:, r:r + 1]).then_inc(counted[r], 1)

                def keep_bit(r, n, at=None):
                    v.wait_ge(count_made[r], n)
                    step(nc.vector.scalar_tensor_tensor(out=gain[:, r:r + 1], in0=total[r], scalar=float((NQ, NKV)[r]),
                                                        in1=bit[:, r:r + 1], op0=ALU.is_ge, op1=ALU.mult), at)
                    step(nc.vector.tensor_tensor(cut[:, r:r + 1], cut[:, r:r + 1], gain[:, r:r + 1], ALU.bitwise_or), at)

                v.wait_ge(turned, SCORES_TURNED)
                step(nc.vector.tensor_copy(s_t[:, :, :], ps_turn[:, 0:2, :]))
                nc.vector.tensor_reduce(part_max[:, :], s_t[:, :, :], AX_X, ALU.max).then_inc(handed, 1)
                v.wait_ge(turned, MAX_TURNED)
                step(nc.vector.tensor_reduce(row_max[:, :], ps_small[0:ROUTES, 0:P].rearrange("r (b t) -> r b t", t=NCH),
                                             AX_X, ALU.max))
                nc.vector.tensor_copy(row_wide[:, :].rearrange("r (b t) -> r b t", t=NCH),
                                      spread(row_max[:, :], [1, BATCH], [0, NCH])).then_inc(handed, 1)
                v.wait_ge(turned, MAX_SPREAD)
                step(nc.vector.tensor_copy(s_max[:, :], ps_small[:, P:P + ROUTES]))
                v.wait_ge(made, MADE)
                for r in range(ROUTES):
                    step(nc.vector.memset(neg_a[:, r:r + 1], float(np.float32(np.log(np.float32(SEQ))) - np.float32(LOG_K[r]))))
                for r in range(ROUTES):
                    start_step(r)
                before_loop = done
                with v.Fori(0, N_ITERS - 2) as i:
                    at = i * ITER_STEPS + before_loop
                    done = 0
                    for r in range(ROUTES):
                        end_step(r, i + 1, at)
                        start_step(r, at)
                assert done == ITER_STEPS
                done = before_loop + done * (N_ITERS - 2)
                for r in range(ROUTES):
                    end_step(r, N_ITERS - 1)
                    nc.vector.tensor_scalar(gap[:, r, :], s_t[:, r, :], neg_a[:, r:r + 1], 0.0,
                                            ALU.subtract, ALU.min).then_inc(gap_made[r], 1)
                step(nc.vector.memset(cut[:, :], 0))
                step(nc.vector.memset(bit[:, :], 1 << BIG_BIT))
                v.wait_ge(scores_made, 1 + ROUTES)
                for r in range(ROUTES):
                    try_bit(r)
                before_loop = done
                with v.Fori(0, BIG_BIT - 1) as i:
                    at = i * BIT_STEPS + before_loop
                    done = 0
                    for r in range(ROUTES):
                        keep_bit(r, i + 1, at)
                        try_bit(r, at)
                assert done == BIT_STEPS
                done = before_loop + done * (BIG_BIT - 1)
                for r in range(ROUTES):
                    keep_bit(r, BIG_BIT)
                for r in range(ROUTES):
                    nc.vector.tensor_scalar(equal[:, r, :], score[:, r, :], cut[:, r:r + 1].bitcast(F32), None, ALU.is_equal)
                    last = nc.vector.tensor_scalar(over[:, r, :], score[:, r, :], cut[:, r:r + 1].bitcast(F32), None,
                                                   ALU.is_gt)
                last.then_inc(handed, 1)
                v.wait_ge(turned, MASKS_TURNED)
                nc.vector.tensor_copy(over_c[:, :, :, :].rearrange("p r b t -> p r (b t)"), ps_back[:, 0])
                nc.vector.tensor_copy(equal_c[:, :, :, :].rearrange("p r b t -> p r (b t)"), ps_back[:, 1]).then_inc(handed, 1)
                step(nc.vector.tensor_copy(score_c[:, :].rearrange("p (r c) -> p r c", r=ROUTES), ps_back[:, 2]))

                def tiles_before():
                    step(nc.vector.tensor_copy(count[:, :, :].rearrange("p r t -> p (r t)"),
                                               ps_turn[:, 0:2, :].rearrange("p a t -> p (a t)")))
                    step(nc.vector.memset(offset[:, :, 0:1], 0.0))
                    for t in range(1, NCH):
                        step(nc.vector.tensor_tensor(offset[:, :, t], offset[:, :, t - 1], count[:, :, t - 1], ALU.add))
                    step(nc.vector.tensor_tensor(place[:, :], ps_before[:, 0:COLS],
                                                 offset[:, :, :].rearrange("p r t -> p (r t)"), ALU.add))

                v.wait_ge(turned, TIES_COUNTED)
                step(nc.vector.tensor_reduce(room[:, :], ps_turn[:, 2:4, :].rearrange("p a (b t) -> p (a b) t", t=NCH), AX_X,
                                             ALU.add))
                step(nc.vector.tensor_tensor(room[:, :].rearrange("p (r b) -> p r b", b=BATCH),
                                             spread(take[:, :], [1, ROUTES], [0, BATCH]),
                                             room[:, :].rearrange("p (r b) -> p r b", b=BATCH), ALU.subtract))
                tiles_before()
                step(nc.vector.tensor_tensor(chosen[:, :].rearrange("p (r t) -> p r t", t=NCH),
                                             place[:, :].rearrange("p (r t) -> p r t", t=NCH),
                                             spread(room[:, :], [1, ROWS], [0, NCH]), ALU.is_lt))
                step(nc.vector.tensor_tensor(chosen[:, :], chosen[:, :],
                                             equal_c[:, :, :, :].rearrange("p r b t -> p (r b t)"), ALU.mult))
                step(nc.vector.tensor_tensor(chosen[:, :], chosen[:, :],
                                             over_c[:, :, :, :].rearrange("p r b t -> p (r b t)"), ALU.add))
                nc.vector.memset(offset[:, :, 0:1], 0.0).then_inc(handed, 1)
                v.wait_ge(turned, PLACES_COUNTED)
                tiles_before()
                step(nc.vector.tensor_copy(place_i[:, :], place[:, :]))
                step(nc.vector.tensor_scalar(block_i[:, :], place_i[:, :], P.bit_length() - 1, None, ALU.logical_shift_right))
                step(nc.vector.tensor_scalar(place_i[:, :], place_i[:, :], P - 1, None, ALU.bitwise_and))
                step(nc.vector.tensor_copy(block_no[:, :], block_i[:, :]))
                step(nc.vector.tensor_copy(column[:, :], place_i[:, :]))
                step(nc.vector.scalar_tensor_tensor(out=column[:, :], in0=column[:, :], scalar=1.0, in1=chosen[:, :],
                                                    op0=ALU.add, op1=ALU.mult))
                step(nc.vector.tensor_scalar(column[:, :], column[:, :], -1.0, None, ALU.add))
                step(nc.vector.tensor_tensor(in_block[:, :, :], spread(block_no[:, :], [1, COLS], [0, HI]),
                                             spread(steps[:, 0:HI], [0, COLS], [1, HI]), ALU.is_equal))
                step(nc.vector.tensor_copy(parts[:, :, 0], token_row[:, :]))
                step(nc.vector.tensor_copy(parts[:, :, 1], token_tile[:, :]))

                def by_route(a):
                    return a.rearrange("p (r c) -> p r c", r=ROUTES)

                values = (score_c[:, :], *(spread(keep[n][:, :], [0, ROUTES], [1, TILES]) for n in ("mean2", "rms_scale")))
                for n, value in enumerate(values):
                    left = rest[:, :] if n == 0 else by_route(rest[:, :])
                    for m in range(3):
                        part = parts[:, :, 2 + 3 * n + m]
                        part = part if n == 0 else by_route(part)
                        step(nc.vector.tensor_copy(part, value if m == 0 else left))
                        if m < 2:
                            step(nc.vector.tensor_tensor(left, value if m == 0 else left, part, ALU.subtract))
                for m in range(PARTS):
                    step(nc.vector.tensor_tensor(what[:, :, m, :], in_block[:, :, :],
                                                 spread(parts[:, :, m:m + 1], [PARTS, COLS], [0, HI]), ALU.mult))
                nc.vector.memset(offset[:, :, 0:1], 0.0).then_inc(handed, 1)

                def hot_of_two(r2):
                    for par in range(2):
                        wait(v, list_made, r2 * 2 + par - 1)
                        nc.vector.tensor_tensor(one_hot[par][:, :, :],
                                                spread(column[:, columns((r2 * 2 + par) * NCH, NCH)], [1, NCH], [0, P]),
                                                spread(steps[:, 0:P], [0, NCH], [1, P]), ALU.is_equal).then_inc(hot_made, 1)

                each(v, ROWS // 2, hot_of_two)
                v.wait_ge(list_kept, ROWS)
                step(nc.vector.scalar_tensor_tensor(out=total_no[:, :, :], in0=listed[:, :, 1, :], scalar=float(P),
                                                    in1=listed[:, :, 0, :], op0=ALU.mult, op1=ALU.add))
                step(nc.vector.tensor_tensor(lists["token"][:, :, :].rearrange("p (r b) h -> p r b h", r=ROUTES),
                                             total_no[:, :, :].rearrange("p (r b) h -> p r b h", r=ROUTES),
                                             spread(first_token[:, :], [0, ROUTES], [1, BATCH], [0, HI]), ALU.add))
                for n, name in enumerate(("factor", "mean", "scale")):
                    step(nc.vector.tensor_tensor(lists[name][:, :, :], listed[:, :, 2 + 3 * n, :], listed[:, :, 3 + 3 * n, :],
                                                 ALU.add))
                    step(nc.vector.tensor_tensor(lists[name][:, :, :], lists[name][:, :, :], listed[:, :, 4 + 3 * n, :],
                                                 ALU.add))
                step(nc.vector.tensor_scalar(total_no[:, :, :], lists["factor"][:, :, :], -1.0, 1.0, ALU.mult, ALU.add))
                step(nc.vector.tensor_tensor(lists["factor"][:, :, :], total_no[:, :, :], lists["factor"][:, :, :], ALU.add))


def heavy_phase(nc, x2, out, w, keep, lists, shared):
    out_rows = out.rearrange("b n d -> (b n) d")
    x2_rows = x2.rearrange("b n d -> (b n) d")
    GT = 4
    GROUPS = 1 + NKV // (GT * P)
    ROWT = GT * GROUPS
    KVG = GROUPS - 1
    KT = NKV // P
    SLOTS = 4
    STEPS = QB * HEADS
    LAST = BATCH * QB - 1

    with ExitStack() as ctx:
        sb, ps, sem = open_tensors(nc, ctx)
        rows_in = [sb(f"h_rows{i}", [P, DIM]) for i in range(SLOTS)]
        xt_hi = sb("h_xt_hi", [P, KC, GT * P], F32R)
        xt_lo = sb("h_xt_lo", [P, KC, GT * P], F32R)
        q2 = sb("h_q2", [P, HEADS, NQ], F32R)
        k2_hi = sb("h_k2_hi", [P, HEADS, NKV], F32R)
        k2_lo = sb("h_k2_lo", [P, HEADS, NKV], F32R)
        val = sb("h_val", [P, KT, HDH])
        neg_null = sb("h_neg_null", [P, QB, HEADS])
        prob = [sb(f"h_prob{i}", [P, NKV]) for i in range(2)]
        probs_t = [sb(f"h_probs_t{i}", [P, KT, P]) for i in range(2)]
        neg_max = sb("h_neg_max", [P, 2, HEADS])
        total = sb("h_total", [P, 2, HEADS])
        null_gap = sb("h_null_gap", [P, 2, HEADS])
        null_exp = sb("h_null_exp", [P, 2, HEADS])
        inv = sb("h_inv", [P, 2, HEADS])
        att = sb("h_att", [P, HEADS, DH])
        att_t = sb("h_att_t", [P, KC, P])
        res = [sb("h_res", [P, DIM]), shared]

        ps_s = [ps(f"h_ps_s{i}", [P, 2, 512]) for i in range(2)]
        ps_t = [ps(f"h_ps_t{i}", [P, KT // 2, P]) for i in range(2)]
        ps_o = ps("h_ps_o", [P, HEADS, DH])
        ps_x = ps("h_ps_x", [P, 512])

        gathered = [sem(f"h_gathered{i}") for i in range(SLOTS)]
        res_out = [sem(f"h_res_out{i}") for i in range(2)]
        (normed, xt_turned, xt_hi_kept, xt_kept, projected, hi_kept, lo_kept, v_kept, group_used, doubled, null_made,
         null_kept, s_made, max_step, max_made, exp_made, pt_made, pt_kept_dve, pt_kept_act, o_made, gap_made,
         null_exp_made, null_part_made, inv_step, o_read, att_made, att_turned, att_kept, out_made, res_made) = (
             sem("h_" + n) for n in (
                 "normed xt_turned xt_hi_kept xt_kept projected hi_kept lo_kept v_kept group_used doubled null_made "
                 "null_kept s_made max_step max_made exp_made pt_made pt_kept_dve pt_kept_act o_made gap_made "
                 "null_exp_made null_part_made inv_step o_read att_made att_turned att_kept out_made res_made").split())
        ident = keep["ident"]

        def entry(name, b, n):
            at = b * KVB + n if n < QB else (b + BATCH) * KVB + n - QB
            flat = lists[name][:, :, :].rearrange("p r h -> p (r h)")
            return flat[:, columns(at, 1)]

        def bank(m):
            return ps_s[m % 4 // 2][:, m % 2, :]

        def rows_bank(n):
            at = bank(n) if n < GT else (ps_t[0], ps_t[1], ps_o, ps_x)[n % GT]
            return at if n < GT else at[:, :] if n % GT == 3 else at[:, :, :].rearrange("p a k -> p (a k)")

        with nc.Block() as block:

            @block.sync
            def _(sp):
                with sp.Fori(0, BATCH) as b:
                    for g in range(KVG):
                        cols = slice(g * GT * P, (g + 1) * GT * P)
                        sp.wait_ge(lo_kept, b * ROWT + GT * (g + 2))
                        for odd in range(2):
                            for k2 in (k2_hi, k2_lo):
                                mine, other = slice(odd * DH, odd * DH + DH), slice(DH - odd * DH, P - odd * DH)
                                sp.dma_start(k2[other, odd::2, cols].bitcast(F32), k2[mine, odd::2, cols].bitcast(F32)).then_inc(doubled, 16)

            def scatter(pool, t):
                pool.wait_ge(res_made, t + 1)
                nc.gpsimd.indirect_dma_start(
                    out=out_rows, out_offset=bass.IndirectOffsetOnAxis(ap=entry("token", t // QB, t % QB), axis=0),
                    in_=res[t % 2][:, :], in_offset=None, compute_op=ALU.add).then_inc(res_out[t % 2], 16)

            @block.gpsimd
            def _(pool):
                def gather(n):
                    if n >= SLOTS:
                        pool.wait_ge(xt_turned, n - SLOTS + 1)
                    b, t = n // ROWT, n % ROWT
                    nc.gpsimd.indirect_dma_start(
                        out=rows_in[n % SLOTS][:, :], out_offset=None, in_=x2_rows,
                        in_offset=bass.IndirectOffsetOnAxis(ap=entry("token", b, t), axis=0)).then_inc(gathered[n % SLOTS], 16)

                for n in range(SLOTS):
                    gather(n)
                for b in range(BATCH):
                    for n in range(b * ROWT + SLOTS, min((b + 1) * ROWT + SLOTS, BATCH * ROWT)):
                        gather(n)
                    for qt in range(QB):
                        t = b * QB + qt
                        pool.wait_ge(null_exp_made, t + 1)
                        pool.wait_ge(att_turned, t)
                        nc.gpsimd.tensor_tensor(att[:, :, :], w["null_v"][:, :].rearrange("p (h d) -> p h d", h=HEADS),
                                                spread(null_exp[:, qt % 2, :], [1, HEADS], [0, DH]),
                                                ALU.mult).then_inc(null_part_made, 1)
                        if t >= 1:
                            scatter(pool, t - 1)
                scatter(pool, LAST)
                for i in range(2):
                    pool.wait_ge(res_out[i], 16 * BATCH * QB // 2)

            @block.tensor
            def _(pe):
                def turn_rows(b, n):
                    pe.wait_ge(normed, b * ROWT + n + 1)
                    if n < GT:
                        wait(pe, exp_made, b * STEPS)
                    if n == GT:
                        wait(pe, o_read, b * QB)
                    if n == GT + 3:
                        wait(pe, res_made, b * QB)
                    if n >= 2 * GT:
                        pe.wait_ge(xt_kept, b * ROWT + n - GT + 1)
                    if n == 2 * GT + 3:
                        pe.wait_ge(null_kept, b + 1)
                    for k in range(KC):
                        last = nc.tensor.transpose(rows_bank(n)[:, k * P:(k + 1) * P],
                                                   rows_in[n % SLOTS][:, k * P:(k + 1) * P], ident[:, :])
                    last.then_inc(xt_turned, 1)

                def project_t(b, m, hi, lo, a):
                    for k in range(KC):
                        cols = slice(a * P, (a + 1) * P)
                        last = product(nc, bank(m), (hi[:, k, cols], lo[:, k, cols]), (xt_hi[:, k, :], xt_lo[:, k, :]),
                                       k == 0, k == KC - 1)
                    last.then_inc(projected, 1)

                def project_v(b, m, t):
                    for k in range(KC):
                        cols = slice(t * P, (t + 1) * P)
                        last = product(nc, bank(m), (xt_hi[:, k, cols], xt_lo[:, k, cols]),
                                       (w["v_hi"][:, k, :], w["v_lo"][:, k, :]), k == 0, k == KC - 1)
                    return last

                def null_scores(b):
                    for qt in range(QB):
                        for h in range(HEADS):
                            at = (qt * HEADS + h) * 2
                            last = nc.tensor.matmul(ps_x[:, at:at + 2], q2[:, h, qt * P:(qt + 1) * P], w["null_k"][:, h, :],
                                                    start=True, stop=True)
                    last.then_inc(null_made, 1)

                def scores(b, i):
                    qt, h = i // HEADS, i % HEADS
                    if i == 0:
                        pe.wait_ge(v_kept, b * KT + KT)
                        pe.wait_ge(doubled, b * KVG * 64 + KVG * 64)
                    if i >= 2:
                        pe.wait_ge(exp_made, b * STEPS + i - 1)
                    for half in range(2):
                        cols = slice(half * 512, half * 512 + 512)
                        left = q2[:, h, qt * P:(qt + 1) * P]
                        nc.tensor.matmul(ps_s[i % 2][:, half, :], left, k2_hi[:, h, cols], start=True, stop=False)
                        last = nc.tensor.matmul(ps_s[i % 2][:, half, :], left, k2_lo[:, h, cols], start=False, stop=True)
                    last.then_inc(s_made, 1)

                def turn_probs(b, i):
                    pe.wait_ge(exp_made, b * STEPS + i + 1)
                    for half in range(2):
                        if i >= 1:
                            pe.wait_ge((pt_kept_dve, pt_kept_act)[half], b * STEPS + i)
                        for n in range(KT // 2):
                            at = (half * (KT // 2) + n) * P
                            last = nc.tensor.transpose(ps_t[half][:, n, :], prob[i % 2][:, at:at + P], ident[:, :])
                        last.then_inc(pt_made, 1)

                def attend(b, i):
                    qt, h = i // HEADS, i % HEADS
                    pe.wait_ge(pt_kept_dve, b * STEPS + i + 1)
                    pe.wait_ge(pt_kept_act, b * STEPS + i + 1)
                    if h == 0:
                        wait(pe, o_read, b * QB + qt)
                    for n in range(KT):
                        last = nc.tensor.matmul(ps_o[:, h, :], probs_t[i % 2][:, n, :], val[:, n, h * DH:(h + 1) * DH],
                                                start=(n == 0), stop=(n == KT - 1))
                    last.then_inc(o_made, 1)

                def turn_att(b, qt):
                    pe.wait_ge(att_made, b * QB + qt + 1)
                    wait(pe, res_made, b * QB + qt)
                    for k in range(KC):
                        last = nc.tensor.transpose(ps_x[:, k * P:(k + 1) * P],
                                                   att[:, 2 * k:2 * k + 2, :].rearrange("p h d -> p (h d)"), ident[:, :])
                    last.then_inc(att_turned, 1)

                def project_out(b, qt):
                    pe.wait_ge(att_kept, b * QB + qt + 1)
                    for k in range(KC):
                        last = nc.tensor.matmul(ps_x[:, :], att_t[:, k, :], w["out"][:, k, :],
                                                start=(k == 0), stop=(k == KC - 1))
                    last.then_inc(out_made, 1)

                def sequence(b):
                    before = not isinstance(b, int)
                    for n in range(GT):
                        turn_rows(b, n)
                    if before:
                        turn_att(b - 1, QB - 1)
                    pe.wait_ge(xt_kept, b * ROWT + GT)
                    for a in range(PAIRS):
                        if before and a == 2:
                            project_out(b - 1, QB - 1)
                        if a == 3:
                            for n in range(GT, 2 * GT):
                                turn_rows(b, n)
                        project_t(b, a, w["q_hi"], w["q_lo"], a)
                    for g in range(1, GROUPS):
                        pe.wait_ge(xt_kept, b * ROWT + (g + 1) * GT)
                        for a in range(PAIRS):
                            if g == 1:
                                pe.wait_ge(lo_kept, b * ROWT + a + 1)
                            else:
                                pe.wait_ge(v_kept, b * KT + (g - 2) * GT + a + 1)
                            project_t(b, g * 8 - 4 + a, w["k_hi"], w["k_lo"], a)
                        if g == 1:
                            null_scores(b)
                        for t in range(GT):
                            if t == 3 and g + 1 < GROUPS:
                                for n in range((g + 1) * GT, (g + 2) * GT):
                                    turn_rows(b, n)
                            pe.wait_ge(lo_kept, b * ROWT + g * GT + t + 1)
                            project_v(b, g * 8 + t, t).then_inc(projected, 1)
                    for i in range(2):
                        scores(b, i)
                    for i in range(STEPS + 1):
                        if i < STEPS:
                            turn_probs(b, i)
                        if i + 2 < STEPS:
                            scores(b, i + 2)
                        if 1 <= i:
                            attend(b, i - 1)
                        if i % HEADS == 1 and i > HEADS:
                            turn_att(b, i // HEADS - 1)
                        if i % HEADS == 2 and i > HEADS:
                            project_out(b, i // HEADS - 1)

                each(pe, BATCH, sequence)
                turn_att(BATCH - 1, QB - 1)
                project_out(BATCH - 1, QB - 1)

            @block.scalar
            def _(act):
                def keep_rows(b, n):
                    act.wait_ge(xt_turned, b * ROWT + n + 1)
                    if n % GT == 0:
                        wait(act, projected, b * 20 + (0, 4, 12)[n // GT])
                    nc.scalar.activation(xt_hi[:, :, n % GT * P:(n % GT + 1) * P],
                                         rows_bank(n).rearrange("p (k t) -> p k t", k=KC), ACT.Identity).then_inc(xt_hi_kept, 1)

                def keep_att(b, qt):
                    act.wait_ge(att_turned, b * QB + qt + 1)
                    nc.scalar.activation(att_t[:, :, :].rearrange("p k t -> p (k t)"), ps_x[:, :],
                                         ACT.Identity).then_inc(att_kept, 1)

                def keep_hi(b, m, dst, cols, n):
                    act.wait_ge(projected, b * 20 + m + 1)
                    for odd in range(2):
                        mine = slice(odd * DH, odd * DH + DH)
                        last = nc.scalar.activation(dst[mine, 2 * (m % 4) + odd, cols], bank(m)[mine, :], ACT.Identity)
                    last.then_inc(hi_kept, 1)

                def exponential(b, i):
                    qt, h = i // HEADS, i % HEADS
                    act.wait_ge(max_made, b * STEPS + i + 1)
                    if i >= 2:
                        act.wait_ge(pt_made, 2 * (b * STEPS + i) - 2)
                    nc.scalar.activation(prob[i % 2][:, :].rearrange("p (a k) -> p a k", a=2), ps_s[i % 2][:, :, :], ACT.Exp,
                                         bias=neg_max[:, qt % 2, h:h + 1],
                                         accum_out=total[:, qt % 2, h:h + 1]).then_inc(exp_made, 1)

                nc.scalar.preload_act_table_set("natural_log_exp_and_others")
                def sequence(b):
                    for g in range(GROUPS):
                        for n in range(g * GT, (g + 1) * GT):
                            keep_rows(b, n)
                        if g == 0:
                            if not isinstance(b, int):
                                keep_att(b - 1, QB - 1)
                            for a in range(PAIRS):
                                keep_hi(b, a, q2, slice(0, NQ), a)
                            continue
                        for a in range(PAIRS):
                            keep_hi(b, g * 8 - 4 + a, k2_hi, slice((g - 1) * GT * P, g * GT * P), a)
                        for t in range(GT):
                            m = g * 8 + t
                            act.wait_ge(projected, b * 20 + m + 1)
                            nc.scalar.activation(val[:, (g - 1) * GT + t, :], bank(m), ACT.Identity,
                                                 scale=entry("factor", b, g * GT + t)).then_inc(v_kept, 1)
                    exponential(b, 0)
                    for i in range(STEPS):
                        if i + 1 < STEPS:
                            exponential(b, i + 1)
                        act.wait_ge(pt_made, 2 * (b * STEPS + i) + 2)
                        nc.scalar.activation(probs_t[i % 2][:, KT // 2:, :], ps_t[1][:, :, :],
                                             ACT.Identity).then_inc(pt_kept_act, 1)
                        if i % HEADS == HEADS - 2:
                            qt = i // HEADS
                            act.wait_ge(gap_made, b * QB + qt + 1)
                            nc.scalar.activation(null_exp[:, qt % 2, :], null_gap[:, qt % 2, :], ACT.Exp).then_inc(null_exp_made, 1)
                        if i % HEADS == 1 and i > HEADS:
                            keep_att(b, i // HEADS - 1)

                each(act, BATCH, sequence)
                keep_att(BATCH - 1, QB - 1)

            @block.vector
            def _(v):
                def normalise(b, n):
                    slot = n % SLOTS
                    v.wait_ge(gathered[slot], (b * (ROWT // SLOTS) + n // SLOTS + 1) * 16)
                    nc.vector.tensor_scalar(rows_in[slot][:, :], rows_in[slot][:, :], entry("mean", b, n), entry("scale", b, n),
                                            ALU.subtract, ALU.mult).then_inc(normed, 1)

                def keep_rows_lo(b, n):
                    v.wait_ge(xt_hi_kept, b * ROWT + n + 1)
                    at = slice(n % GT * P, (n % GT + 1) * P)
                    nc.vector.tensor_tensor(xt_lo[:, :, at], rows_bank(n).rearrange("p (k t) -> p k t", k=KC), xt_hi[:, :, at].bitcast(F32),
                                            ALU.subtract).then_inc(xt_kept, 1)

                def keep_lo(b, m, n):
                    v.wait_ge(hi_kept, b * ROWT + n + 1)
                    for odd in range(2):
                        mine, other = slice(odd * DH, odd * DH + DH), slice(DH - odd * DH, P - odd * DH)
                        h = 2 * (m % 4) + odd
                        if n < GT:
                            last = nc.vector.tensor_tensor(q2[other, h, :], bank(m)[mine, :], q2[mine, h, :].bitcast(F32),
                                                           ALU.subtract)
                        else:
                            cols = slice((n // GT - 1) * GT * P, n // GT * GT * P)
                            last = nc.vector.tensor_tensor(k2_lo[mine, h, cols], bank(m)[mine, :],
                                                           k2_hi[mine, h, cols].bitcast(F32), ALU.subtract)
                    last.then_inc(lo_kept, 1)

                def maximum(b, i):
                    qt, h = i // HEADS, i % HEADS
                    at = neg_max[:, qt % 2, h:h + 1]
                    v.wait_ge(s_made, b * STEPS + i + 1)
                    nc.vector.tensor_reduce(at, ps_s[i % 2][:, :, :].rearrange("p a k -> p (a k)"), AX_X, ALU.max,
                                            negate=True).then_inc(max_step, 1)
                    v.wait_ge(max_step, b * STEPS + i + 1)
                    nc.vector.tensor_tensor(at, at, neg_null[:, qt, h:h + 1], ALU.min).then_inc(max_made, 1)

                def keep_result(b, qt):
                    v.wait_ge(out_made, b * QB + qt + 1)
                    wait(v, res_out[qt % 2], (b * (QB // 2) + qt // 2) * 16)
                    nc.vector.scalar_tensor_tensor(out=res[qt % 2][:, :], in0=ps_x[:, :], scalar=entry("factor", b, qt),
                                                   in1=w["null_row"][:, :], op0=ALU.mult, op1=ALU.subtract).then_inc(res_made, 1)

                def sequence(b):
                    for n in range(GT):
                        normalise(b, n)
                    for n in range(GT):
                        keep_rows_lo(b, n)
                    for n in range(GT, 2 * GT):
                        normalise(b, n)
                    for a in range(PAIRS):
                        if a == 2 and not isinstance(b, int):
                            keep_result(b - 1, QB - 1)
                        keep_lo(b, a, a)
                    for g in range(1, GROUPS):
                        for n in range(g * GT, (g + 1) * GT):
                            keep_rows_lo(b, n)
                        for a in range(PAIRS):
                            keep_lo(b, g * 8 - 4 + a, g * GT + a)
                            if a >= 2 and g + 1 < GROUPS:
                                for n in range(2):
                                    normalise(b, (g + 1) * GT + 2 * (a - 2) + n)
                        if g == 1:
                            v.wait_ge(null_made, b + 1)
                            pairs = ps_x[:, 0:2 * STEPS].rearrange("p (i w) -> p i w", w=2)
                            nc.vector.tensor_reduce(neg_null[:, :, :].rearrange("p q h -> p (q h)"), pairs, AX_X, ALU.add,
                                                    negate=True).then_inc(null_kept, 1)
                            v.wait_ge(null_kept, b + 1)
                    for i in range(2):
                        maximum(b, i)
                    for i in range(STEPS + 1):
                        if i < STEPS:
                            v.wait_ge(pt_made, 2 * (b * STEPS + i) + 1)
                            if i >= 2:
                                v.wait_ge(o_made, b * STEPS + i - 1)
                            nc.vector.tensor_copy(probs_t[i % 2][:, 0:KT // 2, :], ps_t[0][:, :, :]).then_inc(pt_kept_dve, 1)
                        if i + 2 < STEPS:
                            maximum(b, i + 2)
                        qt = i // HEADS
                        if i % HEADS == HEADS - 3 and i < STEPS:
                            v.wait_ge(max_made, b * STEPS + i + 3)
                            nc.vector.tensor_tensor(null_gap[:, qt % 2, :], neg_max[:, qt % 2, :], neg_null[:, qt, :],
                                                    ALU.subtract).then_inc(gap_made, 1)
                        if i % HEADS == HEADS - 1 and i < STEPS:
                            v.wait_ge(null_exp_made, b * QB + qt + 1)
                            v.wait_ge(exp_made, b * STEPS + i + 1)
                            nc.vector.tensor_tensor(inv[:, qt % 2, :], total[:, qt % 2, :], null_exp[:, qt % 2, :],
                                                    ALU.add).then_inc(inv_step, 1)
                            v.wait_ge(inv_step, (b * QB + qt) * 2 + 1)
                            nc.vector.reciprocal(inv[:, qt % 2, :], inv[:, qt % 2, :]).then_inc(inv_step, 1)
                        if i % HEADS == 0 and i > 0:
                            qt -= 1
                            v.wait_ge(o_made, b * STEPS + i)
                            v.wait_ge(null_part_made, b * QB + qt + 1)
                            nc.vector.tensor_tensor(att[:, :, :], ps_o[:, :, :], att[:, :, :], ALU.add).then_inc(o_read, 1)
                            v.wait_ge(o_read, b * QB + qt + 1)
                            v.wait_ge(inv_step, (b * QB + qt) * 2 + 2)
                            nc.vector.tensor_tensor(att[:, :, :], att[:, :, :], spread(inv[:, qt % 2, :], [1, HEADS], [0, DH]),
                                                    ALU.mult).then_inc(att_made, 1)
                        if i % HEADS == 2 and i > HEADS:
                            keep_result(b, qt - 1)

                each(v, BATCH, sequence)
                keep_result(BATCH - 1, QB - 1)


def ssm_then_routed_attention(nc, x, log_A, B_param, C, D, ln_g, ln_b, w_qkv, w_out, null_q, rt_q, rt_kv,
                              rms_g, w_q_h, w_kv_h, null_kv, w_out_h, out):
    kpad = nc.dram_tensor("taps_padded", (DIM, KPAD), F32, kind="Internal").ap()
    x2 = nc.dram_tensor("x2", (BATCH, SEQ, DIM), F32, kind="Internal").ap()

    with ExitStack() as whole:
        sb, _, _ = open_tensors(nc, whole)
        keep = {"ident": sb("ident", [P, P]), "steps": sb("steps", [P, P + 1])}

        with ExitStack() as convolution:
            sb, _, _ = open_tensors(nc, convolution)
            keep |= {n: sb(n, [P, CPAIRS]) for n in ("cb", "log_abar")}
            keep |= {n: sb(n, [P, TILES]) for n in ("mean", "rstd")}
            keep["to_end_rate"] = sb("to_end_rate", [P, 1])
            prepare_phase(nc, x, log_A, B_param, C, D, keep, kpad)
            conv_phase(nc, x, log_A, keep, kpad, x2)

        sb, _, _ = open_tensors(nc, whole)
        lists = {n: sb(f"list_{n}", [P, ROWS, max(QB, KVB)], I32 if n == "token" else F32)
                 for n in ("token", "factor", "mean", "scale")}
        shared = sb("scores_then_results", [P, DIM])
        s_all = shared[:, 0:ROUTES * TILES].rearrange("p (r t) -> p r t", r=ROUTES)
        keep["mean2"], keep["rms_scale"] = shared[:, 2 * TILES:3 * TILES], shared[:, 3 * TILES:4 * TILES]

        with ExitStack() as light:
            sb, _, _ = open_tensors(nc, light)
            keep |= {n: sb(n, [P, TILES]) for n in ("rstd2", "rstd3", "shift2", "rstd23", "shift23")}
            w = {"rt": sb("w_rt", [P, ROUTES, DIM]), "row": sb("w_row", [P, DIM])}
            w |= {n: sb(f"w_{n}", [P, PAIRS]) for n in ("bias_q", "bias_k")}
            w |= {n: sb(f"w_{n}", [P, KC, QKV], F32R) for n in ("qkv_hi", "qkv_lo")}
            w |= {n: sb(f"w_{n}", [P, KC, DIM], F32R) for n in ("out_hi", "out_lo")}
            stats_phase(nc, x2, keep, (ln_g, ln_b, w_qkv, w_out, null_q, rt_q, rt_kv, w))
            light_phase(nc, x2, out, w, keep, s_all)

        sb, _, _ = open_tensors(nc, whole)
        w = {n: sb(f"w_{n}", [P, KC, HDH], F32R) for n in ("q_hi", "q_lo", "k_hi", "k_lo", "v_hi", "v_lo")}
        w |= {"out": sb("w_out_h", [P, KC, DIM]), "null_k": sb("w_null_k", [P, HEADS, 2], F32R)}
        w |= {n: sb(f"w_{n}", [P, DIM]) for n in ("null_v", "null_row")}
        routing_phase(nc, s_all, keep, lists, (rms_g, w_q_h, w_kv_h, null_kv, w_out_h, null_q, w))
        heavy_phase(nc, x2, out, w, keep, lists, shared)


_INS = ["L0_attn_x", "L0_attn_log_A", "L0_attn_B_param", "L0_attn_C", "L0_attn_D", "L0_ffn_ln_g", "L0_ffn_ln_b",
        "L0_ffn_w_qkv_l", "L0_ffn_w_out_l", "L0_ffn_null_q", "L0_ffn_rt_q", "L0_ffn_rt_kv", "L0_ffn_rms_g",
        "L0_ffn_w_q_h", "L0_ffn_w_kv_h", "L0_ffn_null_kv", "L0_ffn_w_out_h"]
_OUT = (BATCH, SEQ, DIM)


def kernel(**inputs):
    import numpy as _np
    import concourse.bacc as _bacc
    from concourse import mybir as _mybir
    from concourse.bass_utils import run_bass_kernel_spmd as _run

    nc = _bacc.Bacc("TRN2", target_bir_lowering=False, num_devices=1)
    arrays, args = {}, []
    for name in _INS:
        a = _np.ascontiguousarray(inputs[name])
        arrays[f"in_{name}_dram"] = a
        args.append(nc.dram_tensor(f"in_{name}_dram", a.shape, _mybir.dt.from_np(a.dtype), kind="ExternalInput").ap())
    args.append(nc.dram_tensor("out_dram", _OUT, _mybir.dt.float32, kind="ExternalOutput").ap())
    ssm_then_routed_attention(nc, *args)
    return _run(nc, [arrays], core_ids=[0]).results[0]["out_dram"]
```

```python
from contextlib import ExitStack

import numpy as np

import concourse.bass as bass
import concourse.mybir as mybir

F32 = mybir.dt.float32
I32 = mybir.dt.int32
U32 = mybir.dt.uint32
BF16 = mybir.dt.bfloat16
F32R = mybir.dt.float32r
ALU = mybir.AluOpType
ACT = mybir.ActivationFunctionType
AX_X = mybir.AxisListType.X

P = 128
BATCH, SEQ, DIM, STATE = 8, 2048, 512, 64
HEADS, DH = 8, 64
HDH = HEADS * DH
QKV = 3 * HDH
WIN = 64
PAIRS = HEADS // 2
CHUNK = P
NCH = SEQ // CHUNK
TILES = BATCH * NCH
KC = DIM // P
DT = 0.1
EPS = 1e-5
N_ITERS = 50
NQ, NKV = 512, 1024
K_EFF_Q, K_EFF_KV = 576.0, 1152.0

CPAIRS = DIM // 2
SUB = 16
SPAIRS = SUB // 2
NSUB = DIM // SUB
SUBS_PER_GROUP = P // SUB
KPAD = 2 * CHUNK - 1


def open_tensors(nc, ctx, dtype=F32):
    def sb(name, shape, dt=dtype):
        return ctx.enter_context(nc.sbuf_tensor(name, shape, dt))

    def ps(name, shape, dt=dtype):
        return ctx.enter_context(nc.psum_tensor(name, shape, dt))

    def sem(name):
        return ctx.enter_context(nc.semaphore(name))

    return sb, ps, sem


def spread(ap, *dims):
    return bass.AP(tensor=ap.tensor, offset=ap.offset, ap=[list(ap.ap[0])] + [list(d) for d in dims])


def wait(eng, sem, value):
    if not isinstance(value, int) or value > 0:
        eng.wait_ge(sem, value)


def each(eng, count, body):
    body(0)
    with eng.Fori(1, count) as i:
        body(i)


def columns(at, n):
    return slice(at, at + n) if isinstance(at, int) else bass.ds(at, n)


def load_group_part(sp, x, to, done, g, chunks):
    x_v = x.rearrange("b (c p) d -> c p b d", p=P)
    for c in chunks:
        sp.dma_start(to[:, c], x_v[c, :, :, g * P:(g + 1) * P]).then_inc(done, 16)


def prepare_phase(nc, x, log_A, B_param, C, D, keep, kpad, first_group, first_in):
    tiles_per_load = 4
    loads = TILES // tiles_per_load
    x_rows = x.rearrange("b (c p) d -> p (b c) d", p=P)

    with ExitStack() as ctx:
        sb, ps, sem = open_tensors(nc, ctx)
        xin = [sb(f"xin{i}", [P, tiles_per_load, DIM]) for i in range(4)]
        bn = sb("bn", [P, TILES, 6])
        raw = sb("raw", [P, 3, 2, P])
        b_t = sb("b_t", [P, CPAIRS])
        c_t = sb("c_t", [P, CPAIRS])
        abar = sb("abar", [P, CPAIRS])
        cb_two = sb("cb_two", [P, CPAIRS, 2])
        powers = [sb(f"powers{i}", [P, SPAIRS, CHUNK]) for i in range(2)]
        taps_t = sb("taps_t", [P, DIM])
        krow = sb("krow", [P, KC, KPAD])
        dcol = sb("dcol", [P, KC])
        tmp = sb("tmp", [P, TILES])
        tmp2 = sb("tmp2", [P, TILES])
        to_end = sb("to_end", [P, 1])
        steps_back = sb("steps_back", [P, CHUNK])
        ps_t = ps("ps_t", [P, 3, 4, P])
        ps_taps = [ps(f"ps_taps{i}", [P, 512]) for i in range(2)]
        ps_rows = ps("ps_rows", [P, KC, P])

        x_in = [sem(f"x_in{i}") for i in range(4)]
        par_in = sem("par_in")
        ident_made = sem("ident_made")
        iota_made = sem("iota_made")
        stats_done = sem("stats_done")
        par_turned = sem("par_turned")
        rates = sem("rates")
        act_chain = sem("act_chain")
        dve = sem("dve")
        cb_made = sem("cb_made")
        powers_made = sem("powers_made")
        taps_made = sem("taps_made")
        taps_kept = sem("taps_kept")
        rows_turned = sem("rows_turned")
        krow_made = sem("krow_made")
        sqrt_done = sem("sqrt_done")
        kpad_out = sem("kpad_out")

        ea = sb("ea", [P, CPAIRS])
        mean, rstd, cb = keep["mean"], keep["rstd"], keep["cb"]
        ident, steps = keep["ident"], keep["steps"]

        with nc.Block() as block:

            @block.sync
            def _(sp):
                for n, a in enumerate((log_A, B_param, C)):
                    rows = a.rearrange("(h p two) n -> p h (two n)", p=P, two=2)
                    sp.dma_start(raw[:, n], rows).then_inc(par_in, 16)
                sp.dma_start(dcol[:, :], D.rearrange("(g p) -> p g", p=P),
                             allow_slow_non_contiguous=True).then_inc(par_in, 16)
                for t in range(loads):
                    if t >= 4:
                        sp.wait_ge(stats_done, (t - 3) * tiles_per_load)
                    sp.dma_start(xin[t % 4][:, :, :],
                                 x_rows[:, t * tiles_per_load:(t + 1) * tiles_per_load, :]).then_inc(x_in[t % 4], 16)
                load_group_part(sp, x, first_group, first_in, 0, range(NCH))
                sp.wait_ge(krow_made, 1)
                sp.dma_start(kpad.rearrange("(g p) k -> p g k", p=P), krow[:, :, :]).then_inc(kpad_out, 16)
                sp.wait_ge(kpad_out, 16)

            @block.gpsimd
            def _(pool):
                nc.gpsimd.memset(ident[:, :], 0.0).then_inc(ident_made, 1)
                pool.wait_ge(ident_made, 1)
                nc.gpsimd.affine_select(out=ident[:, :], in_=ident[:, :], compare_op=ALU.not_equal, fill=1.0,
                                        base=0, pattern=[[-1, P]], channel_multiplier=1).then_inc(ident_made, 1)
                nc.gpsimd.iota(steps[:, :], pattern=[[1, CHUNK + 1]], base=0, channel_multiplier=0,
                               allow_small_or_imprecise_dtypes=True).then_inc(iota_made, 1)
                nc.gpsimd.iota(to_end[:, :], pattern=[[0, 1]], base=CHUNK - 1, channel_multiplier=-1,
                               allow_small_or_imprecise_dtypes=True).then_inc(iota_made, 1)
                nc.gpsimd.iota(steps_back[:, :], pattern=[[-1, CHUNK]], base=CHUNK - 1, channel_multiplier=0,
                               allow_small_or_imprecise_dtypes=True).then_inc(iota_made, 1)
                nc.gpsimd.memset(cb_two[:, :, :], 0.0).then_inc(iota_made, 1)
                nc.gpsimd.memset(krow[:, :, :], 0.0).then_inc(iota_made, 1)

            @block.tensor
            def _(pe):
                pe.wait_ge(par_in, 64)
                pe.wait_ge(ident_made, 2)
                for n in range(3):
                    for h in range(2):
                        last = nc.tensor.transpose(ps_t[:, n, h, :], raw[:, n, h, :], ident[:, :])
                last.then_inc(par_turned, 1)
                pe.wait_ge(cb_made, 1)
                def taps_of_two(s2):
                    for par in range(2):
                        pe.wait_ge(powers_made, s2 * 2 + par + 1)
                        wait(pe, taps_kept, s2 * 2 + par)
                        for q in range(SPAIRS):
                            last = nc.tensor.matmul(ps_taps[par][:, 2 * q:2 * q + 2], powers[par][:, q, :],
                                                    cb_two[:, columns((s2 * 2 + par) * SPAIRS + q, 1), :],
                                                    start=True, stop=True)
                        last.then_inc(taps_made, 1)

                each(pe, NSUB // 2, taps_of_two)
                pe.wait_ge(taps_kept, NSUB)
                for g in range(KC):
                    last = nc.tensor.transpose(ps_rows[:, g, :], taps_t[:, g * P:(g + 1) * P], ident[:, :])
                last.then_inc(rows_turned, 1)

            @block.scalar
            def _(act):
                act.wait_ge(par_turned, 1)
                nc.scalar.activation(ea[:, :], ps_t[:, 0, 0:2].rearrange("p h k -> p (h k)"), ACT.Exp).then_inc(act_chain, 1)
                act.wait_ge(act_chain, 1)
                nc.scalar.activation(abar[:, :], ea[:, :], ACT.Exp, scale=-DT).then_inc(rates, 1)
                act.wait_ge(dve, 3)
                act.wait_ge(iota_made, 3)
                def powers_of_two(s2):
                    for par in range(2):
                        wait(act, taps_made, s2 * 2)
                        for q in range(SPAIRS):
                            last = nc.scalar.activation(
                                powers[par][:, q, :], steps_back[:, :], ACT.Exp,
                                scale=keep["log_abar"][:, columns((s2 * 2 + par) * SPAIRS + q, 1)])
                        last.then_inc(powers_made, 1)

                each(act, NSUB // 2, powers_of_two)
                act.wait_ge(sqrt_done, 1)
                nc.scalar.activation(tmp2[:, :], tmp[:, :], ACT.Sqrt).then_inc(sqrt_done, 1)

            @block.vector
            def _(v):
                v.wait_ge(par_turned, 1)
                nc.vector.tensor_copy(b_t[:, :], ps_t[:, 1, 0:2].rearrange("p h k -> p (h k)")).then_inc(dve, 1)
                nc.vector.tensor_copy(c_t[:, :], ps_t[:, 2, 0:2].rearrange("p h k -> p (h k)")).then_inc(dve, 1)
                v.wait_ge(rates, 1)
                nc.vector.tensor_scalar(keep["log_abar"][:, :], ea[:, :], -DT, None, ALU.mult).then_inc(dve, 1)
                nc.vector.tensor_scalar(abar[:, :], abar[:, :], -1.0, 1.0, ALU.mult, ALU.add).then_inc(dve, 1)
                nc.vector.reciprocal(cb[:, :], ea[:, :]).then_inc(dve, 1)
                v.wait_ge(dve, 5)
                nc.vector.tensor_tensor(cb[:, :], cb[:, :], abar[:, :], ALU.mult).then_inc(dve, 1)
                v.wait_ge(dve, 6)
                nc.vector.tensor_tensor(cb[:, :], cb[:, :], b_t[:, :], ALU.mult).then_inc(dve, 1)
                v.wait_ge(dve, 7)
                nc.vector.tensor_tensor(cb[:, :], cb[:, :], c_t[:, :], ALU.mult).then_inc(dve, 1)
                v.wait_ge(dve, 8)
                v.wait_ge(iota_made, 5)
                nc.vector.tensor_scalar(keep["to_end_rate"][:, :], to_end[:, :], -DT, None, ALU.mult).then_inc(dve, 1)
                nc.vector.tensor_copy(cb_two[0:STATE, :, 0], cb[0:STATE, :]).then_inc(dve, 1)
                nc.vector.tensor_copy(cb_two[STATE:P, :, 1], cb[STATE:P, :]).then_inc(cb_made, 1)
                v.wait_ge(dve, 10)
                with v.Fori(0, loads // 4) as t4:
                    for i in range(4):
                        v.wait_ge(x_in[i], t4 * 16 + 16)
                        for n in range(tiles_per_load):
                            nc.vector.bn_stats(bn[:, bass.ds(t4 * 16 + i * tiles_per_load + n, 1), :],
                                               xin[i][:, n, :]).then_inc(stats_done, 1)
                        v.wait_ge(taps_made, t4 * 4 + i + 1)
                        nc.vector.tensor_copy(taps_t[:, bass.ds((t4 * 4 + i) * SUB, SUB)],
                                              ps_taps[i % 2][:, 0:SUB]).then_inc(taps_kept, 1)
                v.wait_ge(stats_done, TILES)
                finish_stats(nc, v, dve, 10, bn, mean, rstd, tmp, tmp2, sqrt_done)
                v.wait_ge(rows_turned, 1)
                nc.vector.tensor_copy(krow[:, :, 0:CHUNK], ps_rows[:, :, :]).then_inc(dve, 1)
                v.wait_ge(dve, 10 + FINISH_STEPS + 1)
                nc.vector.tensor_tensor(krow[:, :, CHUNK - 1:CHUNK], krow[:, :, CHUNK - 1:CHUNK],
                                        spread(dcol[:, :], [1, KC], [1, 1]), ALU.add).then_inc(krow_made, 1)


FINISH_STEPS = 11


def finish_stats(nc, v, chain, n, bn, mean, rstd, tmp, tmp2, sqrt_done):
    half = DIM // 2

    def step(ins):
        nonlocal n
        n += 1
        ins.then_inc(chain, 1)
        v.wait_ge(chain, n)

    step(nc.vector.tensor_tensor(mean[:, :], bn[:, :, 1], bn[:, :, 4], ALU.add))
    step(nc.vector.tensor_scalar(mean[:, :], mean[:, :], 0.5, None, ALU.mult))
    step(nc.vector.tensor_tensor(tmp[:, :], bn[:, :, 1], bn[:, :, 4], ALU.subtract))
    step(nc.vector.scalar_tensor_tensor(out=tmp[:, :], in0=tmp[:, :], scalar=0.25, in1=tmp[:, :],
                                        op0=ALU.mult, op1=ALU.mult))
    step(nc.vector.tensor_tensor(tmp2[:, :], bn[:, :, 2], bn[:, :, 5], ALU.add))
    step(nc.vector.scalar_tensor_tensor(out=tmp[:, :], in0=tmp2[:, :], scalar=1.0 / (2 * half), in1=tmp[:, :],
                                        op0=ALU.mult, op1=ALU.add))
    nc.vector.tensor_scalar(tmp[:, :], tmp[:, :], EPS, None, ALU.add).then_inc(sqrt_done, 1)
    v.wait_ge(sqrt_done, 2)
    step(nc.vector.reciprocal(rstd[:, :], tmp2[:, :]))
    step(nc.vector.tensor_tensor(tmp2[:, :], rstd[:, :], rstd[:, :], ALU.mult))
    step(nc.vector.tensor_tensor(tmp2[:, :], tmp2[:, :], tmp[:, :], ALU.mult))
    step(nc.vector.tensor_scalar(tmp2[:, :], tmp2[:, :], -0.5, 1.5, ALU.mult, ALU.add))
    step(nc.vector.tensor_tensor(rstd[:, :], rstd[:, :], tmp2[:, :], ALU.mult))


def conv_phase(nc, x, log_A, keep, kpad, x2, first_group, first_in):
    COLS = NCH * BATCH
    x2_v = x2.rearrange("b (c p) d -> c p b d", p=P)
    groups = DIM // P
    SCAN = 2 * (NCH - 2)
    logA_flat = log_A.rearrange("d n -> (d n)")
    NEVER = -1e4
    BANKS = (0, 2, 1, 3)

    with ExitStack() as ctx:
        sb, ps, sem = open_tensors(nc, ctx)
        xg = [first_group, sb("xg1", [P, NCH, BATCH, P])]
        xn = [sb(f"xn{i}", [P, SUB, COLS]) for i in range(2)]
        toep_back = sb("toep_back", [P, SUB, CHUNK])
        toep = [sb(f"toep{i}", [P, SUB, CHUNK]) for i in range(2)]
        ea_all = sb("ea_all", [P, SUB * STATE])
        tail = sb("tail", [P, SUB * STATE])
        powers = [sb(f"cpow{i}", [P, SUB, CHUNK]) for i in range(2)]
        log_own = sb("log_own", [P, CPAIRS, 2])
        state = [sb(f"state{i}", [P, NCH, SPAIRS, BATCH]) for i in range(2)]
        decay = [sb(f"decay{i}", [P, SPAIRS]) for i in range(2)]
        carried = [sb(f"carried{i}", [P, SPAIRS, BATCH]) for i in range(2)]
        ps_state = [ps(f"ps_state{i}", [P, SPAIRS, COLS]) for i in range(2)]
        ps_y = [ps(f"ps_y{i}", [P, 4, COLS]) for i in range(4)]

        x_in = [first_in, sem("cx_in1")]
        toep_in = sem("toep_in")
        toep_made = sem("toep_made")
        ea_in = sem("ea_in")
        ea_exp = sem("ea_exp")
        own_made = sem("own_made")
        tails_made = sem("tails_made")
        powers_made = sem("cpowers_made")
        normed = sem("normed")
        norm_step = sem("norm_step")
        states_summed = sem("states_summed")
        states_kept = sem("states_kept")
        carry = sem("carry")
        y_made = sem("y_made")
        y_added = sem("y_added")
        x2_out = [sem(f"x2_out{k}") for k in range(4)]

        mean, rstd, cb = keep["mean"], keep["rstd"], keep["cb"]

        def by_column(a):
            return spread(a[:, :], [0, SUB // 2], [1, NCH], [NCH, BATCH])

        with nc.Block() as block:

            @block.sync
            def _(sp):
                def quarter(k):
                    return range(k * NCH // 4, (k + 1) * NCH // 4)

                def load_quarter(g, k):
                    if g >= 2:
                        sp.wait_ge(x2_out[k], 16 * NCH // 4 * (g - 1))
                    load_group_part(sp, x, xg[g % 2], x_in[g % 2], g, quarter(k))

                def store_quarter(g, k):
                    sp.wait_ge(y_added, 4 * SUBS_PER_GROUP * (g + 1))
                    for c in quarter(k):
                        sp.dma_start(x2_v[c, :, :, g * P:(g + 1) * P], xg[g % 2][:, c]).then_inc(x2_out[k], 16)

                def load_step(it):
                    if it >= 1:
                        sp.wait_ge(tails_made, it)
                    row = logA_flat[it * SUB * STATE:(it + 1) * SUB * STATE]
                    sp.dma_start(ea_all[:, :], bass.AP(tensor=row.tensor, offset=row.offset,
                                                       ap=[[0, P], [1, SUB * STATE]])).then_inc(ea_in, 16)
                    if it >= 1:
                        sp.wait_ge(toep_made, it)
                    sp.dma_start(toep_back[:, :, :],
                                 bass.AP(tensor=kpad.tensor, offset=kpad.offset + it * SUB * KPAD,
                                         ap=[[1, P], [KPAD, SUB], [1, CHUNK]])).then_inc(toep_in, 16)

                for it in range(NSUB):
                    load_step(it)
                    g, k = it // SUBS_PER_GROUP, it % SUBS_PER_GROUP - 1
                    if 0 <= k < 4 and g >= 1:
                        store_quarter(g - 1, k)
                    if 0 <= k - 1 < 4 and g + 1 < groups:
                        load_quarter(g + 1, k - 1)
                for k in range(4):
                    store_quarter(groups - 1, k)
                for k in range(4):
                    sp.wait_ge(x2_out[k], 16 * NCH // 4 * groups)

            @block.vector
            def _(v):
                HALF = SUB // 2

                def normalise(g, sub, it, par, h):
                    src = xg[g % 2][:, :, :, columns(sub * SUB + h * HALF, HALF)].rearrange("p c b d -> p d c b")
                    dst = xn[par][:, h * HALF:(h + 1) * HALF, :].rearrange("p d (c b) -> p d c b", c=NCH)
                    nc.vector.tensor_tensor(dst, src, by_column(mean), ALU.subtract).then_inc(norm_step, 1)
                    v.wait_ge(norm_step, it * 2 + h + 1)
                    nc.vector.tensor_tensor(dst, dst, by_column(rstd), ALU.mult).then_inc(normed, 1)

                def add_y(g, sub, f):
                    at = xg[g % 2][:, :, :, columns(sub * SUB, SUB)].rearrange(
                        "p c b (q two) -> p two q (c b)", two=2)[:, f // 2, f % 2 * 4:f % 2 * 4 + 4]
                    nc.vector.tensor_tensor(at, ps_y[f][:, :, :], at, ALU.add).then_inc(y_added, 1)

                def step(g, sub, it, par, g_next, sub_next):
                    for h in range(2):
                        v.wait_ge(y_made, it * 4 + 2 * h + 2)
                        if g_next is not None:
                            normalise(g_next, sub_next, it + 2, par, h)
                        for f in BANKS[2 * h:2 * h + 2]:
                            add_y(g, sub, f)

                nc.vector.memset(log_own[:, :, :], NEVER).then_inc(own_made, 1)
                v.wait_ge(own_made, 1)
                nc.vector.tensor_copy(log_own[0:STATE, :, 0], keep["log_abar"][0:STATE, :])
                nc.vector.tensor_copy(log_own[STATE:P, :, 1], keep["log_abar"][STATE:P, :]).then_inc(own_made, 1)
                v.wait_ge(x_in[0], 16 * NCH)
                for it in range(2):
                    for h in range(2):
                        normalise(0, it, it, it, h)
                for g in range(groups):
                    base = g * SUBS_PER_GROUP
                    with v.Fori(0, SUBS_PER_GROUP // 2 - 1) as s2:
                        for par in range(2):
                            sub = s2 * 2 + par
                            step(g, sub, sub + base, par, g, sub + 2)
                    for par in range(2):
                        sub = SUBS_PER_GROUP - 2 + par
                        if g + 1 < groups:
                            v.wait_ge(x_in[(g + 1) % 2], 16 * NCH * ((g + 1) // 2 + 1))
                            step(g, sub, base + sub, par, g + 1, par)
                        else:
                            step(g, sub, base + sub, par, None, None)

            @block.scalar
            def _(act):
                log_flat = log_own[:, :, :].rearrange("p q two -> p (q two)")

                def make_tails(it):
                    act.wait_ge(ea_in, it * 16 + 16)
                    nc.scalar.activation(ea_all[:, :], ea_all[:, :], ACT.Exp).then_inc(ea_exp, 1)
                    act.wait_ge(ea_exp, it + 1)
                    wait(act, states_summed, it * 2)
                    nc.scalar.activation(tail[:, :], ea_all[:, :], ACT.Exp,
                                         scale=keep["to_end_rate"][:, :]).then_inc(tails_made, 1)

                def make_powers(it, par):
                    for ch in range(SUB):
                        last = nc.scalar.activation(powers[par][:, ch, :], keep["steps"][:, 1:CHUNK + 1], ACT.Exp,
                                                    scale=log_flat[:, columns(it * SUB + ch, 1)])
                    last.then_inc(powers_made, 1)

                def keep_states(it, par):
                    for q in range(SPAIRS):
                        if q % 4 == 0:
                            act.wait_ge(states_summed, it * 2 + q // 4 + 1)
                        last = nc.scalar.activation(state[par][:, :, q, :],
                                                    ps_state[par][:, q, :].rearrange("p (c b) -> p c b", c=NCH),
                                                    ACT.Identity, scale=cb[:, columns(it * SPAIRS + q, 1)])
                    last.then_inc(states_kept, 1)

                def make_decay(it, par):
                    nc.scalar.activation(decay[par][:, :], keep["log_abar"][:, columns(it * SPAIRS, SPAIRS)], ACT.Exp,
                                         scale=float(CHUNK))

                def turn_toep(it, par):
                    act.wait_ge(toep_in, it * 16 + 16)
                    nc.scalar.activation(toep[par][:, :, :], toep_back[:, :, ::-1], ACT.Identity).then_inc(toep_made, 1)

                act.wait_ge(own_made, 2)
                make_tails(0)
                make_powers(0, 0)
                make_decay(0, 0)

                def act_step(it, par, ahead):
                    keep_states(it, par)
                    turn_toep(it, par)
                    if ahead:
                        make_tails(it + 1)
                        wait(act, y_made, it * 4)
                        make_powers(it + 1, 1 - par)
                        make_decay(it + 1, 1 - par)

                def act_steps(s2):
                    for par in range(2):
                        act_step(s2 * 2 + par, par, True)

                each(act, NSUB // 2 - 1, act_steps)
                act_step(NSUB - 2, 0, True)
                act_step(NSUB - 1, 1, False)

            @block.gpsimd
            def _(pool):
                with pool.Fori(0, NSUB // 2) as s2:
                    for par in range(2):
                        it = s2 * 2 + par
                        by_seq = spread(decay[par][:, :], [1, SPAIRS], [0, BATCH])
                        pool.wait_ge(states_kept, it + 1)
                        for c in range(1, NCH - 1):
                            if c > 1:
                                pool.wait_ge(carry, it * SCAN + 2 * (c - 1))
                            nc.gpsimd.tensor_tensor(carried[par][:, :, :], state[par][:, c - 1], by_seq,
                                                    ALU.mult).then_inc(carry, 1)
                            pool.wait_ge(carry, it * SCAN + 2 * c - 1)
                            nc.gpsimd.tensor_tensor(state[par][:, c], state[par][:, c], carried[par][:, :, :],
                                                    ALU.add).then_inc(carry, 1)

            @block.tensor
            def _(pe):
                def sum_states(it, par):
                    pe.wait_ge(tails_made, it + 1)
                    for q in range(SPAIRS):
                        if q % 4 == 0:
                            pe.wait_ge(normed, it * 2 + q // 4 + 1)
                        for two in range(2):
                            ch = 2 * q + two
                            last = nc.tensor.matmul(ps_state[par][two * STATE:(two + 1) * STATE, q, :],
                                                    tail[:, ch * STATE:(ch + 1) * STATE], xn[par][:, ch, :],
                                                    start=True, stop=True)
                        if q % 4 == 3:
                            last.then_inc(states_summed, 1)

                def make_y(it, par):
                    pe.wait_ge(toep_made, it + 1)
                    pe.wait_ge(powers_made, it + 1)
                    pe.wait_ge(carry, it * SCAN + SCAN)
                    for n, f in enumerate(BANKS):
                        wait(pe, y_added, (it - 1) * 4 + n + 1)
                        for i in range(4):
                            ch = 2 * (f % 2 * 4 + i) + f // 2
                            nc.tensor.matmul(ps_y[f][:, i, :], toep[par][:, ch, :], xn[par][:, ch, :],
                                             start=True, stop=False)
                            last = nc.tensor.matmul(ps_y[f][:, i, BATCH:], powers[par][:, ch, :],
                                                    state[par][:, 0:NCH - 1, ch // 2, :],
                                                    start=False, stop=True)
                        last.then_inc(y_made, 1)

                sum_states(0, 0)
                def pe_steps(s2):
                    for par in range(2):
                        wait(pe, states_kept, s2 * 2 + par)
                        sum_states(s2 * 2 + par + 1, 1 - par)
                        make_y(s2 * 2 + par, par)

                each(pe, NSUB // 2 - 1, pe_steps)
                pe.wait_ge(states_kept, NSUB - 2)
                sum_states(NSUB - 1, 1)
                make_y(NSUB - 2, 0)
                make_y(NSUB - 1, 1)


def light_weights_phase(nc, ln_g, ln_b, w_qkv, w_out, null_q, rt_q, rt_kv, w):
    with ExitStack() as ctx:
        sb, ps, sem = open_tensors(nc, ctx)
        raw = sb("lw_raw", [P, KC, QKV])
        raw_o = sb("lw_raw_o", [P, KC, DIM])
        g_col = sb("lw_g", [P, KC])
        b_col = sb("lw_b", [P, KC])
        bias_v = sb("lw_bias_v", [P, KC])
        wide = sb("lw_wide", [P, KC, P])
        null_row = sb("lw_null", [P, DIM])
        ps_bias = ps("lw_ps_bias", [P, QKV // P])
        ps_row = ps("lw_ps_row", [P, DIM])
        g_q = sb("lw_g_q", [P, KC])
        cols_in, raw_in, rest_in, made, hi_made, dve = (sem(f"lw_{n}") for n in "cols_in raw_in rest_in made hi dve".split())
        BIAS, ROW = 1, 2
        G_Q, QKV_LO = 1, 1 + KC
        BIAS_KEPT, WIDE, OUT_LO, ROW_KEPT = range(QKV_LO + 1, QKV_LO + 5)
        w_k = w_qkv.rearrange("(k p) n -> k p n", p=P)
        parts = ((slice(0, HDH), g_q), (slice(HDH, QKV), g_col))

        with nc.Block() as block:

            @block.sync
            def _(sp):
                for col, src in ((g_col, ln_g), (b_col, ln_b)):
                    sp.dma_start(col[:, :], src.rearrange("(k p) -> p k", p=P),
                                 allow_slow_non_contiguous=True).then_inc(cols_in, 16)
                for k in range(KC):
                    sp.dma_start(raw[:, k, :], w_k[k]).then_inc(raw_in, 16)
                sp.dma_start(raw_o[:, :, :], w_out.rearrange("(k p) n -> p k n", p=P)).then_inc(rest_in, 16)
                for row, src in ((null_row[:, :], null_q), (w["rt"][:, 0], rt_q[0]), (w["rt"][:, 1], rt_kv[0])):
                    sp.dma_start(row, bass.AP(tensor=src.tensor, offset=src.offset,
                                              ap=[[0, P], [1, DIM]])).then_inc(rest_in, 16)

            @block.tensor
            def _(pe):
                pe.wait_ge(cols_in, 16 * 2)
                pe.wait_ge(raw_in, 16 * KC)
                for n in range(QKV // P):
                    for k in range(KC):
                        last = nc.tensor.matmul(ps_bias[:, n:n + 1], raw[:, k, n * P:(n + 1) * P], b_col[:, k:k + 1],
                                                start=(k == 0), stop=(k == KC - 1))
                last.then_inc(made, 1)
                pe.wait_ge(rest_in, 16 * 4)
                pe.wait_ge(dve, WIDE)
                for k in range(KC):
                    last = nc.tensor.matmul(ps_row[:, :], wide[:, k, :], raw_o[:, k, :],
                                            start=(k == 0), stop=(k == KC - 1))
                last.then_inc(made, 1)

            @block.vector
            def _(v):
                v.wait_ge(cols_in, 16 * 2)
                nc.vector.tensor_scalar(g_q[:, :], g_col[:, :], DH ** -0.5, None, ALU.mult).then_inc(dve, 1)
                v.wait_ge(dve, G_Q)
                for k in range(KC):
                    v.wait_ge(hi_made, k + 1)
                    for cols, scale in parts:
                        last = nc.vector.scalar_tensor_tensor(
                            out=w["qkv_lo"][:, k, cols], in0=raw[:, k, cols], scalar=scale[:, k:k + 1],
                            in1=w["qkv_hi"][:, k, cols].bitcast(F32), op0=ALU.mult, op1=ALU.subtract)
                    last.then_inc(dve, 1)
                v.wait_ge(made, BIAS)
                nc.vector.tensor_scalar(w["bias_q"][:, :], ps_bias[:, 0:4], DH ** -0.5, None, ALU.mult)
                nc.vector.tensor_copy(w["bias_k"][:, :], ps_bias[:, 4:8])
                nc.vector.tensor_copy(bias_v[:, :], ps_bias[:, 8:12]).then_inc(dve, 1)
                v.wait_ge(dve, BIAS_KEPT)
                nc.vector.tensor_copy(wide[:, :, :], spread(bias_v[:, :], [1, KC], [0, P])).then_inc(dve, 1)
                v.wait_ge(hi_made, KC + 1)
                nc.vector.tensor_tensor(w["out_lo"][:, :, :], raw_o[:, :, :], w["out_hi"][:, :, :].bitcast(F32),
                                        ALU.subtract).then_inc(dve, 1)
                v.wait_ge(made, ROW)
                nc.vector.tensor_tensor(w["row"][:, :], ps_row[:, :], null_row[:, :], ALU.add).then_inc(dve, 1)
                v.wait_ge(dve, ROW_KEPT)

            @block.scalar
            def _(act):
                act.wait_ge(cols_in, 16 * 2)
                act.wait_ge(dve, G_Q)
                act.wait_ge(raw_in, 16 * KC)
                for k in range(KC):
                    for cols, scale in parts:
                        last = nc.scalar.activation(w["qkv_hi"][:, k, cols], raw[:, k, cols], ACT.Identity,
                                                    scale=scale[:, k:k + 1])
                    last.then_inc(hi_made, 1)
                act.wait_ge(rest_in, 16 * 4)
                nc.scalar.activation(w["out_hi"][:, :, :], raw_o[:, :, :], ACT.Identity).then_inc(hi_made, 1)


MAIN, SIDE = P, WIN
RING = 4
XRING = 16
AHEAD = 8
GT = 4


def product(nc, out, left, right, first=True, last=True):
    (lh, ll), (rh, rl) = left, right
    nc.tensor.matmul(out, lh, rh, start=first, stop=False)
    nc.tensor.matmul(out, lh, rl, start=False, stop=False)
    return nc.tensor.matmul(out, ll, rh, start=False, stop=last)


def light_phase(nc, x2, out, w, keep, s_all):
    x2_t = x2.rearrange("b (c p) d -> (b c) p d", p=P)
    out_t = out.rearrange("b (c p) d -> (b c) p d", p=P)

    with ExitStack() as ctx:
        sb, ps, sem = open_tensors(nc, ctx)
        xin = sb("l_xin", [P, XRING, DIM])
        bn = sb("l_bn", [P, 2, GT, 6])
        dev = sb("l_dev", [P, GT])
        var = sb("l_var", [P, GT])
        square = sb("l_square", [P, 3, GT])
        root = sb("l_root", [P, 3, GT])
        newton = sb("l_newton", [P, 3, GT])
        x2n = sb("l_x2n", [P, 4, DIM])
        xn = sb("l_xn", [P, 2, DIM])
        dot_out = sb("l_dot_out", [P, DIM])
        dots = sb("l_dots", [P, 2, NCH])
        xt_hi = sb("l_xt_hi", [P, KC, P], F32R)
        xt_lo = sb("l_xt_lo", [P, KC, P], F32R)
        q_tok = sb("l_q_tok", [P, HDH])
        k_tok = sb("l_k_tok", [P, HDH])
        q_t = sb("l_q_t", [P, RING, PAIRS, 2, P])
        k_t = sb("l_k_t", [P, PAIRS, RING * P])
        val = sb("l_val", [P, RING, HDH])
        val_side = sb("l_val_side", [P, RING, HDH])
        prob = [sb(f"l_prob{i}", [P, PAIRS, 2 * (MAIN + SIDE)]) for i in range(2)]
        neg_max = sb("l_neg_max", [P, 2, 2, PAIRS])
        total = sb("l_total", [P, 2, 2, PAIRS])
        inv = sb("l_inv", [P, 2, 2, PAIRS])
        pt_main = sb("l_pt_main", [P, HEADS, P])
        pt_side = sb("l_pt_side", [P, HEADS, P])
        at_hi = sb("l_at_hi", [P, KC, P], F32R)
        at_lo = sb("l_at_lo", [P, KC, P], F32R)
        res = sb("l_res", [P, 2, DIM])

        ps_s = ps("l_ps_s", [P, 2, PAIRS, 2 * P])
        ps_a = ps("l_ps_a", [P, 512])
        ps_b = ps("l_ps_b", [P, 512])
        ps_c = ps("l_ps_c", [P, 512])
        ps_d = ps("l_ps_d", [P, 512])

        x_in = [sem(f"l_x_in{i}") for i in range(AHEAD)]
        res_out = [sem(f"l_res_out{i}") for i in range(2)]
        (bn_made, stat_step, square_made, root_made, stats_made, zeroed, x_normed, xt_made, xt_hi_kept, xt_kept, q_made, q_kept, k_made, k_kept, v_made, v_kept,
         qt_made, qt_kept, kt_made, kt_kept, s_made, max_made, exp_made, inv_made, dot_step,
         p_normed, v_moved, x_plus, pt_made, pt_kept_dve, pt_kept_act, o_made, o_hi_kept, o_kept,
         out_made, res_made) = (sem("l_" + n) for n in (
             "bn_made stat_step square_made root_made stats_made zeroed x_normed xt_made xt_hi_kept xt_kept q_made q_kept k_made k_kept v_made v_kept "
             "qt_made qt_kept kt_made kt_kept s_made max_made exp_made inv_made dot_step "
             "p_normed v_moved x_plus pt_made pt_kept_dve pt_kept_act o_made o_hi_kept o_kept "
             "out_made res_made").split())
        ZEROED = 4

        ident = keep["ident"]

        def keys_of(j, win):
            if win == 0:
                return (SIDE if j == 0 else 0), MAIN + SIDE
            return 0, (MAIN if j == NCH - 1 else MAIN + SIDE)

        def key_runs(j, win):
            at = j % RING * P
            if win == 0:
                if j == 0:
                    return [(SIDE, at, MAIN)]
                if at == 0:
                    return [(0, RING * P - SIDE, SIDE), (SIDE, 0, MAIN)]
                return [(0, at - SIDE, MAIN + SIDE)]
            if j == NCH - 1:
                return [(0, at, MAIN)]
            if at == RING * P - P:
                return [(0, at, MAIN), (MAIN, 0, SIDE)]
            return [(0, at, MAIN + SIDE)]

        def steps(eng, body):
            for g in range(NCH):
                body(g, g, lambda k, g=g: g - k >= 0)
            with eng.Fori(1, BATCH - 1) as b:
                for j in range(NCH):
                    body(b * NCH + j, j, lambda k: True)
            for g in range(TILES - NCH, TILES + 4):
                body(g, g % NCH, lambda k, g=g: g - k < TILES)

        AT = (MAIN + SIDE, 0)
        ALL, NEXT, BEFORE = slice(0, P), slice(0, WIN), slice(WIN, P)

        def by_head(buf, keys, win):
            return buf[keys, :, win * WIN:(win + 1) * WIN].rearrange("p (a h) q -> p a h q", h=2)

        def turned(bank, keys):
            return bank[keys, :].rearrange("p (a h q) -> p a h q", h=2, q=WIN)

        with nc.Block() as block:

            @block.sync
            def _(sp):
                for t in range(AHEAD):
                    sp.dma_start(xin[:, t, :], x2_t[t]).then_inc(x_in[t], 16)

                def body(g, j, live):
                    if live(4):
                        wait(sp, res_made, g - 3)
                        sp.dma_start(out_t[g - 4], res[:, j % 2, :]).then_inc(res_out[j % 2], 16)
                    elif g < 4:
                        sp.wait_ge(x_normed, g + 1)
                    if live(-AHEAD):
                        sp.dma_start(xin[:, (j + AHEAD) % XRING, :], x2_t[g + AHEAD]).then_inc(x_in[j % AHEAD], 16)

                steps(sp, body)
                for i in range(2):
                    sp.wait_ge(res_out[i], 16 * TILES // 2)

            @block.tensor
            def _(pe):
                def transpose_x(g, j):
                    wait(pe, x_normed, g + 1)
                    wait(pe, qt_kept, g)
                    for k in range(KC):
                        last = nc.tensor.transpose(ps_a[:, k * P:(k + 1) * P], xn[:, j % 2, k * P:(k + 1) * P],
                                                   ident[:, :])
                    last.then_inc(xt_made, 1)

                def project(bank, part, done):
                    for k in range(KC):
                        cols = slice(part * HDH, (part + 1) * HDH)
                        last = product(nc, bank[:, :], (xt_hi[:, k, :], xt_lo[:, k, :]),
                                       (w["qkv_hi"][:, k, cols], w["qkv_lo"][:, k, cols]), k == 0, k == KC - 1)
                    last.then_inc(done, 1)

                def turn(bank, src, done):
                    for k in range(KC):
                        last = nc.tensor.transpose(bank[:, k * P:(k + 1) * P], src[:, k * P:(k + 1) * P], ident[:, :])
                    last.then_inc(done, 1)

                def scores(t, j):
                    wait(pe, qt_kept, t + 1)
                    wait(pe, kt_kept, t + 1 if j == NCH - 1 else t + 2)
                    for win in range(2):
                        wait(pe, exp_made, 2 * t + win - 1)
                        for pair in range(PAIRS):
                            for col, key, n in key_runs(j, win):
                                last = nc.tensor.matmul(ps_s[:, win, pair, col:col + n], q_t[:, j % RING, pair, win, :],
                                                        k_t[:, pair, key:key + n], start=True, stop=True)
                        last.then_inc(s_made, 1)

                def turn_probs(bank, j, col):
                    for pair in range(PAIRS):
                        last = nc.tensor.transpose(bank[:, pair * P:(pair + 1) * P],
                                                   prob[j % 2][:, pair, col:col + P], ident[:, :])
                    last.then_inc(pt_made, 1)

                def attend(t, j):
                    wait(pe, pt_kept_dve, 2 * t + 2)
                    wait(pe, pt_kept_act, 2 * t + 2)
                    wait(pe, v_kept, t + 1)
                    wait(pe, v_moved, t + 1 if j == NCH - 1 else t + 2)
                    for h in range(HEADS):
                        cols = slice(h * DH, (h + 1) * DH)
                        to = ps_d[h % 2 * DH:(h % 2 + 1) * DH, h // 2 * P:(h // 2 + 1) * P]
                        nc.tensor.matmul(to, val[:, j % RING, cols], pt_main[:, h, :], start=True, stop=False)
                        last = nc.tensor.matmul(to, val_side[:, j % RING, cols], pt_side[:, h, :], start=False, stop=True)
                    last.then_inc(o_made, 1)

                pe.wait_ge(zeroed, ZEROED)
                transpose_x(0, 0)

                def body(g, j, live):
                    if live(2):
                        scores(g - 2, (j - 2) % NCH)
                    if live(4):
                        wait(pe, o_kept, g - 3)
                        wait(pe, kt_kept, g if live(0) else TILES)
                        for k in range(KC):
                            last = product(nc, ps_c[:, :], (at_hi[:, k, :], at_lo[:, k, :]),
                                           (w["out_hi"][:, k, :], w["out_lo"][:, k, :]), k == 0, k == KC - 1)
                        last.then_inc(out_made, 1)
                    if live(0):
                        wait(pe, xt_kept, g + 1)
                        wait(pe, v_kept, g)
                        project(ps_b, 0, q_made)
                    if live(3):
                        t, jt = g - 3, (j - 3) % NCH
                        wait(pe, p_normed, 2 * t + 2)
                        wait(pe, res_made, g - 3)
                        turn_probs(ps_c, jt, AT[0] + SIDE)
                        turn_probs(ps_d, jt, AT[1])
                    if live(0):
                        project(ps_a, 1, k_made)
                    if live(3):
                        wait(pe, pt_kept_dve, 2 * t + 1)
                        turn_probs(ps_c, jt, MAIN)
                    if live(0):
                        wait(pe, q_kept, g + 1)
                        project(ps_b, 2, v_made)
                        wait(pe, k_kept, g + 1)
                        turn(ps_a, q_tok, qt_made)
                    if live(3):
                        wait(pe, pt_kept_dve, 2 * t + 2)
                        wait(pe, pt_kept_act, 2 * t + 2)
                    if live(0):
                        turn(ps_c, k_tok, kt_made)
                    if live(3):
                        attend(t, jt)
                    if live(-1):
                        transpose_x(g + 1, j + 1)

                steps(pe, body)

            @block.scalar
            def _(act):
                def layernorms(g, j, stats):
                    one = columns(g, 1)
                    wait(act, stats_made, stats)
                    wait(act, dot_step, 2 * g - 6)
                    nc.scalar.activation(x2n[:, j % 4, :], xin[:, j % XRING, :], ACT.Identity,
                                         scale=keep["rstd2"][:, one], bias=keep["shift2"][:, one])
                    nc.scalar.activation(xn[:, j % 2, :], xin[:, j % XRING, :], ACT.Identity,
                                         scale=keep["rstd23"][:, one], bias=keep["shift23"][:, one]).then_inc(x_normed, 1)

                def keep_xt(g):
                    wait(act, xt_made, g + 1)
                    nc.scalar.activation(xt_hi[:, :, :].rearrange("p k t -> p (k t)"), ps_a[:, :],
                                         ACT.Identity).then_inc(xt_hi_kept, 1)

                def roots(done):
                    wait(act, square_made, done)
                    nc.scalar.activation(root[:, :, :], square[:, :, :], ACT.Sqrt).then_inc(root_made, GT)

                roots(GT)
                layernorms(0, 0, GT)
                layernorms(1, 1, GT)
                keep_xt(0)

                def body(g, j, live):
                    if live(2):
                        t, jt = g - 2, (j - 2) % NCH
                        for win in range(2):
                            wait(act, max_made, 2 * t + win + 1)
                            lo, hi = keys_of(jt, win)
                            for pair in range(PAIRS):
                                last = nc.scalar.activation(
                                    prob[jt % 2][:, pair, AT[win] + lo:AT[win] + hi], ps_s[:, win, pair, lo:hi], ACT.Exp,
                                    bias=neg_max[:, jt % 2, win, pair:pair + 1],
                                    accum_out=total[:, jt % 2, win, pair:pair + 1])
                            last.then_inc(exp_made, 1)
                    if live(0):
                        wait(act, q_made, g + 1)
                        nc.scalar.activation(q_tok[:, :], ps_b[:, :], ACT.Identity).then_inc(q_kept, 1)
                    if live(1):
                        wait(act, v_kept, g)
                        lo, hi = slice(0, WIN), slice(WIN, P)
                        if (j - 1) % NCH != 0:
                            last = nc.scalar.activation(val_side[lo, (j - 2) % RING, :], val[lo, (j - 1) % RING, :],
                                                        ACT.Identity)
                        if (j - 1) % NCH != NCH - 1:
                            last = nc.scalar.activation(val_side[hi, j % RING, :], val[hi, (j - 1) % RING, :],
                                                        ACT.Identity)
                        last.then_inc(v_moved, 1)
                    if live(3):
                        t, jt = g - 3, (j - 3) % NCH
                        wait(act, pt_made, 3 * t + 2)
                        nc.scalar.activation(by_head(pt_main, ALL, 1), turned(ps_d, ALL), ACT.Identity).then_inc(pt_kept_act, 1)
                    if live(0):
                        wait(act, k_made, g + 1)
                        nc.scalar.activation(k_tok[:, :], ps_a[:, :], ACT.Identity).then_inc(k_kept, 1)
                    if live(3):
                        wait(act, pt_made, 3 * t + 3)
                        nc.scalar.activation(by_head(pt_side, NEXT, 1), turned(ps_c, NEXT),
                                             ACT.Identity).then_inc(pt_kept_act, 1)
                    if live(0):
                        wait(act, v_made, g + 1)
                        nc.scalar.activation(val[:, j % RING, :], ps_b[:, :], ACT.Identity).then_inc(v_kept, 1)
                    if live(-2):
                        layernorms(g + 2, (j + 2) % NCH, (g - j) + GT * ((j + 2) // GT + 1))
                    if live(3):
                        wait(act, o_made, t + 1)
                        nc.scalar.activation(at_hi[:, :, :].rearrange("p k t -> p (k t)"), ps_d[:, :],
                                             ACT.Identity).then_inc(o_hi_kept, 1)
                    if live(-1):
                        keep_xt(g + 1)
                    if j % GT == 1 and live(-6):
                        roots((g - j) + GT * ((j + 3) // GT + 1))

                steps(act, body)

            @block.vector
            def _(v):
                nc.vector.memset(q_t[:, :, :, :, :].rearrange("p r a w q -> p (r a w q)"), 0.0).then_inc(zeroed, 1)
                nc.vector.memset(pt_side[:, :, :].rearrange("p h q -> p (h q)"), 0.0).then_inc(zeroed, 1)
                nc.vector.memset(val_side[:, :, :].rearrange("p r n -> p (r n)"), 0.0).then_inc(zeroed, 1)
                nc.vector.memset(dots[:, :, :].rearrange("p r n -> p (r n)"), 0.0).then_inc(zeroed, 1)
                v.wait_ge(zeroed, ZEROED)

                def keep_xt_lo(g):
                    wait(v, xt_hi_kept, g + 1)
                    nc.vector.tensor_tensor(xt_lo[:, :, :].rearrange("p k t -> p (k t)"), ps_a[:, :],
                                            xt_hi[:, :, :].bitcast(F32).rearrange("p k t -> p (k t)"),
                                            ALU.subtract).then_inc(xt_kept, 1)

                def tile_stats(t, j, passes):
                    wait(v, x_in[j % AHEAD], passes)
                    nc.vector.bn_stats(bn[:, j // GT % 2, j % GT, :], xin[:, j % XRING, :]).then_inc(bn_made, 1)

                def stat_chain(at):
                    done = 0

                    def step(ins):
                        nonlocal done
                        done += 1
                        ins.then_inc(stat_step, 1)
                        v.wait_ge(stat_step, at + done)
                    return step

                def squares(first, j, at):
                    step, halves, mean = stat_chain(at), bn[:, j // GT % 2], keep["mean2"][:, columns(first, GT)]
                    wait(v, bn_made, first + GT)
                    step(nc.vector.tensor_tensor(mean, halves[:, :, 1], halves[:, :, 4], ALU.add))
                    step(nc.vector.tensor_tensor(dev[:, :], halves[:, :, 1], halves[:, :, 4], ALU.subtract))
                    step(nc.vector.tensor_scalar(mean, mean, 0.5, None, ALU.mult))
                    step(nc.vector.scalar_tensor_tensor(out=dev[:, :], in0=dev[:, :], scalar=0.25, in1=dev[:, :],
                                                        op0=ALU.mult, op1=ALU.mult))
                    step(nc.vector.tensor_tensor(var[:, :], halves[:, :, 2], halves[:, :, 5], ALU.add))
                    step(nc.vector.scalar_tensor_tensor(out=var[:, :], in0=var[:, :], scalar=1.0 / DIM, in1=dev[:, :],
                                                        op0=ALU.mult, op1=ALU.add))
                    step(nc.vector.tensor_scalar(square[:, 0, :], var[:, :], EPS, None, ALU.add))
                    step(nc.vector.reciprocal(dev[:, :], square[:, 0, :]))
                    step(nc.vector.tensor_tensor(var[:, :], var[:, :], dev[:, :], ALU.mult))
                    step(nc.vector.tensor_scalar(square[:, 1, :], var[:, :], EPS, None, ALU.add))
                    nc.vector.tensor_scalar(square[:, 2, :], var[:, :], float(DIM), 1e-24, ALU.mult,
                                            ALU.max).then_inc(square_made, GT)

                def divisors(first, j, at, roots_done):
                    step, one = stat_chain(at + 10), columns(first, GT)
                    wait(v, root_made, roots_done)
                    step(nc.vector.reciprocal(root[:, :, :], root[:, :, :]))
                    step(nc.vector.tensor_tensor(newton[:, :, :], root[:, :, :], root[:, :, :], ALU.mult))
                    step(nc.vector.tensor_tensor(newton[:, :, :], newton[:, :, :], square[:, :, :], ALU.mult))
                    step(nc.vector.tensor_scalar(newton[:, :, :], newton[:, :, :], -0.5, 1.5, ALU.mult, ALU.add))
                    step(nc.vector.tensor_tensor(root[:, :, :], root[:, :, :], newton[:, :, :], ALU.mult))
                    nc.vector.tensor_copy(keep["rstd2"][:, one], root[:, 0, :])
                    nc.vector.tensor_tensor(keep["rstd23"][:, one], root[:, 0, :], root[:, 1, :], ALU.mult)
                    nc.vector.scalar_tensor_tensor(out=keep["rms_scale"][:, one], in0=root[:, 2, :],
                                                   scalar=float(np.float32(DIM ** 0.5)), in1=root[:, 0, :],
                                                   op0=ALU.mult, op1=ALU.mult)
                    step(nc.vector.scalar_tensor_tensor(out=keep["shift2"][:, one], in0=keep["mean2"][:, one], scalar=-1.0,
                                                        in1=root[:, 0, :], op0=ALU.mult, op1=ALU.mult))
                    nc.vector.tensor_tensor(keep["shift23"][:, one], keep["shift2"][:, one], root[:, 1, :],
                                            ALU.mult).then_inc(stats_made, GT)

                STAT_STEPS = 16

                def chain_at(g, j, tiles):
                    return (g - j) * (STAT_STEPS // GT) + (j + tiles) // GT * STAT_STEPS

                for t in range(6):
                    tile_stats(t, t, 16)
                squares(0, 0, 0)
                divisors(0, 0, 0, GT)
                keep_xt_lo(0)

                def body(g, j, live):
                    if live(2):
                        t, jt = g - 2, (j - 2) % NCH
                        for win in range(2):
                            wait(v, s_made, 2 * t + win + 1)
                            lo, hi = keys_of(jt, win)
                            if hi - lo == MAIN:
                                edge = AT[0] if win == 0 else MAIN
                                nc.vector.memset(prob[jt % 2][:, :, edge:edge + SIDE], 0.0)
                            nc.vector.tensor_reduce(neg_max[:, jt % 2, win, :], ps_s[:, win, :, lo:hi], AX_X, ALU.max,
                                                    negate=True).then_inc(max_made, 1)
                    if live(4):
                        t4 = g - 4
                        wait(v, out_made, g - 3)
                        wait(v, x_plus, g - 3)
                        wait(v, res_out[j % 2], (g - j) * 8 + 16 * ((j - 4) // 2))
                        nc.vector.tensor_tensor(res[:, j % 2, :], ps_c[:, :], xin[:, (j - 4) % XRING, :],
                                                ALU.add).then_inc(res_made, 1)
                    if live(3):
                        t3 = g - 3
                        wait(v, pt_made, 3 * t3 + 1)
                        nc.vector.tensor_copy(by_head(pt_main, ALL, 0), turned(ps_c, ALL)).then_inc(pt_kept_dve, 1)
                    if live(2):
                        wait(v, exp_made, 2 * t + 2)
                        nc.vector.reciprocal(inv[:, jt % 2], total[:, jt % 2]).then_inc(inv_made, 1)
                    if live(3):
                        wait(v, pt_made, 3 * t3 + 3)
                        nc.vector.tensor_copy(by_head(pt_side, BEFORE, 0), turned(ps_c, BEFORE)).then_inc(pt_kept_dve, 1)
                    if j % GT == 2 and live(-5):
                        divisors(g + 2, j + 2, chain_at(g, j, 2), (g - j) + GT * ((j + 2) // GT + 1))
                    if live(0):
                        wait(v, qt_made, g + 1)
                        for h in range(2):
                            rows = slice(h * DH, (h + 1) * DH)
                            last = nc.vector.tensor_tensor(
                                q_t[rows, j % RING, :, :, h * WIN:(h + 1) * WIN],
                                ps_a[rows, :].rearrange("p (a w q) -> p a w q", a=PAIRS, w=2),
                                spread(w["bias_q"][rows, :], [1, PAIRS], [0, 2], [0, WIN]), ALU.add)
                        last.then_inc(qt_kept, 1)
                        wait(v, kt_made, g + 1)
                        nc.vector.tensor_tensor(k_t[:, :, j % RING * P:(j % RING + 1) * P],
                                                ps_c[:, :].rearrange("p (a t) -> p a t", a=PAIRS),
                                                spread(w["bias_k"][:, :], [1, PAIRS], [0, P]), ALU.add).then_inc(kt_kept, 1)
                    if live(3):
                        wait(v, o_hi_kept, t3 + 1)
                        nc.vector.tensor_tensor(at_lo[:, :, :].rearrange("p k t -> p (k t)"), ps_d[:, :],
                                                at_hi[:, :, :].bitcast(F32).rearrange("p k t -> p (k t)"),
                                                ALU.subtract).then_inc(o_kept, 1)
                    if live(-1):
                        keep_xt_lo(g + 1)
                    if live(0):
                        wait(v, x_normed, g + 1)
                        for r in range(2):
                            wait(v, dot_step, 2 * g + r)
                            last = nc.vector.tensor_tensor_reduce(dot_out[:, :], x2n[:, j % 4, :], w["rt"][:, r], 1.0, 0.0,
                                                                  ALU.mult, ALU.add, dots[:, r, j:j + 1])
                            last.then_inc(dot_step, 1)
                        if j == NCH - 1:
                            first = g - j
                            at = slice(first, first + NCH) if isinstance(g, int) else bass.ds(first, NCH)
                            wait(v, dot_step, 2 * g + 2)
                            nc.vector.tensor_copy(s_all[:, :, at], dots[:, :, :])
                    if live(-6):
                        tile_stats(g + 6, (j + 6) % NCH, (g - j) * 2 + 16 * ((j + 6) // AHEAD + 1))
                        if j % GT == 1:
                            squares(g + 3, (j + 3) % NCH, chain_at(g, j, 3))

                steps(v, body)

            @block.gpsimd
            def _(pool):
                pool.wait_ge(zeroed, ZEROED)

                def body(g, j, live):
                    if live(2):
                        t, jt = g - 2, (j - 2) % NCH
                        for win in range(2):
                            if win == 0:
                                wait(pool, inv_made, t + 1)
                            mine = prob[jt % 2][:, :, AT[win]:AT[win] + MAIN + SIDE]
                            nc.gpsimd.tensor_tensor(mine, mine, spread(inv[:, jt % 2, win, :], [1, PAIRS], [0, MAIN + SIDE]),
                                                    ALU.mult).then_inc(p_normed, 1)
                    if live(0):
                        wait(pool, x_normed, g + 1)
                        nc.gpsimd.tensor_tensor(xin[:, j % XRING, :], xin[:, j % XRING, :], w["row"][:, :],
                                                ALU.add).then_inc(x_plus, 1)

                steps(pool, body)


ROUTES = 2
ROWS = ROUTES * BATCH
QB, KVB = NQ // P, NKV // P
BIG_BIT = 30


def heavy_weights(nc, ctx, rms_g, w_q, w_kv, null_kv, w_out, null_q, w):
    sb, _, sem = open_tensors(nc, ctx)
    raw_q = sb("hw_raw_q", [P, KC, HDH])
    raw_kv = sb("hw_raw_kv", [P, KC, HEADS, 2, DH])
    raw_parts = sb("hw_raw_parts", [P, 2, KC, HDH])
    raw_null = sb("hw_raw_null", [P, HEADS])
    g_col = sb("hw_g", [P, KC])
    loaded, scaled, hi_made, lo_made = (sem(f"hw_{n}") for n in ("loaded", "scaled", "hi", "lo"))
    LOADS = 8

    def on_sync(sp):
        sp.dma_start(raw_q[:, :, :], w_q.rearrange("(k p) n -> p k n", p=P)).then_inc(loaded, 16)
        sp.dma_start(raw_kv[:, :, :, :, :].rearrange("p k h w d -> p k (h w d)"),
                     w_kv.rearrange("(k p) h n -> p k (h n)", p=P)).then_inc(loaded, 16)
        sp.dma_start(w["out"][:, :, :], w_out.rearrange("(k p) n -> p k n", p=P)).then_inc(loaded, 16)
        sp.dma_start(g_col[:, :], rms_g.rearrange("(k p) -> p k", p=P),
                     allow_slow_non_contiguous=True).then_inc(loaded, 16)
        for half in range(2):
            sp.dma_start(raw_null[half * DH:(half + 1) * DH, :], null_kv[0].rearrange("h d -> d h"),
                         allow_slow_non_contiguous=True).then_inc(loaded, 16)
        for row, src in ((w["null_v"][:, :], null_kv[1]), (w["null_row"][:, :], null_q)):
            sp.dma_start(row, bass.AP(tensor=src.tensor, offset=src.offset,
                                      ap=[[0, P], [1, DIM]])).then_inc(loaded, 16)

    def on_gpsimd(pool):
        pool.wait_ge(loaded, 16 * LOADS)
        for k in range(KC):
            nc.gpsimd.tensor_scalar(raw_q[:, k, :], raw_q[:, k, :], g_col[:, k:k + 1], DH ** -0.5,
                                    ALU.mult, ALU.mult).then_inc(scaled, 1)
            for n in range(2):
                nc.gpsimd.tensor_scalar(raw_parts[:, n, k, :].rearrange("p (h d) -> p h d", h=HEADS),
                                        raw_kv[:, k, :, n, :], g_col[:, k:k + 1], None, ALU.mult).then_inc(scaled, 1)
        pool.wait_ge(scaled, 3 * KC)
        pool.wait_ge(hi_made, 4)
        for hi, lo, raw in ((w["q_hi"], w["q_lo"], raw_q[:, :, :]), (w["k_hi"], w["k_lo"], raw_parts[:, 0]),
                            (w["v_hi"], w["v_lo"], raw_parts[:, 1])):
            nc.gpsimd.tensor_tensor(lo[:, :, :], raw, hi[:, :, :].bitcast(F32), ALU.subtract).then_inc(lo_made, 1)
        nc.gpsimd.tensor_tensor(w["null_k"][:, :, 1], raw_null[:, :], w["null_k"][:, :, 0].bitcast(F32),
                                ALU.subtract).then_inc(lo_made, 1)
        pool.wait_ge(lo_made, 4)

    def on_scalar(act):
        act.wait_ge(loaded, 16 * LOADS)
        nc.scalar.activation(w["null_k"][:, :, 0], raw_null[:, :], ACT.Identity).then_inc(hi_made, 1)
        act.wait_ge(scaled, 3 * KC)
        nc.scalar.activation(w["q_hi"][:, :, :], raw_q[:, :, :], ACT.Identity).then_inc(hi_made, 1)
        nc.scalar.activation(w["k_hi"][:, :, :], raw_parts[:, 0], ACT.Identity).then_inc(hi_made, 1)
        nc.scalar.activation(w["v_hi"][:, :, :], raw_parts[:, 1], ACT.Identity).then_inc(hi_made, 1)

    return on_sync, on_gpsimd, on_scalar


def routing_phase(nc, s_all, keep, lists, weights):
    COLS = ROWS * NCH
    HI = max(QB, KVB)
    PARTS = 2 + 3 * 3
    with ExitStack() as ctx:
        sb, ps, sem = open_tensors(nc, ctx)
        blocks = sb("r_blocks", [P, P])
        ones = sb("r_ones", [P, P])
        before = sb("r_before", [P, P])
        s_t = sb("r_s_t", [P, ROUTES, P])
        gap = sb("r_gap", [P, ROUTES, P])
        score = sb("r_score", [P, ROUTES, P])
        part_max = sb("r_part_max", [P, ROUTES])
        row_max = sb("r_row_max", [ROUTES, BATCH])
        row_wide = sb("r_row_wide", [ROUTES, P])
        s_max = sb("r_s_max", [P, ROUTES])
        neg_a = sb("r_neg_a", [P, ROUTES])
        top = sb("r_top", [P, ROUTES])
        sums = sb("r_sums", [P, ROUTES])
        log_sum = sb("r_log_sum", [P, ROUTES])
        take = sb("r_take", [P, ROUTES])
        cut = sb("r_cut", [P, ROUTES], U32)
        cand = sb("r_cand", [P, ROUTES], U32)
        bit = sb("r_bit", [P, ROUTES], U32)
        gain = sb("r_gain", [P, ROUTES], U32)
        over = sb("r_over", [P, ROUTES, P])
        equal = sb("r_equal", [P, ROUTES, P])
        over_c = sb("r_over_c", [P, ROUTES, BATCH, NCH])
        equal_c = sb("r_equal_c", [P, ROUTES, BATCH, NCH])
        score_c = sb("r_score_c", [P, COLS])
        count = sb("r_count", [P, ROWS, NCH])
        offset = sb("r_offset", [P, ROWS, NCH])
        place = sb("r_place", [P, COLS])
        place_i = sb("r_place_i", [P, COLS], I32)
        block_i = sb("r_block_i", [P, COLS], I32)
        room = sb("r_room", [P, ROWS])
        chosen = sb("r_chosen", [P, COLS])
        column = sb("r_column", [P, COLS])
        block_no = sb("r_block_no", [P, COLS])
        token_row = sb("r_token_row", [P, COLS])
        token_tile = sb("r_token_tile", [P, COLS])
        first_token = sb("r_first_token", [P, BATCH])
        total_no = sb("r_total_no", [P, ROWS, HI])
        in_block = sb("r_in_block", [P, COLS, HI], BF16)
        rest = sb("r_rest", [P, COLS])
        parts = sb("r_parts", [P, COLS, PARTS], BF16)
        what = sb("r_what", [P, COLS, PARTS, HI], BF16)
        row_what = [sb(f"r_row_what{i}", [P, NCH, PARTS, HI], BF16) for i in range(2)]
        one_hot = [sb(f"r_one_hot{i}", [P, NCH, P], BF16) for i in range(2)]
        listed = sb("r_listed", [P, ROWS, PARTS, HI])

        ps_turn = ps("r_ps_turn", [P, 4, P])
        ps_small = ps("r_ps_small", [P, 512])
        ps_sums = ps("r_ps_sums", [P, 512])
        ps_back = ps("r_ps_back", [P, 3, ROUTES, P])
        ps_before = ps("r_ps_before", [P, 512])
        total = [ps_sums[:, 0:1], ps_before[:, 0:1]]
        ps_list = [ps(f"r_ps_list{i}", [P, 512]) for i in range(2)]

        SCORES_TURNED, MAX_TURNED, MAX_SPREAD, MASKS_TURNED, TIES_COUNTED, PLACES_COUNTED = range(1, 7)
        MAX_MADE, MAX_WIDE, MASKS_MADE, TIES_IN, CHOSEN_IN, WHAT_MADE = range(1, 7)
        (made, turned, handed, scores_made, dve, what_moved, hot_made, list_made, list_kept) = (
            sem("r_" + n) for n in "made turned handed scores_made dve what_moved hot_made list_made list_kept".split())
        gap_made, exp_made, total_made, log_made, counted, count_made = (
            [sem(f"r_{n}{r}") for r in range(ROUTES)]
            for n in ("gap_made", "exp_made", "total_made", "log_made", "counted", "count_made"))
        ident, steps = keep["ident"], keep["steps"]
        MADE = 12
        ITER_STEPS = 2 * ROUTES
        BIT_STEPS = 4 * ROUTES
        LOG_K = [float(np.float32(np.log(np.float32(k)))) for k in (K_EFF_Q, K_EFF_KV)]

        load_weights, combine_weights, round_weights = heavy_weights(nc, ctx, *weights)
        with nc.Block() as block:

            @block.sync
            def _(sp):
                load_weights(sp)

            @block.gpsimd
            def _(pool):
                nc.gpsimd.memset(ones[:, :], 1.0).then_inc(made, 1)
                nc.gpsimd.memset(blocks[:, :], 1.0).then_inc(made, 1)
                nc.gpsimd.memset(before[:, :], 1.0).then_inc(made, 1)
                for a, pattern, mult in ((token_row, [[0, COLS]], 1), (token_tile, [[0, ROWS], [1, NCH]], 0),
                                         (first_token, [[SEQ, BATCH]], 0)):
                    nc.gpsimd.iota(a[:, :], pattern=pattern, base=0, channel_multiplier=mult,
                                   allow_small_or_imprecise_dtypes=True).then_inc(made, 1)
                for r, k in enumerate((NQ, NKV)):
                    nc.gpsimd.memset(take[:, r:r + 1], float(k)).then_inc(made, 1)
                pool.wait_ge(made, 8)
                by_seq = blocks[:, :].rearrange("p (b t) -> p b t", t=NCH)
                nc.gpsimd.affine_select(out=by_seq, in_=by_seq, compare_op=ALU.is_ge, fill=0.0, base=0,
                                        pattern=[[-NCH, BATCH], [0, NCH]], channel_multiplier=1).then_inc(made, 1)
                nc.gpsimd.affine_select(out=before[:, :], in_=before[:, :], compare_op=ALU.is_ge, fill=0.0, base=-1,
                                        pattern=[[1, P]], channel_multiplier=-1).then_inc(made, 1)
                pool.wait_ge(made, 10)
                nc.gpsimd.affine_select(out=by_seq, in_=by_seq, compare_op=ALU.is_ge, fill=0.0, base=NCH - 1,
                                        pattern=[[NCH, BATCH], [0, NCH]], channel_multiplier=-1).then_inc(made, 2)
                combine_weights(pool)

            @block.tensor
            def _(pe):
                for r in range(ROUTES):
                    last = nc.tensor.transpose(ps_turn[:, r, :], s_all[:, r, :], ident[:, :])
                last.then_inc(turned, 1)
                pe.wait_ge(handed, MAX_MADE)
                nc.tensor.transpose(ps_small[0:ROUTES, 0:P], part_max[:, :], ident[:, :]).then_inc(turned, 1)
                pe.wait_ge(handed, MAX_WIDE)
                nc.tensor.transpose(ps_small[:, P:P + ROUTES], row_wide[:, :],
                                    ident[0:ROUTES, 0:ROUTES]).then_inc(turned, 1)
                pe.wait_ge(made, MADE)
                with pe.Fori(0, N_ITERS - 1) as i:
                    for r in range(ROUTES):
                        pe.wait_ge(exp_made[r], i + 1)
                        nc.tensor.matmul(total[r], blocks[:, :], sums[:, r:r + 1], start=True,
                                         stop=True).then_inc(total_made[r], 1)
                with pe.Fori(0, BIG_BIT) as i:
                    for r in range(ROUTES):
                        pe.wait_ge(counted[r], i + 1)
                        nc.tensor.matmul(total[r], blocks[:, :], sums[:, r:r + 1], start=True,
                                         stop=True).then_inc(count_made[r], 1)
                pe.wait_ge(handed, MASKS_MADE)
                for n, src in enumerate((over, equal, score)):
                    for r in range(ROUTES):
                        last = nc.tensor.transpose(ps_back[:, n, r, :], src[:, r, :], ident[:, :])
                last.then_inc(turned, 1)
                pe.wait_ge(handed, TIES_IN)
                nc.tensor.matmul(ps_before[:, 0:COLS], before[:, :], equal_c[:, :, :, :].rearrange("p r b t -> p (r b t)"),
                                 start=True, stop=True)
                nc.tensor.matmul(ps_turn[:, 0:2, :].rearrange("p a t -> p (a t)"), ones[:, :],
                                 equal_c[:, :, :, :].rearrange("p r b t -> p (r b t)"), start=True, stop=True)
                nc.tensor.matmul(ps_turn[:, 2:4, :].rearrange("p a t -> p (a t)"), ones[:, :],
                                 over_c[:, :, :, :].rearrange("p r b t -> p (r b t)"), start=True,
                                 stop=True).then_inc(turned, 1)
                pe.wait_ge(handed, CHOSEN_IN)
                nc.tensor.matmul(ps_before[:, 0:COLS], before[:, :], chosen[:, :], start=True, stop=True)
                nc.tensor.matmul(ps_turn[:, 0:2, :].rearrange("p a t -> p (a t)"), ones[:, :], chosen[:, :],
                                 start=True, stop=True).then_inc(turned, 1)
                def lists_of_two(r2):
                    for par in range(2):
                        pe.wait_ge(hot_made, r2 * 2 + par + 1)
                        pe.wait_ge(what_moved, r2 * 2 + par + 1)
                        wait(pe, list_kept, r2 * 2)
                        for t in range(NCH):
                            last = nc.tensor.matmul(ps_list[par][:, 0:PARTS * HI], one_hot[par][:, t, :],
                                                    row_what[par][:, t, :, :], start=(t == 0), stop=(t == NCH - 1))
                        last.then_inc(list_made, 1)

                each(pe, ROWS // 2, lists_of_two)

            @block.scalar
            def _(act):
                act.wait_ge(made, 1)
                nc.scalar.preload_act_table_set("natural_log_exp_and_others")
                nc.scalar.activation(log_sum[0:1, :], ones[0:1, 0:ROUTES], ACT.Exp).then_inc(scores_made, 1)
                with act.Fori(0, N_ITERS - 1) as i:
                    for r in range(ROUTES):
                        act.wait_ge(gap_made[r], i + 1)
                        nc.scalar.activation(score[:, r, :], gap[:, r, :], ACT.Exp,
                                             accum_out=sums[:, r:r + 1]).then_inc(exp_made[r], 1)
                    for r in range(ROUTES):
                        act.wait_ge(total_made[r], i + 1)
                        nc.scalar.activation(log_sum[:, r:r + 1], total[r], ACT.Ln).then_inc(log_made[r], 1)
                for r in range(ROUTES):
                    act.wait_ge(gap_made[r], N_ITERS)
                    nc.scalar.activation(score[:, r, :], gap[:, r, :], ACT.Exp).then_inc(scores_made, 1)
                round_weights(act)
                act.wait_ge(handed, WHAT_MADE)
                def lists_of_two(r2):
                    for par in range(2):
                        row = r2 * 2 + par
                        wait(act, list_made, r2 * 2)
                        nc.scalar.activation(row_what[par][:, :, :, :],
                                             what[:, columns(row * NCH, NCH), :, :], ACT.Identity).then_inc(what_moved, 1)
                    for par in range(2):
                        row = r2 * 2 + par
                        act.wait_ge(list_made, row + 1)
                        nc.scalar.activation(listed[:, columns(row, 1), :, :].rearrange("p o w h -> p (o w h)"),
                                             ps_list[par][:, 0:PARTS * HI], ACT.Identity).then_inc(list_kept, 1)

                each(act, ROWS // 2, lists_of_two)

            @block.vector
            def _(v):
                done = 0

                def step(ins, at=None):
                    nonlocal done
                    done += 1
                    ins.then_inc(dve, 1)
                    v.wait_ge(dve, done if at is None else at + done)

                def start_step(r, at=None):
                    step(nc.vector.tensor_tensor(top[:, r:r + 1], s_max[:, r:r + 1], neg_a[:, r:r + 1], ALU.min), at)
                    nc.vector.tensor_scalar(gap[:, r, :], s_t[:, r, :], neg_a[:, r:r + 1], top[:, r:r + 1],
                                            ALU.min, ALU.subtract).then_inc(gap_made[r], 1)

                def end_step(r, n, at=None):
                    v.wait_ge(log_made[r], n)
                    step(nc.vector.tensor_scalar(neg_a[:, r:r + 1], log_sum[:, r:r + 1], top[:, r:r + 1], LOG_K[r],
                                                 ALU.add, ALU.subtract), at)

                def try_bit(r, at=None):
                    step(nc.vector.tensor_scalar(bit[:, r:r + 1], bit[:, r:r + 1], 1, None, ALU.logical_shift_right), at)
                    step(nc.vector.tensor_tensor(cand[:, r:r + 1], cut[:, r:r + 1], bit[:, r:r + 1], ALU.bitwise_or), at)
                    nc.vector.tensor_scalar(over[:, r, :], score[:, r, :], cand[:, r:r + 1].bitcast(F32), 0.0,
                                            ALU.is_ge, ALU.add, accum_out=sums[:, r:r + 1]).then_inc(counted[r], 1)

                def keep_bit(r, n, at=None):
                    v.wait_ge(count_made[r], n)
                    step(nc.vector.scalar_tensor_tensor(out=gain[:, r:r + 1], in0=total[r], scalar=float((NQ, NKV)[r]),
                                                        in1=bit[:, r:r + 1], op0=ALU.is_ge, op1=ALU.mult), at)
                    step(nc.vector.tensor_tensor(cut[:, r:r + 1], cut[:, r:r + 1], gain[:, r:r + 1], ALU.bitwise_or), at)

                v.wait_ge(turned, SCORES_TURNED)
                step(nc.vector.tensor_copy(s_t[:, :, :], ps_turn[:, 0:2, :]))
                nc.vector.tensor_reduce(part_max[:, :], s_t[:, :, :], AX_X, ALU.max).then_inc(handed, 1)
                v.wait_ge(turned, MAX_TURNED)
                step(nc.vector.tensor_reduce(row_max[:, :], ps_small[0:ROUTES, 0:P].rearrange("r (b t) -> r b t", t=NCH),
                                             AX_X, ALU.max))
                nc.vector.tensor_copy(row_wide[:, :].rearrange("r (b t) -> r b t", t=NCH),
                                      spread(row_max[:, :], [1, BATCH], [0, NCH])).then_inc(handed, 1)
                v.wait_ge(turned, MAX_SPREAD)
                step(nc.vector.tensor_copy(s_max[:, :], ps_small[:, P:P + ROUTES]))
                v.wait_ge(made, MADE)
                for r in range(ROUTES):
                    step(nc.vector.memset(neg_a[:, r:r + 1], float(np.float32(np.log(np.float32(SEQ))) - np.float32(LOG_K[r]))))
                for r in range(ROUTES):
                    start_step(r)
                before_loop = done
                with v.Fori(0, N_ITERS - 2) as i:
                    at = i * ITER_STEPS + before_loop
                    done = 0
                    for r in range(ROUTES):
                        end_step(r, i + 1, at)
                        start_step(r, at)
                assert done == ITER_STEPS
                done = before_loop + done * (N_ITERS - 2)
                for r in range(ROUTES):
                    end_step(r, N_ITERS - 1)
                    nc.vector.tensor_scalar(gap[:, r, :], s_t[:, r, :], neg_a[:, r:r + 1], 0.0,
                                            ALU.subtract, ALU.min).then_inc(gap_made[r], 1)
                step(nc.vector.memset(cut[:, :], 0))
                step(nc.vector.memset(bit[:, :], 1 << BIG_BIT))
                v.wait_ge(scores_made, 1 + ROUTES)
                for r in range(ROUTES):
                    try_bit(r)
                before_loop = done
                with v.Fori(0, BIG_BIT - 1) as i:
                    at = i * BIT_STEPS + before_loop
                    done = 0
                    for r in range(ROUTES):
                        keep_bit(r, i + 1, at)
                        try_bit(r, at)
                assert done == BIT_STEPS
                done = before_loop + done * (BIG_BIT - 1)
                for r in range(ROUTES):
                    keep_bit(r, BIG_BIT)
                for r in range(ROUTES):
                    nc.vector.tensor_scalar(equal[:, r, :], score[:, r, :], cut[:, r:r + 1].bitcast(F32), None, ALU.is_equal)
                    last = nc.vector.tensor_scalar(over[:, r, :], score[:, r, :], cut[:, r:r + 1].bitcast(F32), None,
                                                   ALU.is_gt)
                last.then_inc(handed, 1)
                v.wait_ge(turned, MASKS_TURNED)
                nc.vector.tensor_copy(over_c[:, :, :, :].rearrange("p r b t -> p r (b t)"), ps_back[:, 0])
                nc.vector.tensor_copy(equal_c[:, :, :, :].rearrange("p r b t -> p r (b t)"), ps_back[:, 1]).then_inc(handed, 1)
                step(nc.vector.tensor_copy(score_c[:, :].rearrange("p (r c) -> p r c", r=ROUTES), ps_back[:, 2]))

                def tiles_before():
                    step(nc.vector.tensor_copy(count[:, :, :].rearrange("p r t -> p (r t)"),
                                               ps_turn[:, 0:2, :].rearrange("p a t -> p (a t)")))
                    step(nc.vector.memset(offset[:, :, 0:1], 0.0))
                    for t in range(1, NCH):
                        step(nc.vector.tensor_tensor(offset[:, :, t], offset[:, :, t - 1], count[:, :, t - 1], ALU.add))
                    step(nc.vector.tensor_tensor(place[:, :], ps_before[:, 0:COLS],
                                                 offset[:, :, :].rearrange("p r t -> p (r t)"), ALU.add))

                v.wait_ge(turned, TIES_COUNTED)
                step(nc.vector.tensor_reduce(room[:, :], ps_turn[:, 2:4, :].rearrange("p a (b t) -> p (a b) t", t=NCH), AX_X,
                                             ALU.add))
                step(nc.vector.tensor_tensor(room[:, :].rearrange("p (r b) -> p r b", b=BATCH),
                                             spread(take[:, :], [1, ROUTES], [0, BATCH]),
                                             room[:, :].rearrange("p (r b) -> p r b", b=BATCH), ALU.subtract))
                tiles_before()
                step(nc.vector.tensor_tensor(chosen[:, :].rearrange("p (r t) -> p r t", t=NCH),
                                             place[:, :].rearrange("p (r t) -> p r t", t=NCH),
                                             spread(room[:, :], [1, ROWS], [0, NCH]), ALU.is_lt))
                step(nc.vector.tensor_tensor(chosen[:, :], chosen[:, :],
                                             equal_c[:, :, :, :].rearrange("p r b t -> p (r b t)"), ALU.mult))
                step(nc.vector.tensor_tensor(chosen[:, :], chosen[:, :],
                                             over_c[:, :, :, :].rearrange("p r b t -> p (r b t)"), ALU.add))
                nc.vector.memset(offset[:, :, 0:1], 0.0).then_inc(handed, 1)
                v.wait_ge(turned, PLACES_COUNTED)
                tiles_before()
                step(nc.vector.tensor_copy(place_i[:, :], place[:, :]))
                step(nc.vector.tensor_scalar(block_i[:, :], place_i[:, :], P.bit_length() - 1, None, ALU.logical_shift_right))
                step(nc.vector.tensor_scalar(place_i[:, :], place_i[:, :], P - 1, None, ALU.bitwise_and))
                step(nc.vector.tensor_copy(block_no[:, :], block_i[:, :]))
                step(nc.vector.tensor_copy(column[:, :], place_i[:, :]))
                step(nc.vector.scalar_tensor_tensor(out=column[:, :], in0=column[:, :], scalar=1.0, in1=chosen[:, :],
                                                    op0=ALU.add, op1=ALU.mult))
                step(nc.vector.tensor_scalar(column[:, :], column[:, :], -1.0, None, ALU.add))
                step(nc.vector.tensor_tensor(in_block[:, :, :], spread(block_no[:, :], [1, COLS], [0, HI]),
                                             spread(steps[:, 0:HI], [0, COLS], [1, HI]), ALU.is_equal))
                step(nc.vector.tensor_copy(parts[:, :, 0], token_row[:, :]))
                step(nc.vector.tensor_copy(parts[:, :, 1], token_tile[:, :]))

                def by_route(a):
                    return a.rearrange("p (r c) -> p r c", r=ROUTES)

                values = (score_c[:, :], *(spread(keep[n][:, :], [0, ROUTES], [1, TILES]) for n in ("mean2", "rms_scale")))
                for n, value in enumerate(values):
                    left = rest[:, :] if n == 0 else by_route(rest[:, :])
                    for m in range(3):
                        part = parts[:, :, 2 + 3 * n + m]
                        part = part if n == 0 else by_route(part)
                        step(nc.vector.tensor_copy(part, value if m == 0 else left))
                        if m < 2:
                            step(nc.vector.tensor_tensor(left, value if m == 0 else left, part, ALU.subtract))
                for m in range(PARTS):
                    step(nc.vector.tensor_tensor(what[:, :, m, :], in_block[:, :, :],
                                                 spread(parts[:, :, m:m + 1], [PARTS, COLS], [0, HI]), ALU.mult))
                nc.vector.memset(offset[:, :, 0:1], 0.0).then_inc(handed, 1)

                def hot_of_two(r2):
                    for par in range(2):
                        wait(v, list_made, r2 * 2 + par - 1)
                        nc.vector.tensor_tensor(one_hot[par][:, :, :],
                                                spread(column[:, columns((r2 * 2 + par) * NCH, NCH)], [1, NCH], [0, P]),
                                                spread(steps[:, 0:P], [0, NCH], [1, P]), ALU.is_equal).then_inc(hot_made, 1)

                each(v, ROWS // 2, hot_of_two)
                v.wait_ge(list_kept, ROWS)
                step(nc.vector.scalar_tensor_tensor(out=total_no[:, :, :], in0=listed[:, :, 1, :], scalar=float(P),
                                                    in1=listed[:, :, 0, :], op0=ALU.mult, op1=ALU.add))
                step(nc.vector.tensor_tensor(lists["token"][:, :, :].rearrange("p (r b) h -> p r b h", r=ROUTES),
                                             total_no[:, :, :].rearrange("p (r b) h -> p r b h", r=ROUTES),
                                             spread(first_token[:, :], [0, ROUTES], [1, BATCH], [0, HI]), ALU.add))
                for n, name in enumerate(("factor", "mean", "scale")):
                    step(nc.vector.tensor_tensor(lists[name][:, :, :], listed[:, :, 2 + 3 * n, :], listed[:, :, 3 + 3 * n, :],
                                                 ALU.add))
                    step(nc.vector.tensor_tensor(lists[name][:, :, :], lists[name][:, :, :], listed[:, :, 4 + 3 * n, :],
                                                 ALU.add))
                step(nc.vector.tensor_scalar(total_no[:, :, :], lists["factor"][:, :, :], -1.0, 1.0, ALU.mult, ALU.add))
                step(nc.vector.tensor_tensor(lists["factor"][:, :, :], total_no[:, :, :], lists["factor"][:, :, :], ALU.add))


def heavy_phase(nc, x2, out, w, keep, lists, shared):
    out_rows = out.rearrange("b n d -> (b n) d")
    x2_rows = x2.rearrange("b n d -> (b n) d")
    GROUPS = 1 + NKV // (GT * P)
    ROWT = GT * GROUPS
    KVG = GROUPS - 1
    KT = NKV // P
    SLOTS = 4
    STEPS = QB * HEADS
    LAST = BATCH * QB - 1

    with ExitStack() as ctx:
        sb, ps, sem = open_tensors(nc, ctx)
        rows_in = [sb(f"h_rows{i}", [P, DIM]) for i in range(SLOTS)]
        at_prob = nc.sbuf_base
        prob = [sb(f"h_prob{i}", [P, NKV]) for i in range(2)]
        at_probs_t = nc.sbuf_base
        probs_t = [sb(f"h_probs_t{i}", [P, KT, P]) for i in range(2)]
        rows_shape = [P, KC, GT * P]
        xt_hi = [sb("h_xt_hi0", rows_shape, F32R), nc.alloc_sbuf_tensor_at("h_xt_hi1", rows_shape, F32R, offset=at_prob)]
        xt_lo = [sb("h_xt_lo0", rows_shape, F32R), nc.alloc_sbuf_tensor_at("h_xt_lo1", rows_shape, F32R, offset=at_probs_t)]
        q2 = sb("h_q2", [P, HEADS, NQ], F32R)
        k2_hi = sb("h_k2_hi", [P, HEADS, NKV], F32R)
        k2_lo = sb("h_k2_lo", [P, HEADS, NKV], F32R)
        val = sb("h_val", [P, KT, HDH])
        neg_null = sb("h_neg_null", [P, QB, HEADS])
        neg_max = sb("h_neg_max", [P, 2, HEADS])
        total = sb("h_total", [P, 2, HEADS])
        null_gap = sb("h_null_gap", [P, 2, HEADS])
        null_exp = sb("h_null_exp", [P, 2, HEADS])
        inv = sb("h_inv", [P, 2, HEADS])
        att = sb("h_att", [P, HEADS, DH])
        att_t = sb("h_att_t", [P, KC, P])
        res = [sb("h_res", [P, DIM]), shared]

        ps_s = [ps(f"h_ps_s{i}", [P, 2, 512]) for i in range(2)]
        ps_t = [ps(f"h_ps_t{i}", [P, KT // 2, P]) for i in range(2)]
        ps_o = ps("h_ps_o", [P, HEADS, DH])
        ps_x = ps("h_ps_x", [P, 512])

        gathered = [sem(f"h_gathered{i}") for i in range(SLOTS)]
        res_out = [sem(f"h_res_out{i}") for i in range(2)]
        doubled = [sem(f"h_doubled{a}") for a in range(PAIRS)]
        (normed, xt_turned, xt_hi_kept, xt_kept, projected, hi_kept, lo_kept, v_kept, null_made,
         null_kept, s_made, max_step, max_made, exp_made, pt_made, pt_kept_dve, pt_kept_act, o_made, gap_made,
         null_exp_made, null_part_made, inv_step, o_read, att_made, att_turned, att_kept, out_made, res_made) = (
             sem("h_" + n) for n in (
                 "normed xt_turned xt_hi_kept xt_kept projected hi_kept lo_kept v_kept null_made "
                 "null_kept s_made max_step max_made exp_made pt_made pt_kept_dve pt_kept_act o_made gap_made "
                 "null_exp_made null_part_made inv_step o_read att_made att_turned att_kept out_made res_made").split())
        ident = keep["ident"]

        def sequences(eng, body):
            body(0, False, True)
            with eng.Fori(1, BATCH - 1) as b:
                body(b, True, True)
            body(BATCH - 1, True, False)

        def entry(name, b, n):
            at = b * KVB + n if n < QB else (b + BATCH) * KVB + n - QB
            flat = lists[name][:, :, :].rearrange("p r h -> p (r h)")
            return flat[:, columns(at, 1)]

        def bank(m):
            return ps_s[m % 4 // 2][:, m % 2, :]

        def rows_bank(n):
            at = bank(n) if n < GT else (ps_t[0], ps_t[1], ps_o, ps_x)[n % GT]
            return at if n < GT else at[:, :] if n % GT == 3 else at[:, :, :].rearrange("p a k -> p (a k)")

        with nc.Block() as block:

            @block.sync
            def _(sp):
                with sp.Fori(0, BATCH) as b:
                    for g in range(KVG):
                        cols = slice(g * GT * P, (g + 1) * GT * P)
                        for a in range(PAIRS):
                            sp.wait_ge(lo_kept, b * ROWT + GT * (g + 1) + a + 1)
                            for odd in range(2):
                                mine, other = slice(odd * DH, odd * DH + DH), slice(DH - odd * DH, P - odd * DH)
                                for k2 in (k2_hi, k2_lo):
                                    sp.dma_start(k2[other, 2 * a + odd, cols].bitcast(F32),
                                                 k2[mine, 2 * a + odd, cols].bitcast(F32)).then_inc(doubled[a], 16)

            def scatter(pool, t):
                pool.wait_ge(res_made, t + 1)
                nc.gpsimd.indirect_dma_start(
                    out=out_rows, out_offset=bass.IndirectOffsetOnAxis(ap=entry("token", t // QB, t % QB), axis=0),
                    in_=res[t % 2][:, :], in_offset=None, compute_op=ALU.add).then_inc(res_out[t % 2], 16)

            @block.gpsimd
            def _(pool):
                def gather(n):
                    if n >= SLOTS:
                        pool.wait_ge(xt_turned, n - SLOTS + 1)
                    b, t = n // ROWT, n % ROWT
                    nc.gpsimd.indirect_dma_start(
                        out=rows_in[n % SLOTS][:, :], out_offset=None, in_=x2_rows,
                        in_offset=bass.IndirectOffsetOnAxis(ap=entry("token", b, t), axis=0)).then_inc(gathered[n % SLOTS], 16)

                for n in range(SLOTS):
                    gather(n)
                for b in range(BATCH):
                    for n in range(b * ROWT + SLOTS, min((b + 1) * ROWT + SLOTS, BATCH * ROWT)):
                        gather(n)
                    for qt in range(QB):
                        t = b * QB + qt
                        pool.wait_ge(null_exp_made, t + 1)
                        pool.wait_ge(att_turned, t)
                        nc.gpsimd.tensor_tensor(att[:, :, :], w["null_v"][:, :].rearrange("p (h d) -> p h d", h=HEADS),
                                                spread(null_exp[:, qt % 2, :], [1, HEADS], [0, DH]),
                                                ALU.mult).then_inc(null_part_made, 1)
                        if t >= 1:
                            scatter(pool, t - 1)
                scatter(pool, LAST)
                for i in range(2):
                    pool.wait_ge(res_out[i], 16 * BATCH * QB // 2)

            @block.tensor
            def _(pe):
                def turn_rows(b, n):
                    pe.wait_ge(normed, b * ROWT + n + 1)
                    if n < GT:
                        wait(pe, exp_made, b * STEPS - 1 + n // 2)
                    if n == GT:
                        wait(pe, o_read, b * QB)
                    if n == GT + 3:
                        wait(pe, res_made, b * QB)
                    if n >= 2 * GT:
                        pe.wait_ge(xt_kept, b * ROWT + n - GT + 1)
                    if n == 2 * GT + 3:
                        pe.wait_ge(null_kept, b + 1)
                    for k in range(KC):
                        last = nc.tensor.transpose(rows_bank(n)[:, k * P:(k + 1) * P],
                                                   rows_in[n % SLOTS][:, k * P:(k + 1) * P], ident[:, :])
                    last.then_inc(xt_turned, 1)

                def project_t(b, g, m, hi, lo, a):
                    for k in range(KC):
                        cols = slice(a * P, (a + 1) * P)
                        last = product(nc, bank(m), (hi[:, k, cols], lo[:, k, cols]), (xt_hi[g % 2][:, k, :], xt_lo[g % 2][:, k, :]),
                                       k == 0, k == KC - 1)
                    last.then_inc(projected, 1)

                def project_v(b, g, t):
                    for k in range(KC):
                        cols = slice(t * P, (t + 1) * P)
                        last = product(nc, bank(t), (xt_hi[g % 2][:, k, cols], xt_lo[g % 2][:, k, cols]),
                                       (w["v_hi"][:, k, :], w["v_lo"][:, k, :]), k == 0, k == KC - 1)
                    last.then_inc(projected, 1)

                def null_scores(b):
                    for qt in range(QB):
                        for h in range(HEADS):
                            at = (qt * HEADS + h) * 2
                            last = nc.tensor.matmul(ps_x[:, at:at + 2], q2[:, h, qt * P:(qt + 1) * P], w["null_k"][:, h, :],
                                                    start=True, stop=True)
                    last.then_inc(null_made, 1)

                def scores(b, i):
                    qt, h = i // HEADS, i % HEADS
                    if i < 2:
                        pe.wait_ge(v_kept, b * KT + KT - 2 + 2 * i)
                    if i >= 2:
                        pe.wait_ge(exp_made, b * STEPS + i - 1)
                    if i < HEADS and h % 2 == 0:
                        pe.wait_ge(doubled[h // 2], (b + 1) * KVG * 64)
                    for half in range(2):
                        cols = slice(half * 512, half * 512 + 512)
                        left = q2[:, h, qt * P:(qt + 1) * P]
                        nc.tensor.matmul(ps_s[i % 2][:, half, :], left, k2_hi[:, h, cols], start=True, stop=False)
                        last = nc.tensor.matmul(ps_s[i % 2][:, half, :], left, k2_lo[:, h, cols], start=False, stop=True)
                    last.then_inc(s_made, 1)

                def turn_probs(b, i):
                    pe.wait_ge(exp_made, b * STEPS + i + 1)
                    for half in range(2):
                        if i >= 1:
                            pe.wait_ge((pt_kept_dve, pt_kept_act)[half], b * STEPS + i)
                        for n in range(KT // 2):
                            at = (half * (KT // 2) + n) * P
                            last = nc.tensor.transpose(ps_t[half][:, n, :], prob[i % 2][:, at:at + P], ident[:, :])
                        last.then_inc(pt_made, 1)

                def attend(b, i):
                    qt, h = i // HEADS, i % HEADS
                    pe.wait_ge(pt_kept_dve, b * STEPS + i + 1)
                    pe.wait_ge(pt_kept_act, b * STEPS + i + 1)
                    if h == 0:
                        wait(pe, o_read, b * QB + qt)
                    for n in range(KT):
                        last = nc.tensor.matmul(ps_o[:, h, :], probs_t[i % 2][:, n, :], val[:, n, h * DH:(h + 1) * DH],
                                                start=(n == 0), stop=(n == KT - 1))
                    last.then_inc(o_made, 1)

                def turn_att(b, qt):
                    pe.wait_ge(att_made, b * QB + qt + 1)
                    wait(pe, res_made, b * QB + qt)
                    for k in range(KC):
                        last = nc.tensor.transpose(ps_x[:, k * P:(k + 1) * P],
                                                   att[:, 2 * k:2 * k + 2, :].rearrange("p h d -> p (h d)"), ident[:, :])
                    last.then_inc(att_turned, 1)

                def project_out(b, qt):
                    pe.wait_ge(att_kept, b * QB + qt + 1)
                    for k in range(KC):
                        last = nc.tensor.matmul(ps_x[:, :], att_t[:, k, :], w["out"][:, k, :],
                                                start=(k == 0), stop=(k == KC - 1))
                    last.then_inc(out_made, 1)

                def sequence(b, before, after):
                    pe.wait_ge(xt_kept, b * ROWT + GT)
                    for a in range(PAIRS):
                        if a == 1 and before:
                            turn_att(b - 1, QB - 1)
                        if a == 2 and before:
                            project_out(b - 1, QB - 1)
                        if a == 3:
                            for n in range(GT, 2 * GT):
                                turn_rows(b, n)
                        project_t(b, 0, a, w["q_hi"], w["q_lo"], a)
                    for g in range(1, GROUPS):
                        pe.wait_ge(xt_kept, b * ROWT + (g + 1) * GT)
                        for a in range(PAIRS):
                            if g == 1:
                                pe.wait_ge(lo_kept, b * ROWT + a + 1)
                            else:
                                pe.wait_ge(v_kept, b * KT + (g - 2) * GT + a + 1)
                            project_t(b, g, g * 8 - 4 + a, w["k_hi"], w["k_lo"], a)
                        if g == 1:
                            null_scores(b)
                        for t in range(GT):
                            if t == 2 and g + 1 < GROUPS:
                                for n in range((g + 1) * GT, (g + 2) * GT):
                                    turn_rows(b, n)
                            if t == 3 and g + 1 == GROUPS:
                                scores(b, 0)
                            pe.wait_ge(lo_kept, b * ROWT + g * GT + t + 1)
                            project_v(b, g, t)
                    scores(b, 1)
                    for i in range(STEPS + 1):
                        if i < STEPS:
                            turn_probs(b, i)
                        if i + 2 < STEPS:
                            scores(b, i + 2)
                        elif i < STEPS and after:
                            for n in range(2):
                                turn_rows(b + 1, (i + 2 - STEPS) * 2 + n)
                        if 1 <= i:
                            attend(b, i - 1)
                        if i % HEADS == 1 and i > HEADS:
                            turn_att(b, i // HEADS - 1)
                        if i % HEADS == 2 and i > HEADS:
                            project_out(b, i // HEADS - 1)

                for n in range(GT):
                    turn_rows(0, n)
                sequences(pe, sequence)
                turn_att(BATCH - 1, QB - 1)
                project_out(BATCH - 1, QB - 1)

            @block.scalar
            def _(act):
                def keep_rows(b, n):
                    act.wait_ge(xt_turned, b * ROWT + n + 1)
                    if n == 0:
                        wait(act, projected, b * 20)
                    if n == 2 * GT:
                        act.wait_ge(projected, b * 20 + 4)
                    nc.scalar.activation(xt_hi[n // GT % 2][:, :, n % GT * P:(n % GT + 1) * P],
                                         rows_bank(n).rearrange("p (k t) -> p k t", k=KC), ACT.Identity).then_inc(xt_hi_kept, 1)

                def keep_att(b, qt):
                    act.wait_ge(att_turned, b * QB + qt + 1)
                    nc.scalar.activation(att_t[:, :, :].rearrange("p k t -> p (k t)"), ps_x[:, :],
                                         ACT.Identity).then_inc(att_kept, 1)

                def keep_hi(b, m, dst, cols, n):
                    act.wait_ge(projected, b * 20 + m + 1)
                    for odd in range(2):
                        mine = slice(odd * DH, odd * DH + DH)
                        last = nc.scalar.activation(dst[mine, 2 * (m % 4) + odd, cols], bank(m)[mine, :], ACT.Identity)
                    last.then_inc(hi_kept, 1)

                def exponential(b, i):
                    qt, h = i // HEADS, i % HEADS
                    act.wait_ge(max_made, b * STEPS + i + 1)
                    if i >= 2:
                        act.wait_ge(pt_made, 2 * (b * STEPS + i) - 2)
                    nc.scalar.activation(prob[i % 2][:, :].rearrange("p (a k) -> p a k", a=2), ps_s[i % 2][:, :, :], ACT.Exp,
                                         bias=neg_max[:, qt % 2, h:h + 1],
                                         accum_out=total[:, qt % 2, h:h + 1]).then_inc(exp_made, 1)

                nc.scalar.preload_act_table_set("natural_log_exp_and_others")
                def sequence(b, before, after):
                    for a in range(PAIRS):
                        if a == 3:
                            for n in range(GT, 2 * GT):
                                keep_rows(b, n)
                        keep_hi(b, a, q2, slice(0, NQ), a)
                        if a == 0 and before:
                            keep_att(b - 1, QB - 1)
                    for g in range(1, GROUPS):
                        for a in range(PAIRS):
                            keep_hi(b, g * 8 - 4 + a, k2_hi, slice((g - 1) * GT * P, g * GT * P), a)
                        for t in range(GT):
                            if t == 2 and g + 1 < GROUPS:
                                for n in range((g + 1) * GT, (g + 2) * GT):
                                    keep_rows(b, n)
                            if t == 3 and g + 1 == GROUPS:
                                exponential(b, 0)
                            act.wait_ge(projected, b * 20 + g * 8 + t + 1)
                            nc.scalar.activation(val[:, (g - 1) * GT + t, :], bank(t), ACT.Identity,
                                                 scale=entry("factor", b, g * GT + t)).then_inc(v_kept, 1)
                    for i in range(STEPS):
                        if i + 1 < STEPS:
                            exponential(b, i + 1)
                        act.wait_ge(pt_made, 2 * (b * STEPS + i) + 2)
                        nc.scalar.activation(probs_t[i % 2][:, KT // 2:, :], ps_t[1][:, :, :],
                                             ACT.Identity).then_inc(pt_kept_act, 1)
                        if i >= STEPS - 2 and after:
                            for n in range(2):
                                keep_rows(b + 1, (i + 2 - STEPS) * 2 + n)
                        if i % HEADS == HEADS - 2:
                            qt = i // HEADS
                            act.wait_ge(gap_made, b * QB + qt + 1)
                            nc.scalar.activation(null_exp[:, qt % 2, :], null_gap[:, qt % 2, :], ACT.Exp).then_inc(null_exp_made, 1)
                        if i % HEADS == 1 and i > HEADS:
                            keep_att(b, i // HEADS - 1)

                for n in range(GT):
                    keep_rows(0, n)
                sequences(act, sequence)
                keep_att(BATCH - 1, QB - 1)

            @block.vector
            def _(v):
                def normalise(b, n):
                    slot = n % SLOTS
                    v.wait_ge(gathered[slot], (b * (ROWT // SLOTS) + n // SLOTS + 1) * 16)
                    nc.vector.tensor_scalar(rows_in[slot][:, :], rows_in[slot][:, :], entry("mean", b, n), entry("scale", b, n),
                                            ALU.subtract, ALU.mult).then_inc(normed, 1)

                def keep_rows_lo(b, n):
                    v.wait_ge(xt_hi_kept, b * ROWT + n + 1)
                    at = slice(n % GT * P, (n % GT + 1) * P)
                    nc.vector.tensor_tensor(xt_lo[n // GT % 2][:, :, at], rows_bank(n).rearrange("p (k t) -> p k t", k=KC),
                                            xt_hi[n // GT % 2][:, :, at].bitcast(F32), ALU.subtract).then_inc(xt_kept, 1)

                def keep_lo(b, m, n):
                    v.wait_ge(hi_kept, b * ROWT + n + 1)
                    for odd in range(2):
                        mine, other = slice(odd * DH, odd * DH + DH), slice(DH - odd * DH, P - odd * DH)
                        h = 2 * (m % 4) + odd
                        if n < GT:
                            last = nc.vector.tensor_tensor(q2[other, h, :], bank(m)[mine, :], q2[mine, h, :].bitcast(F32),
                                                           ALU.subtract)
                        else:
                            cols = slice((n // GT - 1) * GT * P, n // GT * GT * P)
                            last = nc.vector.tensor_tensor(k2_lo[mine, h, cols], bank(m)[mine, :],
                                                           k2_hi[mine, h, cols].bitcast(F32), ALU.subtract)
                    last.then_inc(lo_kept, 1)

                def maximum(b, i):
                    qt, h = i // HEADS, i % HEADS
                    at = neg_max[:, qt % 2, h:h + 1]
                    v.wait_ge(s_made, b * STEPS + i + 1)
                    nc.vector.tensor_reduce(at, ps_s[i % 2][:, :, :].rearrange("p a k -> p (a k)"), AX_X, ALU.max,
                                            negate=True).then_inc(max_step, 1)
                    v.wait_ge(max_step, b * STEPS + i + 1)
                    nc.vector.tensor_tensor(at, at, neg_null[:, qt, h:h + 1], ALU.min).then_inc(max_made, 1)

                def keep_result(b, qt):
                    v.wait_ge(out_made, b * QB + qt + 1)
                    wait(v, res_out[qt % 2], (b * (QB // 2) + qt // 2) * 16)
                    nc.vector.scalar_tensor_tensor(out=res[qt % 2][:, :], in0=ps_x[:, :], scalar=entry("factor", b, qt),
                                                   in1=w["null_row"][:, :], op0=ALU.mult, op1=ALU.subtract).then_inc(res_made, 1)

                def sequence(b, before, after):
                    for n in range(GT, 2 * GT):
                        normalise(b, n)
                    for a in range(PAIRS):
                        if a == 2 and before:
                            keep_result(b - 1, QB - 1)
                        if a == 3:
                            for n in range(GT, 2 * GT):
                                keep_rows_lo(b, n)
                        keep_lo(b, a, a)
                    for g in range(1, GROUPS):
                        for a in range(PAIRS):
                            keep_lo(b, g * 8 - 4 + a, g * GT + a)
                            if g + 1 < GROUPS:
                                normalise(b, (g + 1) * GT + a)
                        if g == 1:
                            v.wait_ge(null_made, b + 1)
                            pairs = ps_x[:, 0:2 * STEPS].rearrange("p (i w) -> p i w", w=2)
                            nc.vector.tensor_reduce(neg_null[:, :, :].rearrange("p q h -> p (q h)"), pairs, AX_X, ALU.add,
                                                    negate=True).then_inc(null_kept, 1)
                            v.wait_ge(null_kept, b + 1)
                        if g + 1 < GROUPS:
                            for n in range((g + 1) * GT, (g + 2) * GT):
                                keep_rows_lo(b, n)
                    for i in range(2):
                        maximum(b, i)
                    for i in range(STEPS + 1):
                        if i < STEPS:
                            v.wait_ge(pt_made, 2 * (b * STEPS + i) + 1)
                            if i >= 2:
                                v.wait_ge(o_made, b * STEPS + i - 1)
                            nc.vector.tensor_copy(probs_t[i % 2][:, 0:KT // 2, :], ps_t[0][:, :, :]).then_inc(pt_kept_dve, 1)
                        if i + 2 < STEPS:
                            maximum(b, i + 2)
                        if after and STEPS - HEADS <= i < STEPS - HEADS + GT:
                            normalise(b + 1, i + HEADS - STEPS)
                        if after and STEPS - 2 <= i < STEPS:
                            for n in range(2):
                                keep_rows_lo(b + 1, (i + 2 - STEPS) * 2 + n)
                        qt = i // HEADS
                        if i % HEADS == HEADS - 3 and i < STEPS:
                            v.wait_ge(max_made, b * STEPS + i + 3)
                            nc.vector.tensor_tensor(null_gap[:, qt % 2, :], neg_max[:, qt % 2, :], neg_null[:, qt, :],
                                                    ALU.subtract).then_inc(gap_made, 1)
                        if i % HEADS == HEADS - 1 and i < STEPS:
                            v.wait_ge(null_exp_made, b * QB + qt + 1)
                            v.wait_ge(exp_made, b * STEPS + i + 1)
                            nc.vector.tensor_tensor(inv[:, qt % 2, :], total[:, qt % 2, :], null_exp[:, qt % 2, :],
                                                    ALU.add).then_inc(inv_step, 1)
                            v.wait_ge(inv_step, (b * QB + qt) * 2 + 1)
                            nc.vector.reciprocal(inv[:, qt % 2, :], inv[:, qt % 2, :]).then_inc(inv_step, 1)
                        if i % HEADS == 0 and i > 0:
                            qt -= 1
                            v.wait_ge(o_made, b * STEPS + i)
                            v.wait_ge(null_part_made, b * QB + qt + 1)
                            nc.vector.tensor_tensor(att[:, :, :], ps_o[:, :, :], att[:, :, :], ALU.add).then_inc(o_read, 1)
                            v.wait_ge(o_read, b * QB + qt + 1)
                            v.wait_ge(inv_step, (b * QB + qt) * 2 + 2)
                            nc.vector.tensor_tensor(att[:, :, :], att[:, :, :], spread(inv[:, qt % 2, :], [1, HEADS], [0, DH]),
                                                    ALU.mult).then_inc(att_made, 1)
                        if i % HEADS == 2 and i > HEADS:
                            keep_result(b, qt - 1)

                for n in range(GT):
                    normalise(0, n)
                for n in range(GT):
                    keep_rows_lo(0, n)
                sequences(v, sequence)
                keep_result(BATCH - 1, QB - 1)


def ssm_then_routed_attention(nc, x, log_A, B_param, C, D, ln_g, ln_b, w_qkv, w_out, null_q, rt_q, rt_kv,
                              rms_g, w_q_h, w_kv_h, null_kv, w_out_h, out):
    kpad = nc.dram_tensor("taps_padded", (DIM, KPAD), F32, kind="Internal").ap()
    x2 = nc.dram_tensor("x2", (BATCH, SEQ, DIM), F32, kind="Internal").ap()

    with ExitStack() as whole:
        sb, _, _ = open_tensors(nc, whole)
        keep = {"ident": sb("ident", [P, P]), "steps": sb("steps", [P, P + 1])}

        with ExitStack() as convolution:
            sb, _, _ = open_tensors(nc, convolution)
            keep |= {n: sb(n, [P, CPAIRS]) for n in ("cb", "log_abar")}
            keep |= {n: sb(n, [P, TILES]) for n in ("mean", "rstd")}
            keep["to_end_rate"] = sb("to_end_rate", [P, 1])
            first_group = sb("xg0", [P, NCH, BATCH, P])
            first_in = convolution.enter_context(nc.semaphore("cx_in0"))
            prepare_phase(nc, x, log_A, B_param, C, D, keep, kpad, first_group, first_in)
            conv_phase(nc, x, log_A, keep, kpad, x2, first_group, first_in)

        sb, _, _ = open_tensors(nc, whole)
        lists = {n: sb(f"list_{n}", [P, ROWS, max(QB, KVB)], I32 if n == "token" else F32)
                 for n in ("token", "factor", "mean", "scale")}
        shared = sb("scores_then_results", [P, DIM])
        s_all = shared[:, 0:ROUTES * TILES].rearrange("p (r t) -> p r t", r=ROUTES)
        keep["mean2"], keep["rms_scale"] = shared[:, 2 * TILES:3 * TILES], shared[:, 3 * TILES:4 * TILES]

        with ExitStack() as light:
            sb, _, _ = open_tensors(nc, light)
            keep |= {n: sb(n, [P, TILES]) for n in ("rstd2", "shift2", "rstd23", "shift23")}
            w = {"rt": sb("w_rt", [P, ROUTES, DIM]), "row": sb("w_row", [P, DIM])}
            w |= {n: sb(f"w_{n}", [P, PAIRS]) for n in ("bias_q", "bias_k")}
            w |= {n: sb(f"w_{n}", [P, KC, QKV], F32R) for n in ("qkv_hi", "qkv_lo")}
            w |= {n: sb(f"w_{n}", [P, KC, DIM], F32R) for n in ("out_hi", "out_lo")}
            light_weights_phase(nc, ln_g, ln_b, w_qkv, w_out, null_q, rt_q, rt_kv, w)
            light_phase(nc, x2, out, w, keep, s_all)

        sb, _, _ = open_tensors(nc, whole)
        w = {n: sb(f"w_{n}", [P, KC, HDH], F32R) for n in ("q_hi", "q_lo", "k_hi", "k_lo", "v_hi", "v_lo")}
        w |= {"out": sb("w_out_h", [P, KC, DIM]), "null_k": sb("w_null_k", [P, HEADS, 2], F32R)}
        w |= {n: sb(f"w_{n}", [P, DIM]) for n in ("null_v", "null_row")}
        routing_phase(nc, s_all, keep, lists, (rms_g, w_q_h, w_kv_h, null_kv, w_out_h, null_q, w))
        heavy_phase(nc, x2, out, w, keep, lists, shared)


_INS = ["L0_attn_x", "L0_attn_log_A", "L0_attn_B_param", "L0_attn_C", "L0_attn_D", "L0_ffn_ln_g", "L0_ffn_ln_b",
        "L0_ffn_w_qkv_l", "L0_ffn_w_out_l", "L0_ffn_null_q", "L0_ffn_rt_q", "L0_ffn_rt_kv", "L0_ffn_rms_g",
        "L0_ffn_w_q_h", "L0_ffn_w_kv_h", "L0_ffn_null_kv", "L0_ffn_w_out_h"]
_OUT = (BATCH, SEQ, DIM)


def kernel(**inputs):
    import numpy as _np
    import concourse.bacc as _bacc
    from concourse import mybir as _mybir
    from concourse.bass_utils import run_bass_kernel_spmd as _run

    nc = _bacc.Bacc("TRN2", target_bir_lowering=False, num_devices=1)
    arrays, args = {}, []
    for name in _INS:
        a = _np.ascontiguousarray(inputs[name])
        arrays[f"in_{name}_dram"] = a
        args.append(nc.dram_tensor(f"in_{name}_dram", a.shape, _mybir.dt.from_np(a.dtype), kind="ExternalInput").ap())
    args.append(nc.dram_tensor("out_dram", _OUT, _mybir.dt.float32, kind="ExternalOutput").ap())
    ssm_then_routed_attention(nc, *args)
    return _run(nc, [arrays], core_ids=[0]).results[0]["out_dram"]
```
